# Optimizing a Trainium2 kernel written in Bass

```python
import numpy as np
import jax
import jax.numpy as jnp

def _softmax(x, axis=-1):
    return jax.nn.softmax(x, axis=axis)

def _gelu(x):
    return jax.nn.gelu(x, approximate=True)

def _silu(x):
    return jax.nn.silu(x)

def _sigmoid(x):
    return jax.nn.sigmoid(x)

def _layernorm(x, axis=-1, eps=1e-05):
    m = jnp.mean(x, axis=axis, keepdims=True)
    v = jnp.var(x, axis=axis, keepdims=True)
    return (x - m) / jnp.sqrt(v + eps)

def _scatter_add(tgt, idx, src, axis=0):
    return tgt.at[idx].add(src)

def _segment_sum(src, seg, n):
    return jax.ops.segment_sum(src, seg, n)
kernel_name = 'mk_sandwich_d2_jaxref_r8_b0694c'

def setup_inputs(seed: int=0):
    np.random.seed(seed)
    _w = jnp.asarray

    def _L0_attn_setup():
        import jax, jax.numpy as jnp
        import numpy as np
        INDIM = 128
        NHEADS = 16
        DK = INDIM // NHEADS
        DV = INDIM // NHEADS
        B, S = (4, 256)
        key = jax.random.key(seed)
        ks = jax.random.split(key, 5)
        x = jax.random.normal(ks[0], (B, S, INDIM), dtype=jnp.float32)
        std_qk = np.sqrt(2.0 / (INDIM + DK)).astype(np.float32)
        std_v = np.sqrt(2.0 / (INDIM + DV)).astype(np.float32)
        Wq = jax.random.normal(ks[1], (NHEADS * DK, INDIM), dtype=jnp.float32) * std_qk
        Wk = jax.random.normal(ks[2], (NHEADS * DK, INDIM), dtype=jnp.float32) * std_qk
        Wv = jax.random.normal(ks[3], (NHEADS * DV, INDIM), dtype=jnp.float32) * std_v
        std_o = np.sqrt(2.0 / (NHEADS * DV + INDIM)).astype(np.float32)
        Wo = jax.random.normal(ks[4], (INDIM, NHEADS * DV), dtype=jnp.float32) * std_o
        bq = jnp.zeros((NHEADS * DK,), jnp.float32)
        bk = jnp.zeros((NHEADS * DK,), jnp.float32)
        bv = jnp.zeros((NHEADS * DV,), jnp.float32)
        bo = jnp.zeros((INDIM,), jnp.float32)
        return {'x': x, 'Wq': Wq, 'bq': bq, 'Wk': Wk, 'bk': bk, 'Wv': Wv, 'bv': bv, 'Wo': Wo, 'bo': bo}
    _L0_attn_in = _L0_attn_setup()

    def _L0_ffn_setup():
        import jax, jax.numpy as jnp
        import numpy as np
        D_MODEL = 128
        N_HEADS = 16
        D_HEAD = D_MODEL // N_HEADS
        N_EXPERTS = 8
        TOP_K = 2
        D_FF = 256
        EPS = 1e-06

        def rmsnorm(x, w):
            return x * jax.lax.rsqrt(jnp.mean(x * x, axis=-1, keepdims=True) + EPS) * w

        def swiglu(x, w_gate, w_up, w_down):
            return jax.nn.silu(x @ w_gate) * (x @ w_up) @ w_down
        key = jax.random.key(seed)
        ks = jax.random.split(key, 16)
        s = 0.02
        B, S = (2, 256)
        return {'X': jax.random.normal(ks[0], (B, S, D_MODEL), dtype=jnp.float32), 'norm1_w': jnp.ones((D_MODEL,), jnp.float32), 'norm2_w': jnp.ones((D_MODEL,), jnp.float32), 'wq': jax.random.normal(ks[1], (D_MODEL, D_MODEL), jnp.float32) * s, 'wk': jax.random.normal(ks[2], (D_MODEL, D_MODEL), jnp.float32) * s, 'wv': jax.random.normal(ks[3], (D_MODEL, D_MODEL), jnp.float32) * s, 'wo': jax.random.normal(ks[4], (D_MODEL, D_MODEL), jnp.float32) * s, 'router_w': jax.random.normal(ks[5], (D_MODEL, N_EXPERTS), jnp.float32) * s, 'sh_gate': jax.random.normal(ks[6], (D_MODEL, D_FF), jnp.float32) * s, 'sh_up': jax.random.normal(ks[7], (D_MODEL, D_FF), jnp.float32) * s, 'sh_down': jax.random.normal(ks[8], (D_FF, D_MODEL), jnp.float32) * s, 'e_gate': jax.random.normal(ks[9], (N_EXPERTS, D_MODEL, D_FF), jnp.float32) * s, 'e_up': jax.random.normal(ks[10], (N_EXPERTS, D_MODEL, D_FF), jnp.float32) * s, 'e_down': jax.random.normal(ks[11], (N_EXPERTS, D_FF, D_MODEL), jnp.float32) * s}
    _L0_ffn_in = _L0_ffn_setup()

    def _L1_attn_setup():
        import jax, jax.numpy as jnp
        import numpy as np
        import math
        N_HEAD = 16
        DEG = 2
        EPS = 1e-07
        key = jax.random.key(seed)
        k1, k2 = jax.random.split(key)
        B, T, C = (2, 256, 128)
        x = jax.random.normal(k1, (B, T, C), dtype=jnp.float32)
        W = jax.random.normal(k2, (3 * C + N_HEAD, C), dtype=jnp.float32) * (1.0 / math.sqrt(C))
        return {'x': x, 'W': W}
    _L1_attn_in = _L1_attn_setup()

    def _L1_ffn_setup():
        import math
        import jax, jax.numpy as jnp
        import numpy as np
        NUM_EXPERTS = 8
        TOP_K = 2
        CAPACITY_FACTOR = 1.0
        B, S, H, I = (4, 256, 128, 512)
        key = jax.random.key(seed)
        k_x, k_rw, k_wi, k_wo = jax.random.split(key, 4)
        x = jax.random.normal(k_x, (B, S, H), dtype=jnp.float32)
        lim = math.sqrt(6.0 / (H + NUM_EXPERTS))
        router_w = jax.random.uniform(k_rw, (NUM_EXPERTS, H), minval=-lim, maxval=lim, dtype=jnp.float32)
        router_b = jnp.zeros((NUM_EXPERTS,), dtype=jnp.float32)
        experts_inter = jax.random.normal(k_wi, (NUM_EXPERTS - 1, H, I), dtype=jnp.float32) / math.sqrt(H)
        experts_out = jax.random.normal(k_wo, (NUM_EXPERTS - 1, I, H), dtype=jnp.float32) / math.sqrt(I)
        return {'x': x, 'router_w': router_w, 'router_b': router_b, 'experts_inter': experts_inter, 'experts_out': experts_out}
    _L1_ffn_in = _L1_ffn_setup()
    _d = {'L0_attn_x': _L0_attn_in['x'], 'L0_attn_Wq': _L0_attn_in['Wq'], 'L0_attn_bq': _L0_attn_in['bq'], 'L0_attn_Wk': _L0_attn_in['Wk'], 'L0_attn_bk': _L0_attn_in['bk'], 'L0_attn_Wv': _L0_attn_in['Wv'], 'L0_attn_bv': _L0_attn_in['bv'], 'L0_attn_Wo': _L0_attn_in['Wo'], 'L0_attn_bo': _L0_attn_in['bo'], 'L0_ffn_norm1_w': _L0_ffn_in['norm1_w'], 'L0_ffn_norm2_w': _L0_ffn_in['norm2_w'], 'L0_ffn_wq': _L0_ffn_in['wq'], 'L0_ffn_wk': _L0_ffn_in['wk'], 'L0_ffn_wv': _L0_ffn_in['wv'], 'L0_ffn_wo': _L0_ffn_in['wo'], 'L0_ffn_router_w': _L0_ffn_in['router_w'], 'L0_ffn_sh_gate': _L0_ffn_in['sh_gate'], 'L0_ffn_sh_up': _L0_ffn_in['sh_up'], 'L0_ffn_sh_down': _L0_ffn_in['sh_down'], 'L0_ffn_e_gate': _L0_ffn_in['e_gate'], 'L0_ffn_e_up': _L0_ffn_in['e_up'], 'L0_ffn_e_down': _L0_ffn_in['e_down'], 'L1_attn_W': _L1_attn_in['W'], 'L1_ffn_router_w': _L1_ffn_in['router_w'], 'L1_ffn_router_b': _L1_ffn_in['router_b'], 'L1_ffn_experts_inter': _L1_ffn_in['experts_inter'], 'L1_ffn_experts_out': _L1_ffn_in['experts_out']}
    _x0 = _d['L0_attn_x']
    _d['L0_attn_x'] = jax.random.normal(jax.random.fold_in(jax.random.key(seed), 1), (16, 256, 128), dtype=_x0.dtype)
    del _x0
    return _d

def reference(L0_attn_x, L0_attn_Wq, L0_attn_bq, L0_attn_Wk, L0_attn_bk, L0_attn_Wv, L0_attn_bv, L0_attn_Wo, L0_attn_bo, L0_ffn_norm1_w, L0_ffn_norm2_w, L0_ffn_wq, L0_ffn_wk, L0_ffn_wv, L0_ffn_wo, L0_ffn_router_w, L0_ffn_sh_gate, L0_ffn_sh_up, L0_ffn_sh_down, L0_ffn_e_gate, L0_ffn_e_up, L0_ffn_e_down, L1_attn_W, L1_ffn_router_w, L1_ffn_router_b, L1_ffn_experts_inter, L1_ffn_experts_out):

    def _L0_attn_ref(x, Wq, bq, Wk, bk, Wv, bv, Wo, bo):
        import jax, jax.numpy as jnp
        import numpy as np
        INDIM = 128
        NHEADS = 16
        DK = INDIM // NHEADS
        DV = INDIM // NHEADS
        B, S = (4, 256)
        b, s, _ = x.shape
        q = (x @ Wq.T + bq).reshape(b, s, NHEADS, DK)
        k = (x @ Wk.T + bk).reshape(b, s, NHEADS, DK)
        v = (x @ Wv.T + bv).reshape(b, s, NHEADS, DV)
        w = jnp.einsum('bshd,bzhd->bhsz', q, k)
        w = w / jnp.sqrt(jnp.float32(DV))
        w = jax.nn.softmax(w, axis=-1)
        vw = jnp.einsum('bhsz,bzhd->bshd', w, v)
        vw = vw.reshape(b, s, NHEADS * DV)
        out = vw @ Wo.T + bo
        return out

    def _L0_ffn_ref(X, norm1_w, norm2_w, wq, wk, wv, wo, router_w, sh_gate, sh_up, sh_down, e_gate, e_up, e_down):
        import jax, jax.numpy as jnp
        import numpy as np
        D_MODEL = 128
        N_HEADS = 16
        D_HEAD = D_MODEL // N_HEADS
        N_EXPERTS = 8
        TOP_K = 2
        D_FF = 256
        EPS = 1e-06

        def rmsnorm(x, w):
            return x * jax.lax.rsqrt(jnp.mean(x * x, axis=-1, keepdims=True) + EPS) * w

        def swiglu(x, w_gate, w_up, w_down):
            return jax.nn.silu(x @ w_gate) * (x @ w_up) @ w_down
        B, S, d = X.shape
        scale = 1.0 / jnp.sqrt(jnp.asarray(D_HEAD, X.dtype))
        h = rmsnorm(X, norm1_w)
        q = (h @ wq).reshape(B, S, N_HEADS, D_HEAD)
        k = (h @ wk).reshape(B, S, N_HEADS, D_HEAD)
        v = (h @ wv).reshape(B, S, N_HEADS, D_HEAD)
        scores = jnp.einsum('bshd,bthd->bhst', q, k) * scale
        attn = jax.nn.softmax(scores, axis=-1)
        ctx = jnp.einsum('bhst,bthd->bshd', attn, v).reshape(B, S, d)
        X = X + ctx @ wo
        h2 = rmsnorm(X, norm2_w).reshape(B * S, d)
        logits = h2 @ router_w
        probs = jax.nn.softmax(logits, axis=-1)
        topw, topi = jax.lax.top_k(probs, TOP_K)
        topw = jax.nn.softmax(topw, axis=-1)
        combine = jnp.sum(jax.nn.one_hot(topi, N_EXPERTS, dtype=h2.dtype) * topw[..., None], axis=1)
        shared = swiglu(h2, sh_gate, sh_up, sh_down)
        gate = jnp.einsum('td,edf->etf', h2, e_gate)
        up = jnp.einsum('td,edf->etf', h2, e_up)
        eout = jnp.einsum('etf,efd->etd', jax.nn.silu(gate) * up, e_down)
        spec = jnp.einsum('etd,te->td', eout, combine)
        moe_out = (shared + spec).reshape(B, S, d)
        return X + moe_out

    def _L1_attn_ref(x, W):
        import jax, jax.numpy as jnp
        import numpy as np
        import math
        N_HEAD = 16
        DEG = 2
        EPS = 1e-07
        B, T, C = x.shape
        nh = N_HEAD
        hs = C // nh
        scale = 1.0 / math.sqrt(hs)
        qkvgr = jnp.einsum('btc,oc->bto', x, W)
        q, k, v = (qkvgr[..., :C], qkvgr[..., C:2 * C], qkvgr[..., 2 * C:3 * C])
        log_g = jax.nn.log_sigmoid(qkvgr[..., 3 * C:].astype(jnp.float32))
        log_G = jnp.cumsum(log_g, axis=1).transpose(0, 2, 1)

        def heads(a):
            return a.reshape(B, T, nh, hs).transpose(0, 2, 1, 3)
        Q, K, V = (heads(q), heads(k), heads(v))
        S = jnp.einsum('bhtd,bhsd->bhts', Q, K)
        Tm = DEG * jnp.log(jnp.abs(S) + EPS) + jnp.log(jnp.float32(scale))
        Z = Tm + log_G[..., :, None] - log_G[..., None, :]
        mask = jnp.tril(jnp.ones((T, T), dtype=bool))
        Z = jnp.where(mask, Z, -jnp.inf)
        Z_rowmax = jax.lax.stop_gradient(jnp.max(Z, axis=-1, keepdims=True))
        P = jnp.exp(Z - Z_rowmax)
        norm = jnp.sum(P, axis=-1)
        O = jnp.einsum('bhts,bhsd->bhtd', P, V)
        y = O / norm[..., None]
        return y.transpose(0, 2, 1, 3).reshape(B, T, C)

    def _L1_ffn_ref(x, router_w, router_b, experts_inter, experts_out):
        import math
        import jax, jax.numpy as jnp
        import numpy as np
        NUM_EXPERTS = 8
        TOP_K = 2
        CAPACITY_FACTOR = 1.0
        B, S, H, I = (4, 256, 128, 512)
        batch, seq, hidden = x.shape
        n_exp = router_w.shape[0]
        n_tok = batch * seq
        cap = math.ceil(n_tok / n_exp * CAPACITY_FACTOR)
        logits = jnp.einsum('bsh,eh->bse', x, router_w) + router_b
        weights_flat = jax.nn.softmax(logits, axis=-1).reshape(n_tok, n_exp)
        x_flat = x.reshape(n_tok, hidden)
        topk_vals, topk_idx = jax.lax.top_k(weights_flat, TOP_K)
        rows = jnp.arange(n_tok)[:, None]
        topk_flat = jnp.zeros_like(weights_flat).at[rows, topk_idx].set(topk_vals)
        routing_mask = (topk_flat > 0).astype(jnp.int32)
        noop_w = topk_flat[:, -1]
        noop_mask = routing_mask[:, -1].astype(x.dtype)
        expert_w = topk_flat[:, :-1]
        expert_mask = routing_mask[:, :-1]
        sorted_indices = jnp.argsort(-expert_mask, axis=0)[:cap]
        sorted_mask = jnp.take_along_axis(expert_mask, sorted_indices, axis=0)
        used_idx = (sorted_indices * sorted_mask).reshape(-1)
        inputs = x_flat[used_idx] * sorted_mask.reshape(-1).astype(x.dtype)[:, None]
        inputs = inputs.reshape(cap, n_exp - 1, hidden)
        in_w = jnp.take_along_axis(expert_w, sorted_indices, axis=0)
        h = jax.nn.relu(jnp.einsum('ceh,ehi->cei', inputs, experts_inter))
        out = jnp.einsum('cei,eih->ceh', h, experts_out) * in_w[..., None]
        combined = jnp.zeros_like(x_flat).at[used_idx].add(out.reshape(-1, hidden))
        combined = combined + x_flat * (noop_w * noop_mask)[:, None]
        return combined.reshape(batch, seq, hidden)
    x = L0_attn_x
    x = x + _layernorm(_L0_attn_ref(_layernorm(x, axis=-1), L0_attn_Wq, L0_attn_bq, L0_attn_Wk, L0_attn_bk, L0_attn_Wv, L0_attn_bv, L0_attn_Wo, L0_attn_bo), axis=-1)
    x = x + _layernorm(_L0_ffn_ref(_layernorm(x, axis=-1), L0_ffn_norm1_w, L0_ffn_norm2_w, L0_ffn_wq, L0_ffn_wk, L0_ffn_wv, L0_ffn_wo, L0_ffn_router_w, L0_ffn_sh_gate, L0_ffn_sh_up, L0_ffn_sh_down, L0_ffn_e_gate, L0_ffn_e_up, L0_ffn_e_down), axis=-1)
    x = x + _layernorm(_L1_attn_ref(_layernorm(x, axis=-1), L1_attn_W), axis=-1)
    x = x + _layernorm(_L1_ffn_ref(_layernorm(x, axis=-1), L1_ffn_router_w, L1_ffn_router_b, L1_ffn_experts_inter, L1_ffn_experts_out), axis=-1)
    return x

_drawn_inputs = setup_inputs


def setup_inputs(seed=0):
    import zlib

    import numpy as np

    out = dict(_drawn_inputs(seed))
    spreads = {'L0_attn_bq': (0.0, 0.1),
     'L0_attn_bk': (0.0, 0.8),
     'L0_attn_bv': (0.0, 0.1),
     'L0_attn_bo': (0.0, 0.1),
     'L0_ffn_norm1_w': (1.0, 0.6),
     'L0_ffn_norm2_w': (1.0, 0.6),
     'L1_ffn_router_b': (0.0, 0.1)}
    factors = {'L0_ffn_wq': 8.0,
     'L0_ffn_wk': 8.0,
     'L0_ffn_router_w': 3.108,
     'L0_ffn_sh_gate': 3.273,
     'L0_ffn_sh_up': 2.885,
     'L0_ffn_sh_down': 3.424,
     'L0_ffn_e_gate': 2.947,
     'L0_ffn_e_up': 2.778,
     'L0_ffn_e_down': 2.975}
    for name, (base, spread) in spreads.items():
        noise = np.random.default_rng([zlib.crc32(name.encode()), seed]).standard_normal(out[name].shape)
        drawn = base * np.exp(spread * noise) if base else spread * noise
        out[name] = jnp.asarray(drawn.astype(out[name].dtype))
    for name, factor in factors.items():
        out[name] = (out[name] * factor).astype(out[name].dtype)
    return out
```

```python
from contextlib import ExitStack

import concourse.bass as bass
from concourse import mybir
import numpy as np

F32 = mybir.dt.float32
F16 = mybir.dt.float16
BF16 = mybir.dt.bfloat16
I32 = mybir.dt.int32
U32 = mybir.dt.uint32
ALU = mybir.AluOpType
ACT = mybir.ActivationFunctionType
AX = mybir.AxisListType
ds = bass.ds

P = 128
NB, S, D = 16, 256, 128
NT = NB * S
NTILE = NT // P
TC = S // P
H, DH = 16, 8
NG, NJ = 4, 4
NE = 8
F0 = 256
F1 = 512
EPS_LN = 1e-5
EPS_RMS = 1e-6
EPS_POW = 1e-7
SCALE = float(DH) ** -0.5
SHIFT_ROW = 24
MASKED = -1e30
BIAS_RMS, BIAS_PLAIN = 0, 1

C_IDENT = 0
C_TRI = 128
C_LATE = 384
C_COL = 512
(K_LOW_Q, K_LOW_K, K_SHIFT, K_M0, K_M1, K_M2, K_M345, K_N3, K_N4, K_N5, K_M012) = range(11)
C_PRI = C_COL + 16
C_BASE = C_PRI + 8
C_ALL = C_BASE + 8


def constant_table():
    c = np.zeros((P, C_ALL), np.float32)
    p = np.arange(P)
    c[:, C_IDENT:C_IDENT + P] = np.eye(P)
    c[:, C_TRI:C_TRI + P] = p[:, None] <= p[None, :]
    c[:, C_TRI + P:C_TRI + 2 * P] = 1.0
    c[:, C_LATE:C_LATE + P] = np.where(p[:, None] > p[None, :], MASKED, 0.0)
    r = p % 32
    c[:, C_COL + K_LOW_Q] = -1.0 * ((r >= 16) & (r < 24))
    c[:, C_COL + K_LOW_K] = -1.0 * ((r >= 8) & (r < 16))
    c[:, C_COL + K_SHIFT] = r == SHIFT_ROW
    r = p % 8
    for k in range(3):
        c[:, C_COL + K_M0 + k] = r == k
        c[:, C_COL + K_N3 + k] = -1.0 * (r == 3 + k)
    c[:, C_COL + K_M345] = (r >= 3) & (r < 6)
    c[:, C_COL + K_M012] = r < 3
    c[:, C_PRI:C_PRI + 8] = 8 - np.arange(8)
    c[:, C_BASE:C_BASE + 8] = np.arange(8) * 512
    return c


def has(b):
    return not isinstance(b, int) or 0 <= b < NB


def upto(eng, sem, per, b, k):
    if isinstance(b, int) and per * b + k <= 0:
        return
    eng.wait_ge(sem, b * per + k)


def drive(eng, body):
    for b in (-2, -1, 0, 1):
        body(b, b % 3)
    with eng.Fori(0, 4) as i:
        for k in range(3):
            body(i * 3 + (2 + k), (2 + k) % 3)
    for b in range(14, NB + 1):
        body(b, b % 3)


class Link:

    def __init__(self, eng, sem, per, b):
        self.eng, self.sem, self.per, self.b, self.k = eng, sem, per, b, 0

    def __call__(self, *instructions):
        for ins in instructions:
            self.k += 1
            ins.then_inc(self.sem, 1)
        self.eng.wait_ge(self.sem, self.b * self.per + self.k)

    def skip_to(self, k):
        self.k = k
        return self


def semaphores(nc, ctx):
    taken = []

    def clear():
        nc.clear_and_free_semaphores(taken)
        nc.all_engine_barrier()

    def take(name):
        taken.append(nc.alloc_semaphore(name))
        return taken[-1]

    ctx.callback(clear)
    return take


def attention_layer(nc, kind, X, XB, cst, cstb, w):
    soft = kind < 2
    lag = 1 if soft else 3
    NU = H // 2
    WU = 2 * S * 2 if soft else 2 * S + 2 * P
    LINKS_LN = 10 if kind == 1 else 5
    with ExitStack() as ctx:
        take = semaphores(nc, ctx)

        def sb(name, shape, dt):
            return ctx.enter_context(nc.sbuf_tensor(f"{name}{kind}", shape, dt))

        def pb(name, shape, dt):
            return ctx.enter_context(nc.psum_tensor(f"{name}{kind}", shape, dt))

        def sem(name):
            return take(f"{name}{kind}")

        score_ps = pb("score", [P, 2, 512], F32)
        st_ps = pb("st", [P, 2, 1024], F32)
        pv_ps = pb("pv", [P, 512], F32)
        misc = pb("misc", [P, 512], F32)

        pad = sb("pad", [1, 1], F32)
        stats = sb("stats", [P, TC, 6], F32)
        mv = sb("mv", [P, TC, 2], F32)
        ve = sb("ve", [P, 2, TC], F32)
        rs = sb("rs", [P, 2, TC], F32)
        half = sb("half", [P, TC], F32)
        pstats = sb("pstats", [P, TC, 6], F32)
        pmv = sb("pmv", [P, TC, 2], F32)
        pve = sb("pve", [P, TC], F32)
        prs = sb("prs", [P, TC], F32)
        y = sb("y", [P, TC, D], F32)
        yT = sb("yT", [P, S], F32)
        xq = sb("xq", [P, 2, 2, S], F32)
        hi = sb("hi", [P, 2, 2, S], F16)
        Kp = sb("Kp", [P, NG, S], F16)
        Qp = sb("Qp", [P, 3, NG, S], F16)
        Kz = sb("Kz", [P, 3, NG, NJ, S], F16)
        Vx = sb("Vx", [P, 3, TC, H, 32], F32)
        PT = sb("PT", [P, 2, WU], F32)
        OS = sb("OS", [P, 2, 2, S], F32)
        rc = sb("rc", [P, TC, 8], F32)
        yn = sb("yn", [P, TC, D], F32)
        ynT = sb("ynT", [P, S], F32)
        ob = sb("ob", [P, TC, D], F32)
        tmp = sb("tmp", [P, TC, D], F32)
        if kind == 1:
            tmp2 = sb("tmp2", [P, 2, TC], F32)
            rs2 = sb("rs2", [P, TC], F32)
        if soft:
            mxs = sb("mxs", [P, 2, TC, 8], F32)
            nm = sb("nm", [8, 2, S], F16)
        else:
            rr = sb("rr", [P, 2, WU], F32)
            tt = sb("tt", [P, 2, WU], F32)
            uu = sb("uu", [P, 2, WU], F32)
            gl = sb("gl", [P, TC, H], F32)
            ga = sb("ga", [P, TC, H], F32)
            gm = sb("gm", [P, TC, H], F32)
            ge = sb("ge", [P, TC, H], F32)
            lgr = sb("lgr", [P, TC, H, 8], F32)
            LG = sb("LG", [P, S], F32)
            l1 = sb("l1", [P, S], BF16)
            l2 = sb("l2", [P, S], BF16)
            l3 = sb("l3", [P, S], BF16)
            lrem = sb("lrem", [P, 2, S], F32)
            Mt = sb("Mt", [P, 2, S], BF16)
            Ms = sb("Ms", [P, 3, 2, S], BF16)
            Mz = sb("Mz", [P, 3, H, S], BF16)

        steps = (["MXb", "OTa", "T", "OTb", "Qa", "YT", "Ka", "PR", "Qb", "Kb", "MXa", "V"] if soft
                 else ["OTa", "T", "Qa", "CS", "Ka", "OTb", "Qb", "Kb", "V"])
        offset = dict(MXb=0, OTa=-1, T=2, OTb=-1, Qa=2, YT=-1, Ka=2, PR=-1, Qb=2, Kb=2, MXa=1, V=2, CS=1)
        full = {n: sem(f"full_{n}") for n in steps}
        free = {n: sem(f"free_{n}") for n in steps}
        s_init = sem("s_init")
        s_ve = sem("s_ve")
        s_rs = sem("s_rs")
        s_y = sem("s_y")
        s_pack = sem("s_pack")
        s_kz = [sem(f"s_kz{a}") for a in range(2)]
        s_S = sem("s_S")
        s_max = sem("s_max")
        s_sh = [sem(f"s_sh{a}") for a in range(2)]
        s_st = sem("s_st")
        s_exp = sem("s_exp")
        s_pv = sem("s_pv")
        s_os = sem("s_os")
        s_ln = sem("s_ln")
        s_lp = sem("s_lp")
        s_lo = sem("s_lo")
        s_pve = sem("s_pve")
        s_prs = sem("s_prs")
        s_post = sem("s_post")
        if not soft:
            s_dexp = sem("s_dexp")
            s_t = sem("s_t")
            s_u = sem("s_u")
            s_sqd = sem("s_sqd")
            s_sqp = sem("s_sqp")
            s_gl = sem("s_gl")
            s_ga = sem("s_ga")
            s_ge = sem("s_ge")
            s_gd = sem("s_gd")
            s_lgr = sem("s_lgr")
            s_lm = sem("s_lm")
            s_mz = sem("s_mz")

        def before(name, b):
            at, body = steps.index(name), b
            while True:
                at -= 1
                if at < 0:
                    at, body = len(steps) - 1, body - 1
                if isinstance(body, int) and body < -2:
                    return None
                if has(body + offset[steps[at]]):
                    return steps[at], body + offset[steps[at]]

        BY_DVE = (1, 4, 6)

        def squared(eng, b, u):
            if soft:
                upto(eng, s_exp, NU, b, u + 1)
            elif u in BY_DVE:
                upto(eng, s_sqd, len(BY_DVE), b, sum(v <= u for v in BY_DVE))
            else:
                upto(eng, s_sqp, NU - len(BY_DVE), b, sum(v not in BY_DVE for v in range(u + 1)))

        def squares(eng, b, u):
            u, b = (u - 1, b) if u >= 1 else (NU - 1, b - 1)
            by_dve = u in BY_DVE
            if has(b) and by_dve == (eng is nc.vector):
                upto(eng, s_u, NU, b, u + 1)
                upto(eng, s_pv, NU, b, u - 1)
                eng.tensor_tensor(PT[:, u % 2, :], uu[:, u % 2, :], uu[:, u % 2, :], ALU.mult)\
                   .then_inc(s_sqd if by_dve else s_sqp, 1)

        block = ctx.enter_context(nc.Block())

        @block.sync
        def _(sp):
            def body(b, slot):
                nxt = (slot + 2) % 3
                if soft and has(b):
                    upto(sp, free["MXb"], 1, b, 1)
                    for j in range(NJ):
                        sp.dma_start(Qp[32 * j + SHIFT_ROW:32 * j + SHIFT_ROW + 1, slot, 2:4, :],
                                     nm[2 * j:2 * j + 2, 1, :]).then_inc(s_sh[1], 16)
                if not soft and has(b + 1):
                    upto(sp, s_lm, 10, b + 1, 10)
                    for h in range(H):
                        sp.dma_start(Mz[8 * h:8 * h + 8, (slot + 1) % 3, h, :],
                                     Mt[8 * h:8 * h + 8, 1, :]).then_inc(s_mz, 16)
                for a in range(2):
                    if has(b + 2):
                        upto(sp, s_pack, 8, b + 2, 4 * a + 4)
                        upto(sp, s_st, NU, b - 1, NU)
                        if a == 0:
                            sp.wait_ge(s_init, 5)
                        for j in range(NJ):
                            sp.dma_start(Kz[32 * j:32 * j + 32, nxt, 2 * a:2 * a + 2, j, :],
                                         Kp[32 * j:32 * j + 32, 2 * a:2 * a + 2, :]).then_inc(s_kz[a], 16)
                if soft and has(b + 1):
                    upto(sp, free["MXa"], 1, b + 1, 1)
                    for j in range(NJ):
                        sp.dma_start(Qp[32 * j + SHIFT_ROW:32 * j + SHIFT_ROW + 1, (slot + 1) % 3, 0:2, :],
                                     nm[2 * j:2 * j + 2, 0, :]).then_inc(s_sh[0], 16)

            drive(sp, body)

        @block.gpsimd
        def _(pool):
            pool.memset(half[:], -0.5).then_inc(s_init, 1)
            pool.memset(Kz[:].rearrange("p a g j s -> p (a g j s)").bitcast(F32), 0.0).then_inc(s_init, 1)
            if not soft:
                pool.memset(Mz[:].rearrange("p a h s -> p (a h s)").bitcast(F32), 0.0).then_inc(s_init, 1)
            else:
                pool.memset(tmp[:], 0.0).then_inc(s_init, 1)
            pool.wait_ge(s_init, 3)

            def body(b, slot):
                nxt = (slot + 2) % 3
                for u in range(NU):
                    if u == 0 and has(b + 2):
                        for k in range(2 if kind == 1 else 1):
                            upto(pool, s_ve, 2 if kind == 1 else 1, b + 2, k + 1)
                            pool.tensor_tensor(rs[:, k, :], ve[:, k, :], half[:], ALU.pow).then_inc(s_rs, 1)
                    if not soft:
                        squares(pool, b, u)
                    if u == 6 and kind != 1 and has(b - 1):
                        upto(pool, s_pve, 1, b - 1, 1)
                        pool.tensor_tensor(prs[:], pve[:], half[:], ALU.pow).then_inc(s_prs, 1)

            drive(pool, body)

        @block.scalar
        def _(act):
            def drain(name, b):
                upto(act, full[name], 1, b, 1)

            def project(b, n, name):
                drain(name, b)
                upto(act, s_pack, 8, b, 2 * n - 2)
                if kind == 0:
                    bias = w["bq"] if n % 2 == 0 else w["bk"]
                    for k in range(2):
                        last = act.activation(xq[:, n % 2, k, :], misc[:, k * S:(k + 1) * S], ACT.Identity,
                                              bias=bias[:, n // 2 * 2 + k:n // 2 * 2 + k + 1])
                    last.then_inc(free[name], 1)
                    return
                flat = xq[:, n % 2, :, :].rearrange("p a s -> p (a s)")
                if n % 2 == 0 or not soft:
                    act.activation(flat, misc[:, :], ACT.Copy).then_inc(free[name], 1)
                else:
                    act.activation(flat, misc[:, :], ACT.Identity,
                                   bias=cst[:, C_COL + K_SHIFT:C_COL + K_SHIFT + 1]).then_inc(free[name], 1)

            def body(b, slot):
                nxt = (slot + 2) % 3
                for u in range(NU):
                    if soft and u == 0 and has(b):
                        drain("MXb", b)
                        upto(act, s_sh[1], 64, b - 1, 64)
                        act.activation(nm[:, 1, :], misc[0:8, 0:S], ACT.Copy, scale=-1.0).then_inc(free["MXb"], 1)
                    if u == lag and has(b - 1):
                        upto(act, s_pv, NU, b - 1, 8)
                        upto(act, full["OTb"], 1, b - 2, 1)
                        act.activation(OS[:, 1, :, :].rearrange("p a s -> p (a s)"), pv_ps[:], ACT.Copy)\
                           .then_inc(s_os, 1)
                    if u == 4 + lag and has(b):
                        upto(act, s_pv, NU, b, 4)
                        upto(act, full["OTa"], 1, b - 1, 1)
                        act.activation(OS[:, 0, :, :].rearrange("p a s -> p (a s)"), pv_ps[:], ACT.Copy)\
                           .then_inc(s_os, 1)
                    if soft and has(b):
                        upto(act, s_st, NU, b, u + 1)
                        upto(act, s_pv, NU, b, u - 1)
                        act.activation(PT[:, u % 2, :], st_ps[:, u % 2, :], ACT.Exp, scale=SCALE).then_inc(s_exp, 1)
                    if not soft:
                        if has(b):
                            upto(act, s_S, NU, b, u + 1)
                            upto(act, s_u, NU, b, u - 1)
                            act.activation(rr[:, u % 2, :], score_ps[:].rearrange("p a s -> p (a s)")[:, 0:WU],
                                           ACT.Exp, scale=0.5).then_inc(s_dexp, 1)
                            upto(act, s_st, NU, b, u + 1)
                            upto(act, s_u, NU, b, u - 1)
                            act.activation(tt[:, u % 2, :], st_ps[:, u % 2, 0:WU], ACT.Abs).then_inc(s_t, 1)
                        if u == 1 and has(b + 1):
                            upto(act, s_ga, 2, b + 1, 2)
                            upto(act, s_lgr, 1, b, 1)
                            act.activation(ge[:], ga[:], ACT.Exp, scale=-1.0).then_inc(s_ge, 1)
                            upto(act, s_ge, 2, b + 1, 1)
                            act.activation(ge[:], ge[:], ACT.Ln, bias=1.0).then_inc(s_ge, 1)
                    if u == 2 and has(b + 2):
                        drain("T", b + 2)
                        upto(act, full["V"], 1, b + 1, 1)
                        act.activation(yT[:], misc[:, 0:S], ACT.Copy).then_inc(free["T"], 1)
                    if has(b + 2) and 3 <= u <= 6:
                        project(b + 2, u - 3, ["Qa", "Ka", "Qb", "Kb"][u - 3])
                    if soft and u == 3 and has(b - 1):
                        drain("YT", b - 1)
                        upto(act, full["PR"], 1, b - 2, 1)
                        act.activation(ynT[:], misc[:, 0:S], ACT.Copy).then_inc(free["YT"], 1)
                    if soft and u == 4 and has(b - 1):
                        drain("PR", b - 1)
                        upto(act, s_post, 1, b - 2, 1)
                        act.activation(ob[:].rearrange("p c d -> p (c d)"), misc[:, 0:S], ACT.Copy)\
                           .then_inc(free["PR"], 1)
                    if soft and u == 6 and has(b + 1):
                        drain("MXa", b + 1)
                        upto(act, s_sh[0], 64, b, 64)
                        act.activation(nm[:, 0, :], misc[0:8, 0:S], ACT.Copy, scale=-1.0).then_inc(free["MXa"], 1)
                    if u == 7 and has(b + 2):
                        drain("V", b + 2)
                        upto(act, s_pv, NU, b - 1, NU)
                        act.wait_ge(s_init, 5)
                        wide = misc[:].rearrange("p (c s) -> p c s", c=TC)
                        if not soft:
                            upto(act, s_ga, 2, b + 1, 2)
                            act.activation(gl[:], wide[:, :, D:D + H], ACT.Copy).then_inc(s_gl, 1)
                        act.activation(Vx[:, nxt, :, :, 0:DH],
                                       wide[:, :, 0:D].rearrange("p c (h d) -> p c h d", d=DH), ACT.Copy)\
                           .then_inc(free["V"], 1)

            drive(act, body)

        @block.vector
        def _(dve):
            dve.memset(Vx[:], 0.0).then_inc(s_init, 1)
            dve.wait_ge(s_init, 4)
            dve.memset(Vx[:, :, :, :, DH:DH + 1], 1.0).then_inc(s_init, 1)

            def pack(b, slot, n):
                a, is_k = n // 2, n % 2
                lk = Link(dve, s_pack, 8, b).skip_to(2 * n)
                upto(dve, free[["Qa", "Ka", "Qb", "Kb"][n]], 1, b, 1)
                upto(dve, s_pack, 8, b, 2 * n - 2)
                lk(dve.tensor_copy(hi[:, n % 2, :, :].rearrange("p a s -> p (a s)"),
                                   xq[:, n % 2, :, :].rearrange("p a s -> p (a s)")))
                mask = cst[:, C_COL + (K_LOW_K if is_k else K_LOW_Q):][:, 0:1]
                if is_k:
                    upto(dve, s_kz[a], 64, b - 1, 64)
                    dst = Kp[:, 2 * a:2 * a + 2, :]
                else:
                    upto(dve, s_st, NU, b - 3, NU)
                    dst = Qp[:, slot, 2 * a:2 * a + 2, :]
                dve.scalar_tensor_tensor(dst, hi[:, n % 2, :, :], mask, xq[:, n % 2, :, :], ALU.mult, ALU.add)\
                   .then_inc(s_pack, 1)

            def ln_stats(b):
                lk = Link(dve, s_ln, LINKS_LN, b)
                lk(*[dve.bn_stats(stats[:, c, :], X[:, ds(b * TC + c, 1), :].rearrange("p a d -> p (a d)"))
                     for c in range(TC)])
                dve.memset(pad[:], 0.0)
                lk(*[dve.bn_aggr(mv[:, c, :], stats[:, c, :]) for c in range(TC)])
                dve.tensor_scalar(ve[:, 0, :], mv[:, :, 1], EPS_LN, None, ALU.add).then_inc(s_ve, 1)
                if kind == 1:
                    upto(dve, s_rs, 2, b, 1)
                    lk(dve.tensor_tensor(tmp2[:, 0, :], mv[:, :, 1], rs[:, 0, :], ALU.mult))
                    lk(dve.tensor_tensor(tmp2[:, 1, :], tmp2[:, 0, :], rs[:, 0, :], ALU.mult))
                    dve.tensor_scalar(ve[:, 1, :], tmp2[:, 1, :], EPS_RMS, None, ALU.add).then_inc(s_ve, 1)

            def ln_apply(b):
                lk = Link(dve, s_ln, LINKS_LN, b).skip_to(6 if kind == 1 else 4)
                upto(dve, s_rs, 2 if kind == 1 else 1, b, 2 if kind == 1 else 1)
                upto(dve, full["T"], 1, b - 1, 1)
                rstd = rs[:, 0, :]
                if kind == 1:
                    lk(dve.tensor_tensor(rs2[:], rs[:, 0, :], rs[:, 1, :], ALU.mult))
                    rstd = rs2[:]
                    for c in range(TC):
                        lk(dve.tensor_scalar(XB[:, ds(b * TC + c, 1), :].rearrange("p a d -> p (a d)"),
                                             X[:, ds(b * TC + c, 1), :].rearrange("p a d -> p (a d)"),
                                             mv[:, c, 0:1], rs[:, 0, c:c + 1], ALU.subtract, ALU.mult))
                for c in range(TC):
                    last = dve.tensor_scalar(y[:, c, :], X[:, ds(b * TC + c, 1), :].rearrange("p a d -> p (a d)"),
                                             mv[:, c, 0:1], rstd[:, c:c + 1], ALU.subtract, ALU.mult)
                    if c == 0:
                        last.then_inc(s_ln, 1)
                last.then_inc(s_y, 1)

            def normalize(b, a):
                name = "OTa" if a == 0 else "OTb"
                upto(dve, full[name], 1, b, 1)
                if a == 0:
                    if soft:
                        upto(dve, full["YT"], 1, b - 1, 1)
                v = misc[:].rearrange("p (c k r) -> p c k r", c=TC, r=32)
                dve.reciprocal(rc[:], v[:, :, :, DH]).then_inc(s_lo, 1)
                upto(dve, s_lo, 2, b, a + 1)
                dve.tensor_tensor(yn[:, :, 64 * a:64 * a + 64].rearrange("p c (k r) -> p c k r", r=DH),
                                  v[:, :, :, 0:DH], rc[:].unsqueeze(3).to_broadcast([P, TC, 8, DH]),
                                  ALU.mult).then_inc(free[name], 1)

            src = ob if soft else yn

            def post_stats(b):
                upto(dve, free["PR" if soft else "OTb"], 1, b, 1)
                if kind == 1:
                    xt = XB[:, ds(b * TC, TC), :]
                    dve.tensor_tensor(xt, xt, src[:], ALU.add).then_inc(s_post, 1)
                    return
                lk = Link(dve, s_lp, 6, b)
                lk(*[dve.bn_stats(pstats[:, c, :], src[:, c, :]) for c in range(TC)])
                dve.memset(pad[:], 0.0)
                lk(*[dve.bn_aggr(pmv[:, c, :], pstats[:, c, :]) for c in range(TC)])
                dve.tensor_scalar(pve[:], pmv[:, :, 1], EPS_LN, None, ALU.add).then_inc(s_pve, 1)

            def post_apply(b):
                lk = Link(dve, s_lp, 6, b).skip_to(4)
                upto(dve, s_prs, 1, b, 1)
                lk(*[dve.tensor_scalar(tmp[:, c, :], src[:, c, :], pmv[:, c, 0:1], prs[:, c:c + 1],
                                       ALU.subtract, ALU.mult) for c in range(TC)])
                xt = X[:, ds(b * TC, TC), :]
                dve.tensor_tensor(xt, xt, tmp[:], ALU.add).then_inc(s_post, 1)

            def body(b, slot):
                for u in range(NU):
                    if u == 0 and has(b + 2):
                        ln_stats(b + 2)
                    if u == 0 and has(b - 1):
                        normalize(b - 1, 0)
                    if not soft and u == 0 and has(b + 1):
                        upto(dve, s_gl, 1, b + 1, 1)
                        dve.scalar_tensor_tensor(ga[:], gl[:], -1.0, gl[:], ALU.mult, ALU.max).then_inc(s_ga, 1)
                        dve.tensor_scalar(gm[:], gl[:], 0.0, None, ALU.min).then_inc(s_ga, 1)
                    if u == 1 and has(b + 2):
                        ln_apply(b + 2)
                    if u == 2 and soft and has(b - 1):
                        normalize(b - 1, 1)
                    if u == 5 and not soft and has(b - 1):
                        normalize(b - 1, 1)
                    if soft and has(b + 1):
                        for c in range(TC):
                            upto(dve, s_S, 2 * NU, b + 1, 2 * u + c + 1)
                            if u in (0, 4) and c == 0:
                                upto(dve, full["MXa" if u == 0 else "MXb"], 1, b, 1)
                            j = 2 * (u % 2)
                            g2 = u // 2 % 2
                            dve.tensor_reduce(mxs[:, u // 4, c, 2 * j + g2:2 * j + g2 + 3:2],
                                              score_ps[:, c, :].rearrange("p (h s) -> p h s", h=2),
                                              AX.X, ALU.max).then_inc(s_max, 1)
                    if not soft:
                        squares(dve, b, u)
                    if not soft and has(b):
                        upto(dve, s_dexp, NU, b, u + 1)
                        upto(dve, s_t, NU, b, u + 1)
                        if u >= 2:
                            squared(dve, b, u - 2)
                        elif has(b - 1):
                            squared(dve, b - 1, u + NU - 2)
                        dve.scalar_tensor_tensor(uu[:, u % 2, :], tt[:, u % 2, :], EPS_POW, rr[:, u % 2, :],
                                                 ALU.add, ALU.mult).then_inc(s_u, 1)
                    if not soft and u == 2 and has(b + 1):
                        upto(dve, s_ge, 2, b + 1, 2)
                        upto(dve, full["CS"], 1, b, 1)
                        dve.tensor_tensor(lgr[:], gm[:].unsqueeze(3).to_broadcast([P, TC, H, 8]),
                                          ge[:].unsqueeze(3).to_broadcast([P, TC, H, 8]),
                                          ALU.subtract).then_inc(s_lgr, 1)
                    if not soft and u == 4 and has(b + 1):
                        cum_split(b + 1, (slot + 1) % 3)
                    if u >= 4 and has(b + 2):
                        pack(b + 2, (slot + 2) % 3, u - 4)
                    if u == 6 and has(b - 1):
                        post_stats(b - 1)
                    if u == 7 and has(b - 1) and kind != 1:
                        post_apply(b - 1)

            def cum_split(b, slot):
                upto(dve, full["CS"], 1, b, 1)
                lk = Link(dve, s_lm, 10, b)
                upto(dve, s_mz, 256, b - 1, 256)
                col = lambda k: cst[:, C_COL + k:C_COL + k + 1]
                dve.tensor_copy(LG[:], misc[:, 0:S]).then_inc(free["CS"], 1)
                upto(dve, free["CS"], 1, b, 1)
                lk(dve.tensor_copy(l1[:], LG[:]))
                lk(dve.tensor_tensor(lrem[:, 0, :], LG[:], l1[:], ALU.subtract))
                lk(dve.tensor_copy(l2[:], lrem[:, 0, :]))
                lk(dve.tensor_tensor(l3[:], lrem[:, 0, :], l2[:], ALU.subtract),
                   dve.tensor_scalar(Mt[:, 0, :], l1[:], col(K_M0), col(K_M345), ALU.mult, ALU.add),
                   dve.tensor_scalar(Ms[:, slot, 0, :], l1[:], col(K_N3), col(K_M012), ALU.mult, ALU.add))
                lk(dve.scalar_tensor_tensor(lrem[:, 0, :], l2[:], col(K_M1), Mt[:, 0, :], ALU.mult, ALU.add),
                   dve.scalar_tensor_tensor(lrem[:, 1, :], l2[:], col(K_N4), Ms[:, slot, 0, :],
                                            ALU.mult, ALU.add))
                lk(dve.scalar_tensor_tensor(Ms[:, slot, 1, :], l3[:], col(K_N5), lrem[:, 1, :],
                                            ALU.mult, ALU.add),
                   dve.scalar_tensor_tensor(Mt[:, 1, :], l3[:], col(K_M2), lrem[:, 0, :], ALU.mult, ALU.add))

            drive(dve, body)

        @block.tensor
        def _(pe):
            ident = cst[:, C_IDENT:C_IDENT + P]

            def open_bank(name, b):
                at = before(name, b)
                if at is not None:
                    upto(pe, free[at[0]], 1, at[1], 1)

            def transposes(b):
                open_bank("T", b)
                upto(pe, s_y, 1, b + 2, 1)
                for c in range(TC):
                    last = pe.transpose(misc[:, c * P:(c + 1) * P], y[:, c, :], ident)
                last.then_inc(full["T"], 1)

            def project(b, n):
                name = ["Qa", "Ka", "Qb", "Kb"][n]
                open_bank(name, b)
                upto(pe, free["T"], 1, b + 2, 1)
                wt = w["wq"] if n % 2 == 0 else w["wk"]
                for k in range(2):
                    g = n // 2 * 2 + k
                    last = pe.matmul(misc[:, k * S:(k + 1) * S], wt[:, g, :], yT[:], start=True, stop=True)
                last.then_inc(full[name], 1)

            def values(b):
                open_bank("V", b)
                n = D if soft else D + H
                for c in range(TC):
                    out = misc[:, c * S:c * S + n]
                    last = pe.matmul(out, yT[:, c * P:(c + 1) * P], w["wv"][:, 0:n], start=True, stop=kind != 0)
                    if kind == 0:
                        last = pe.matmul(out, cst[0:1, C_TRI + P:C_TRI + 2 * P], w["bv"][0:1, :],
                                         start=False, stop=True)
                last.then_inc(full["V"], 1)

            def shift_rows(b, batch, a):
                name = "MXb" if a else "MXa"
                open_bank(name, b)
                upto(pe, s_max, 2 * NU, batch, NU * (a + 1))
                for c in range(TC):
                    last = pe.transpose(misc[0:8, c * P:(c + 1) * P], mxs[:, a, c, :], ident)
                last.then_inc(full[name], 1)

            def turn_out(b, a):
                name = "OTb" if a else "OTa"
                open_bank(name, b)
                upto(pe, s_os, 2, b - 1, a + 1)
                for c in range(TC):
                    for k in range(2):
                        o = (c * 2 + k) * P
                        last = pe.transpose(misc[:, o:o + P], OS[:, a, k, c * P:(c + 1) * P], ident)
                last.then_inc(full[name], 1)

            def out_turn(b):
                open_bank("YT", b)
                upto(pe, free["OTb"], 1, b - 1, 1)
                for c in range(TC):
                    last = pe.transpose(misc[:, c * P:(c + 1) * P], yn[:, c, :], ident)
                last.then_inc(full["YT"], 1)

            def out_project(b):
                open_bank("PR", b)
                upto(pe, free["YT"], 1, b - 1, 1)
                for c in range(TC):
                    out = misc[:, c * D:(c + 1) * D]
                    last = pe.matmul(out, ynT[:, c * P:(c + 1) * P], w["wo"][:, :], start=True, stop=kind != 0)
                    if kind == 0:
                        last = pe.matmul(out, cst[0:1, C_TRI + P:C_TRI + 2 * P], w["bo"][0:1, :],
                                         start=False, stop=True)
                last.then_inc(full["PR"], 1)

            def scores(b, slot, u):
                g, j = u // 2, 2 * (u % 2)
                if u in (0, 4):
                    upto(pe, s_kz[u // 4], 64, b, 64)
                    upto(pe, s_pack, 8, b, 4 * (u // 4) + 2)
                for c in range(TC):
                    upto(pe, s_max, 2 * NU, b, 2 * u + c - 1)
                    pe.matmul(score_ps[:, c, :], Qp[:, slot, g, c * P:(c + 1) * P],
                              Kz[:, slot, g, j:j + 2, :].rearrange("p j s -> p (j s)"),
                              start=True, stop=True).then_inc(s_S, 1)

            def key_scores(b, slot, u):
                g, j = u // 2, 2 * (u % 2)
                if soft:
                    if u in (0, 4):
                        upto(pe, s_sh[u // 4], 64, b, 64)
                    upto(pe, s_exp, NU, b, u - 1)
                else:
                    if u in (0, 4):
                        upto(pe, s_kz[u // 4], 64, b, 64)
                        upto(pe, s_pack, 8, b, 4 * (u // 4) + 2)
                    upto(pe, s_t, NU, b, u - 1)
                for c in range(TC):
                    for k in range(2):
                        if soft:
                            last = pe.matmul(st_ps[:, u % 2, 2 * S * c + S * k:2 * S * c + S * k + S],
                                             Kz[:, slot, g, j + k, c * P:(c + 1) * P], Qp[:, slot, g, :],
                                             start=True, stop=True)
                        else:
                            n = S - P * c
                            o = 2 * S * c + n * k
                            last = pe.matmul(st_ps[:, u % 2, o:o + n], Kz[:, slot, g, j + k, c * P:(c + 1) * P],
                                             Qp[:, slot, g, S - n:S], start=True, stop=True)
                last.then_inc(s_st, 1)

            def decays(b, slot, u):
                if u == 0:
                    upto(pe, s_mz, 256, b, 256)
                    upto(pe, s_lm, 10, b, 10)
                upto(pe, s_dexp, NU, b, u)
                late = cstb[:, P:2 * P].unsqueeze(1).to_broadcast([P, 2, P])
                for c in range(TC):
                    n = S - P * c
                    out = score_ps[:, c, 0:2 * n].rearrange("p (h s) -> p h s", h=2)
                    pe.matmul(out, Ms[:, slot, 1, c * P:(c + 1) * P], Mz[:, slot, 2 * u:2 * u + 2, S - n:S],
                              start=True, stop=False)
                    last = pe.matmul(out[:, :, 0:P], cstb[:, 0:P], late, start=False, stop=True)
                last.then_inc(s_S, 1)

            def times_v(b, slot, u):
                g, j = u // 2, 2 * (u % 2)
                squared(pe, b, u)
                if u in (0, 4):
                    upto(pe, s_os, 2, b, u // 4)
                if u == 0:
                    upto(pe, free["V"], 1, b, 1)
                for k in range(2):
                    h = 2 * u + k
                    for c in range(TC):
                        n = S if soft else S - P * c
                        o = 2 * S * c + n * k
                        q = g % 2 * S + S
                        last = pe.matmul(pv_ps[32 * (j + k):32 * (j + k) + 32, q - n:q], Vx[:, slot, c, h, :],
                                         PT[:, u % 2, o:o + n], start=(c == 0), stop=(c == TC - 1),
                                         skip_group_check=True)
                last.then_inc(s_pv, 1)

            def body(b, slot):
                for u in range(NU):
                    if soft and has(b + 1):
                        scores(b + 1, (slot + 1) % 3, u)
                    if soft and u == 0 and has(b):
                        shift_rows(b, b, 1)
                    if u == 0 and has(b - 1):
                        turn_out(b, 0)
                    if not soft and has(b):
                        decays(b, slot, u)
                    if has(b):
                        key_scores(b, slot, u)
                    if u == 2 and has(b + 2):
                        transposes(b)
                    if soft and u == 2 and has(b - 1):
                        turn_out(b, 1)
                    if u == 3 and has(b + 2):
                        project(b, 0)
                    if not soft and u == 3 and has(b + 1):
                        cumulate(b)
                    if soft and u == 3 and has(b - 1):
                        out_turn(b)
                    if u == 4 and has(b + 2):
                        project(b, 1)
                    if not soft and u == 4 and has(b - 1):
                        turn_out(b, 1)
                    if soft and u == 4 and has(b - 1):
                        out_project(b)
                    if u == 5 and has(b + 2):
                        project(b, 2)
                    if u == 6 and has(b + 2):
                        project(b, 3)
                    if soft and u == 6 and has(b + 1):
                        shift_rows(b, b + 1, 0)
                    if u == 7 and has(b + 2):
                        values(b)
                    if u >= lag and has(b):
                        times_v(b, slot, u - lag)
                    if u < lag and has(b - 1):
                        times_v(b - 1, (slot + 2) % 3, u + NU - lag)

            def cumulate(b):
                open_bank("CS", b)
                upto(pe, s_lgr, 1, b + 1, 1)
                pe.matmul(misc[:, 0:S], lgr[:, 0, :, :].rearrange("p h r -> p (h r)"),
                          cst[:, C_TRI:C_TRI + S], start=True, stop=False)
                pe.matmul(misc[:, P:S], lgr[:, 1, :, :].rearrange("p h r -> p (h r)"),
                          cst[:, C_TRI:C_TRI + P], start=False, stop=True).then_inc(full["CS"], 1)

            drive(pe, body)


def load_weights(nc, cst, cstb, X, w, weights, dram):
    with ExitStack() as ctx:
        take = semaphores(nc, ctx)

        def sem(name):
            return take(name)

        names = ["wq0", "wk0", "wv0", "wo0", "wq2", "wk2", "wv2"]
        rows = ctx.enter_context(nc.sbuf_tensor("rows", [P, len(names), D], F32))
        gates = ctx.enter_context(nc.sbuf_tensor("gates", [H + NE, D], F32))
        flat = ctx.enter_context(nc.sbuf_tensor("flat", [P, 3, D], F32))
        norm = ctx.enter_context(nc.sbuf_tensor("norm", [P, 2], F32))
        route0 = ctx.enter_context(nc.sbuf_tensor("route0", [P, NE], F32))
        bias = ctx.enter_context(nc.sbuf_tensor("bias", [1, 2, D], F32))
        wide = ctx.enter_context(nc.sbuf_tensor("wide", [1, 2, NG, NJ, 4, DH], F32))
        turned = ctx.enter_context(nc.psum_tensor("turned", [P, 8, 512], F32))
        s_rows = sem("s_rows")
        s_flat = sem("s_flat")
        s_x = sem("s_x")
        s_zero = sem("s_zero")
        s_turned = sem("s_turned")
        s_wide = sem("s_wide")
        s_columns = sem("s_columns")
        s_done = sem("s_done")
        block = ctx.enter_context(nc.Block())
        packed = {}
        for n in range(3):
            for name in ("wq", "wk"):
                packed[name, n] = weights[n][name][:].rearrange("p g (j c d) -> p g j c d", j=NJ, c=4)

        def heads(ap):
            return ap.rearrange("p (g j d) -> p g j d", g=NG, j=NJ)

        @block.sync
        def _(sp):
            for k, src in enumerate([dram["L0_attn_Wq"], dram["L0_attn_Wk"], dram["L0_attn_Wv"], dram["L0_attn_Wo"]]):
                sp.dma_start(rows[:, k, :], src).then_inc(s_rows, 16)
            sp.dma_start(rows[:, 4:7, :], dram["L1_attn_W"][0:3 * D, :].rearrange("(a p) d -> p a d", a=3))\
                .then_inc(s_rows, 16)
            sp.dma_start(gates[0:H, :], dram["L1_attn_W"][3 * D:3 * D + H, :]).then_inc(s_rows, 16)
            sp.dma_start(gates[H:H + NE, :], dram["L1_ffn_router_w"]).then_inc(s_rows, 16)
            sp.dma_start(cst[:], dram["constants"]).then_inc(s_rows, 16)
            for k, name in enumerate(["L0_attn_bq", "L0_attn_bk"]):
                sp.dma_start(bias[0:1, k, :], dram[name].rearrange("(a d) -> a d", a=1)).then_inc(s_flat, 16)
            sp.dma_start(weights[0]["bv"][:], dram["L0_attn_bv"].rearrange("(a d) -> a d", a=1)).then_inc(s_flat, 16)
            sp.dma_start(weights[0]["bo"][:], dram["L0_attn_bo"].rearrange("(a d) -> a d", a=1)).then_inc(s_flat, 16)
            for k, name in enumerate(["L0_ffn_wq", "L0_ffn_wk", "L0_ffn_wv"]):
                sp.dma_start(flat[:, k, :], dram[name]).then_inc(s_flat, 16)
            sp.dma_start(weights[1]["wo"][:], dram["L0_ffn_wo"]).then_inc(s_flat, 16)
            sp.dma_start(route0[:], dram["L0_ffn_router_w"]).then_inc(s_flat, 16)
            sp.dma_start(norm[:, 1:2], dram["L0_ffn_norm2_w"].rearrange("(d a) -> d a", a=1)).then_inc(s_flat, 16)
            sp.dma_start(norm[:, 0:1], dram["L0_ffn_norm1_w"].rearrange("(d a) -> d a", a=1)).then_inc(s_flat, 16)
            xt = dram["L0_attn_x"].rearrange("b (c p) d -> p (b c) d", p=P)
            for k in range(4):
                sp.dma_start(X[:, 8 * k:8 * k + 8, :], xt[:, 8 * k:8 * k + 8, :]).then_inc(s_x, 16)
            sp.wait_ge(s_x, 64)

        @block.gpsimd
        def _(pool):
            for n in range(3):
                for name in ("wq", "wk"):
                    pool.memset(packed[name, n][:, :, :, 3, :], 0.0).then_inc(s_zero, 1)
            pool.memset(wide[:], 0.0).then_inc(s_zero, 1)
            pool.wait_ge(s_zero, 7)
            pool.memset(wide[:, 1, :, :, 3, 0:1], 1.0).then_inc(s_zero, 1)

        @block.tensor
        def _(pe):
            pe.wait_ge(s_rows, 128)
            for k in range(len(names)):
                pe.transpose(turned[:, k, 0:P], rows[:, k, :], cst[:, 0:P]).then_inc(s_turned, 1)
            pe.transpose(turned[:, 7, 0:H + NE], gates[:], cst[0:H + NE, 0:H + NE]).then_inc(s_turned, 1)
            pe.wait_ge(s_wide, 6)
            pe.wait_ge(s_zero, 8)
            pe.wait_ge(s_done, 3)
            for k in range(2):
                for g in range(NG):
                    last = pe.matmul(turned[:, 0, k * NG + g:k * NG + g + 1],
                                     wide[0:1, k, g, :, :, :].rearrange("p j c d -> p (j c d)"),
                                     cst[0:1, C_TRI + P:C_TRI + P + 1], start=True, stop=True)
            last.then_inc(s_columns, 1)

        @block.vector
        def _(dve):
            dve.wait_ge(s_flat, 176)
            dve.wait_ge(s_zero, 8)
            for k in range(2):
                for c in range(3):
                    dve.tensor_copy(wide[:, k, :, :, c, :], heads(bias[0:1, k, :])).then_inc(s_wide, 1)
            for k, dst in enumerate([("wq", 0), ("wk", 0), None, None, ("wq", 2), ("wk", 2)]):
                dve.wait_ge(s_turned, k + 1)
                if dst:
                    for c in range(3):
                        dve.tensor_copy(packed[dst][:, :, :, c, :], heads(turned[:, k, 0:P])).then_inc(s_done, 1)
            dve.tensor_copy(weights[0]["wv"][:], turned[:, 2, 0:P])
            dve.tensor_copy(weights[0]["wo"][:], turned[:, 3, 0:P])
            dve.wait_ge(s_turned, 8)
            dve.tensor_copy(weights[2]["wv"][:, 0:D], turned[:, 6, 0:P])
            dve.tensor_copy(weights[2]["wv"][:, D:D + H], turned[:, 7, 0:H])
            dve.tensor_copy(w["router1"][:], turned[:, 7, H:H + NE])
            for k, name in enumerate(("wq", "wk")):
                for c in range(3):
                    dve.tensor_scalar(packed[name, 1][:, :, :, c, :], heads(flat[:, k, :]), norm[:, 0:1],
                                      None, ALU.mult)
            dve.tensor_scalar(weights[1]["wv"][:], flat[:, 2, :], norm[:, 0:1], None, ALU.mult)
            dve.tensor_scalar(w["router0"][:], route0[:], norm[:, 1:2], None, ALU.mult)
            dve.tensor_copy(cstb[:, 0:P], cst[:, C_IDENT:C_IDENT + P])
            dve.tensor_copy(cstb[:, P:2 * P], cst[:, C_LATE:C_LATE + P])
            dve.wait_ge(s_columns, 1)
            dve.tensor_copy(weights[0]["bq"][:], turned[:, 0, 0:NG])
            dve.tensor_copy(weights[0]["bk"][:], turned[:, 0, NG:2 * NG]).then_inc(s_done, 1)
            dve.wait_ge(s_done, 13)


def router_layer(nc, kind, cst, src, yall, hT, logits, router):
    NBLK, TB = 8, 4
    with ExitStack() as ctx:
        take = semaphores(nc, ctx)

        def sb(name, shape, dt):
            return ctx.enter_context(nc.sbuf_tensor(f"r{name}{kind}", shape, dt))

        def sem(name):
            return take(f"r{name}{kind}")

        pad = sb("pad", [1, 1], F32)
        stats = sb("stats", [P, TB, 6], F32)
        mv = sb("mv", [P, TB, 2], F32)
        sq = sb("sq", [P, TB], F32)
        ve = sb("ve", [P, TB], F32)
        rs = sb("rs", [P, TB], F32)
        half = sb("half", [P, TB], F32)
        y = sb("y", [P, 2, TB, D], F32)
        yT = sb("yT", [P, 2, TB * P], F32)
        turn_ps = ctx.enter_context(nc.psum_tensor(f"rturn{kind}", [P, 2, 512], F32))
        log_ps = ctx.enter_context(nc.psum_tensor(f"rlog{kind}", [P, 2, 512], F32))
        s_half = sem("s_half")
        s_link = sem("s_link")
        s_ve = sem("s_ve")
        s_rs = sem("s_rs")
        s_y = sem("s_y")
        s_turn = sem("s_turn")
        s_yT = sem("s_yT")
        s_log = sem("s_log")
        s_logits = sem("s_logits")
        block = ctx.enter_context(nc.Block())
        LINKS = 10 if kind == 0 else 8

        def loop(eng, body):
            body(0, 0)
            body(1, 1)
            with eng.Fori(0, NBLK // 2 - 1) as i:
                for k in range(2):
                    body(i * 2 + (2 + k), k)

        @block.vector
        def _(dve):
            def body(n, k):
                lk = Link(dve, s_link, LINKS, n)
                rows = [src[:, ds(n * TB + c, 1), :].rearrange("p a d -> p (a d)") for c in range(TB)]
                lk(*[dve.bn_stats(stats[:, c, :], rows[c]) for c in range(TB)])
                dve.memset(pad[:], 0.0)
                lk(*[dve.bn_aggr(mv[:, c, :], stats[:, c, :]) for c in range(TB)])
                if kind == 0:
                    lk(dve.tensor_tensor(sq[:], mv[:, :, 0], mv[:, :, 0], ALU.mult))
                    lk(dve.tensor_tensor(sq[:], sq[:], mv[:, :, 1], ALU.add))
                    dve.tensor_scalar(ve[:], sq[:], EPS_RMS, None, ALU.add).then_inc(s_ve, 1)
                else:
                    dve.tensor_scalar(ve[:], mv[:, :, 1], EPS_LN, None, ALU.add).then_inc(s_ve, 1)
                upto(dve, s_rs, 1, n, 1)
                upto(dve, s_turn, 1, n - 2, 1)
                for c in range(TB):
                    out = y[:, k, c, :] if kind == 0 else yall[:, ds(n * TB + c, 1), :].rearrange("p a d -> p (a d)")
                    if kind == 0:
                        last = dve.tensor_scalar(out, rows[c], rs[:, c:c + 1], None, ALU.mult)
                    else:
                        last = dve.tensor_scalar(out, rows[c], mv[:, c, 0:1], rs[:, c:c + 1],
                                                 ALU.subtract, ALU.mult)
                        lastc = dve.tensor_scalar(y[:, k, c, :], rows[c], mv[:, c, 0:1], rs[:, c:c + 1],
                                                  ALU.subtract, ALU.mult)
                        last = lastc
                last.then_inc(s_y, 1)
                upto(dve, s_log, 1, n, 1)
                dve.tensor_copy(logits[:, ds(n * TB, TB), :],
                                log_ps[:, k, 0:TB * NE].rearrange("p (c e) -> p c e", e=NE)).then_inc(s_logits, 1)

            loop(dve, body)

        @block.gpsimd
        def _(pool):
            pool.memset(half[:], -0.5).then_inc(s_half, 1)
            pool.wait_ge(s_half, 1)

            def body(n, k):
                upto(pool, s_ve, 1, n, 1)
                pool.tensor_tensor(rs[:], ve[:], half[:], ALU.pow).then_inc(s_rs, 1)

            loop(pool, body)

        @block.tensor
        def _(pe):
            def body(n, k):
                upto(pe, s_y, 1, n, 1)
                upto(pe, s_yT, 1, n - 2, 1)
                for c in range(TB):
                    last = pe.transpose(turn_ps[:, k, c * P:(c + 1) * P], y[:, k, c, :], ident)
                last.then_inc(s_turn, 1)
                upto(pe, s_yT, 1, n, 1)
                upto(pe, s_logits, 1, n - 2, 1)
                for c in range(TB):
                    last = pe.matmul(log_ps[:, k, c * NE:(c + 1) * NE], yT[:, k, c * P:(c + 1) * P], router[:],
                                     start=True, stop=True)
                last.then_inc(s_log, 1)

            ident = cst[:, C_IDENT:C_IDENT + P]
            loop(pe, body)

        @block.scalar
        def _(act):
            def body(n, k):
                upto(act, s_turn, 1, n, 1)
                if kind == 0:
                    act.activation(hT[:, ds(n * TB * P, TB * P)], turn_ps[:, k, :], ACT.Copy)
                upto(act, s_log, 1, n - 2, 1)
                act.activation(yT[:, k, :], turn_ps[:, k, :], ACT.Copy).then_inc(s_yT, 1)

            loop(act, body)


def route(nc, kind, cst, logits, bias_row, comb, idx, wsel, noop):
    T = NTILE
    with ExitStack() as ctx:
        take = semaphores(nc, ctx)

        def sb(name, shape, dt=F32):
            return ctx.enter_context(nc.sbuf_tensor(f"t{name}{kind}", shape, dt))

        def sem(name):
            return take(f"t{name}{kind}")

        c8 = [P, T, NE]
        pr = sb("pr", c8)
        p2 = sb("p2", c8)
        sc = sb("sc", c8)
        sel = sb("sel", [P, 2, T, NE])
        m = sb("m", [P, 2, T])
        one = sb("one", [P, T])
        two = sb("two", [P, T])
        s_v = sem("s_v")
        s_a = sem("s_a")
        s_p = sem("s_p")
        s_b = sem("s_b")
        if kind == 1:
            bias8 = sb("bias8", [P, NE])
            bias1 = sb("bias1", [1, NE])
            mask = sb("mask", c8)
            ranks = sb("ranks", c8)
            totals = sb("totals", [P, NE, T])
            prefix = sb("prefix", [P, NE, T])
            zeros = sb("zeros", [P, T])
            slot = sb("slot", [P, T])
            ok = sb("ok", [P, T])
            ps = ctx.enter_context(nc.psum_tensor("tps", [P, 3, 512], F32))
        block = ctx.enter_context(nc.Block())
        EXP0, EXP1 = 1, 2

        def wide(ap):
            return ap.unsqueeze(2).to_broadcast(c8)

        def row(at):
            return cst[:, at:at + NE].unsqueeze(1).to_broadcast(c8)

        marks = {}

        @block.vector
        def _(dve):
            lk = Link(dve, s_v, 0, 0)
            lg = logits[:]
            if kind == 1:
                dve.wait_ge(s_p, 1)
                lk(dve.tensor_copy(bias8[:], ps[:, 2, 0:NE]))
                lk(dve.tensor_tensor(lg, lg, bias8[:].unsqueeze(1).to_broadcast(c8), ALU.add))
                lk(dve.memset(zeros[:], 0.0))
            lk(dve.tensor_reduce(one[:], lg, AX.X, ALU.max))
            lk(dve.tensor_tensor(pr[:], lg, wide(one[:]), ALU.subtract))
            marks["pr"] = lk.k
            dve.wait_ge(s_a, EXP0)
            lk(dve.tensor_reduce(one[:], pr[:], AX.X, ALU.add))
            lk(dve.reciprocal(two[:], one[:]))
            lk(dve.tensor_tensor(pr[:], pr[:], wide(two[:]), ALU.mult))
            probs = pr
            for c in range(2):
                lk(dve.tensor_reduce(m[:, c, :], probs[:], AX.X, ALU.max))
                lk(dve.tensor_tensor(sc[:], probs[:], wide(m[:, c, :]), ALU.is_equal))
                lk(dve.tensor_tensor(sc[:], sc[:], row(C_PRI), ALU.mult))
                lk(dve.tensor_reduce(one[:], sc[:], AX.X, ALU.max))
                lk(dve.tensor_tensor(sel[:, c, :, :], sc[:], wide(one[:]), ALU.is_equal))
                if c == 0:
                    lk(dve.scalar_tensor_tensor(p2[:].rearrange("p t e -> p (t e)"),
                                                sel[:, 0, :, :].rearrange("p t e -> p (t e)"), -2.0,
                                                pr[:].rearrange("p t e -> p (t e)"), ALU.mult, ALU.add))
                    probs = p2
            if kind == 0:
                lk(dve.tensor_tensor(one[:], m[:, 1, :], m[:, 0, :], ALU.subtract))
                marks["d"] = lk.k
                dve.wait_ge(s_a, EXP1)
                lk(dve.tensor_scalar(two[:], one[:], 1.0, None, ALU.add))
                lk(dve.reciprocal(m[:, 0, :], two[:]))
                lk(dve.tensor_tensor(m[:, 1, :], one[:], m[:, 0, :], ALU.mult))
                lk(dve.tensor_tensor(sc[:], sel[:, 0, :, :], wide(m[:, 0, :]), ALU.mult))
                lk(dve.tensor_tensor(p2[:], sel[:, 1, :, :], wide(m[:, 1, :]), ALU.mult))
                lk(dve.tensor_tensor(comb[:], sc[:], p2[:], ALU.add))
                return
            for c in range(2):
                lk(dve.tensor_scalar(one[:], m[:, c, :], 0.0, None, ALU.is_gt))
                lk(dve.tensor_tensor(sel[:, c, :, :], sel[:, c, :, :], wide(one[:]), ALU.mult))
            lk(dve.tensor_tensor(mask[:], sel[:, 0, :, :], sel[:, 1, :, :], ALU.add))
            marks["mask"] = lk.k
            dve.wait_ge(s_p, 3)
            lk(dve.tensor_copy(totals[:], ps[:, 1, 0:T * NE].rearrange("p (t e) -> p e t", e=NE)))
            for e in range(NE):
                lk(dve.tensor_tensor_scan(prefix[:, e, :], totals[:, e, :], zeros[:], 0.0, ALU.add, ALU.add))
            lk(dve.tensor_tensor(prefix[:], prefix[:], totals[:], ALU.subtract))
            lk(dve.tensor_tensor(ranks[:], ps[:, 0, 0:T * NE].rearrange("p (t e) -> p t e", e=NE),
                                 prefix[:].rearrange("p e t -> p t e"), ALU.add))
            for c in range(2):
                lk(dve.tensor_tensor(sc[:], sel[:, c, :, :], ranks[:], ALU.mult))
                lk(dve.tensor_reduce(one[:], sc[:], AX.X, ALU.add))
                lk(dve.tensor_tensor(sc[:], sel[:, c, :, :], row(C_BASE), ALU.mult))
                lk(dve.tensor_reduce(two[:], sc[:], AX.X, ALU.add))
                lk(dve.scalar_tensor_tensor(slot[:], one[:], -1.0, two[:], ALU.add, ALU.add))
                lk(dve.tensor_scalar(ok[:], one[:], float(CAP), None, ALU.is_le))
                lk(dve.scalar_tensor_tensor(ok[:], one[:], 1.0, ok[:], ALU.is_ge, ALU.mult))
                lk(dve.scalar_tensor_tensor(ok[:], two[:], float(CAP * (NE - 1)), ok[:], ALU.is_lt, ALU.mult))
                lk(dve.tensor_tensor(wsel[:, c, :], ok[:], m[:, c, :], ALU.mult))
                lk(dve.tensor_scalar(ok[:], ok[:], -float(BEYOND), float(BEYOND), ALU.mult, ALU.add))
                lk(dve.scalar_tensor_tensor(slot[:], slot[:], 0.0, ok[:], ALU.max, ALU.add))
                lk(dve.tensor_copy(idx[:, c, :], slot[:]))
            lk(dve.tensor_tensor(one[:], sel[:, 0, :, NE - 1], m[:, 0, :], ALU.mult))
            lk(dve.tensor_tensor(two[:], sel[:, 1, :, NE - 1], m[:, 1, :], ALU.mult))
            lk(dve.tensor_tensor(noop[:], one[:], two[:], ALU.add))

        @block.scalar
        def _(act):
            act.wait_ge(s_v, marks["pr"])
            act.activation(pr[:], pr[:], ACT.Exp).then_inc(s_a, 1)
            if kind == 0:
                act.wait_ge(s_v, marks["d"])
                act.activation(one[:], one[:], ACT.Exp).then_inc(s_a, 1)

        if kind == 1:
            @block.sync
            def _(sp):
                sp.dma_start(bias1[:], bias_row).then_inc(s_b, 16)

            @block.tensor
            def _(pe):
                pe.wait_ge(s_b, 16)
                pe.matmul(ps[:, 2, 0:NE], cst[0:1, C_TRI + P:C_TRI + 2 * P], bias1[:], start=True, stop=True)\
                  .then_inc(s_p, 1)
                pe.wait_ge(s_v, marks["mask"])
                flat = mask[:].rearrange("p t e -> p (t e)")
                pe.matmul(ps[:, 0, 0:T * NE], cst[:, C_TRI:C_TRI + P], flat, start=True, stop=True).then_inc(s_p, 1)
                pe.matmul(ps[:, 1, 0:T * NE], cst[:, C_TRI + P:C_TRI + 2 * P], flat, start=True, stop=True)\
                  .then_inc(s_p, 1)


CAP = NT // NE
BEYOND = 1 << 20


def gated_mixture(nc, hT, comb, XB, X, cst, dram):
    NBLK, TB, EX, FC = 8, 4, NE + 1, F0 // P
    NQ = EX * FC
    with ExitStack() as ctx:
        take = semaphores(nc, ctx)

        def sb(name, shape, dt=F32):
            return ctx.enter_context(nc.sbuf_tensor(f"g{name}", shape, dt))

        def sem(name):
            return take(f"g{name}")

        wg = sb("wg", [P, EX, F0])
        wu = sb("wu", [P, EX, F0])
        wd = sb("wd", [P, EX, FC, D])
        norm = sb("norm", [P, 1])
        sg = sb("sg", [P, 2, 512])
        hid = sb("hid", [P, 2, FC, 512])
        acc = sb("acc", [P, 2, TB, D])
        pad = sb("pad", [1, 1])
        stats = sb("stats", [P, TB, 6])
        mv = sb("mv", [P, TB, 2])
        ve = sb("ve", [P, TB])
        rs = sb("rs", [P, TB])
        half = sb("half", [P, TB])
        tmp = sb("tmp", [P, TB, D])
        gate_ps = ctx.enter_context(nc.psum_tensor("gate_ps", [P, 2, 512], F32))
        up_ps = ctx.enter_context(nc.psum_tensor("up_ps", [P, 2, 512], F32))
        down_ps = ctx.enter_context(nc.psum_tensor("down_ps", [P, 2, 512], F32))
        s_w = sem("s_w")
        s_half = sem("s_half")
        s_scaled = sem("s_scaled")
        s_gu = sem("s_gu")
        s_sg = sem("s_sg")
        s_hid = sem("s_hid")
        s_down = sem("s_down")
        s_acc = sem("s_acc")
        s_l = sem("s_l")
        s_ve = sem("s_ve")
        s_rs = sem("s_rs")
        s_res = sem("s_res")
        block = ctx.enter_context(nc.Block())

        def blocks(eng, body):
            body(0)
            with eng.Fori(1, NBLK) as i:
                body(i)

        @block.sync
        def _(sp):
            sp.dma_start(wg[:, 0:NE, :], dram["L0_ffn_e_gate"].rearrange("e d f -> d e f")).then_inc(s_w, 16)
            sp.dma_start(wg[:, NE, :], dram["L0_ffn_sh_gate"]).then_inc(s_w, 16)
            sp.dma_start(wu[:, 0:NE, :], dram["L0_ffn_e_up"].rearrange("e d f -> d e f")).then_inc(s_w, 16)
            sp.dma_start(wu[:, NE, :], dram["L0_ffn_sh_up"]).then_inc(s_w, 16)
            for e in range(NE):
                sp.dma_start(wd[:, e, :, :], dram["L0_ffn_e_down"][e].rearrange("(c f) d -> f c d", f=P))\
                    .then_inc(s_w, 16)
            sp.dma_start(wd[:, NE, :, :], dram["L0_ffn_sh_down"].rearrange("(c f) d -> f c d", f=P)).then_inc(s_w, 16)
            sp.dma_start(norm[:], dram["L0_ffn_norm2_w"].rearrange("(d a) -> d a", a=1)).then_inc(s_w, 16)

        @block.gpsimd
        def _(pool):
            pool.memset(half[:], -0.5).then_inc(s_half, 1)
            pool.wait_ge(s_half, 1)

            def body(i):
                upto(pool, s_ve, 1, i, 1)
                pool.tensor_tensor(rs[:], ve[:], half[:], ALU.pow).then_inc(s_rs, 1)

            blocks(pool, body)

        @block.tensor
        def _(pe):
            pe.wait_ge(s_scaled, 2)

            def hidden(i, q):
                e, c = q // FC, q % FC
                upto(pe, s_hid, NQ, i, q - 1 if q >= 2 else 0)
                rhs = hT[:, ds(i * 512, 512)]
                pe.matmul(gate_ps[:, q % 2, :], wg[:, e, c * P:(c + 1) * P], rhs, start=True, stop=True)
                pe.matmul(up_ps[:, q % 2, :], wu[:, e, c * P:(c + 1) * P], rhs, start=True, stop=True)\
                  .then_inc(s_gu, 1)

            def down(i, e):
                upto(pe, s_hid, NQ, i, FC * (e + 1))
                if e >= 2:
                    upto(pe, s_acc, EX * TB, i, TB * (e - 1))
                else:
                    upto(pe, s_acc, EX * TB, i, 0)
                for t in range(TB):
                    for c in range(FC):
                        last = pe.matmul(down_ps[:, e % 2, t * D:(t + 1) * D], hid[:, e % 2, c, t * P:(t + 1) * P],
                                         wd[:, e, c, :], start=(c == 0), stop=(c == FC - 1))
                last.then_inc(s_down, 1)

            def body(i):
                for q in range(FC):
                    hidden(i, q)
                for e in range(EX):
                    for c in range(FC if e + 1 < EX else 0):
                        hidden(i, FC * (e + 1) + c)
                    down(i, e)

            blocks(pe, body)

        @block.scalar
        def _(act):
            def body(i):
                for q in range(NQ):
                    upto(act, s_gu, NQ, i, q + 1)
                    if q >= 2:
                        upto(act, s_hid, NQ, i, q - 1)
                    else:
                        upto(act, s_hid, NQ, i, 0)
                    act.activation(sg[:, q % 2, :], gate_ps[:, q % 2, :], ACT.Silu).then_inc(s_sg, 1)

            blocks(act, body)

        @block.vector
        def _(dve):
            dve.wait_ge(s_w, 14 * 16)
            for wt in (wg, wu):
                flat = wt[:].rearrange("p e f -> p (e f)")
                dve.tensor_scalar(flat, flat, norm[:, 0:1], None, ALU.mult).then_inc(s_scaled, 1)

            def body(i):
                def product(q):
                    e, c = q // FC, q % FC
                    upto(dve, s_sg, NQ, i, q + 1)
                    if e >= 2:
                        upto(dve, s_down, EX, i, e - 1)
                    else:
                        upto(dve, s_down, EX, i, 0)
                    dve.tensor_tensor(hid[:, e % 2, c, :], sg[:, q % 2, :], up_ps[:, q % 2, :], ALU.mult)\
                       .then_inc(s_hid, 1)

                def add(e):
                    upto(dve, s_down, EX, i, e + 1)
                    if e == 0:
                        upto(dve, s_res, 1, i, 0)
                    else:
                        dve.wait_ge(s_acc, i * (EX * TB) + TB * e)
                    for t in range(TB):
                        d = down_ps[:, e % 2, t * D:(t + 1) * D]
                        into = acc[:, e % 2, t, :]
                        xt = XB[:, ds(i * TB + t, 1), :].rearrange("p a d -> p (a d)")
                        if e == 0:
                            ins = dve.scalar_tensor_tensor(into, d, comb[:, ds(i * TB + t, 1), e], xt,
                                                           ALU.mult, ALU.add)
                        elif e < NE:
                            ins = dve.scalar_tensor_tensor(into, d, comb[:, ds(i * TB + t, 1), e],
                                                           acc[:, (e - 1) % 2, t, :], ALU.mult, ALU.add)
                        else:
                            ins = dve.tensor_tensor(into, d, acc[:, (e - 1) % 2, t, :], ALU.add)
                        ins.then_inc(s_acc, 1)

                for c in range(FC):
                    product(c)
                for e in range(EX):
                    if e + 1 < EX:
                        for c in range(FC):
                            product(FC * (e + 1) + c)
                    add(e)
                dve.wait_ge(s_acc, i * (EX * TB) + EX * TB)
                a = acc[:, (EX - 1) % 2, :, :]
                lk = Link(dve, s_l, 3 * TB, i)
                lk(*[dve.bn_stats(stats[:, t, :], a[:, t, :]) for t in range(TB)])
                dve.memset(pad[:], 0.0)
                lk(*[dve.bn_aggr(mv[:, t, :], stats[:, t, :]) for t in range(TB)])
                dve.tensor_scalar(ve[:], mv[:, :, 1], EPS_LN, None, ALU.add).then_inc(s_ve, 1)
                upto(dve, s_rs, 1, i, 1)
                lk(*[dve.tensor_scalar(tmp[:, t, :], a[:, t, :], mv[:, t, 0:1], rs[:, t:t + 1],
                                       ALU.subtract, ALU.mult) for t in range(TB)])
                xt = X[:, ds(i * TB, TB), :]
                dve.tensor_tensor(xt, xt, tmp[:], ALU.add).then_inc(s_res, 1)

            blocks(dve, body)
            dve.wait_ge(s_res, NBLK)


def capped_mixture(nc, idx, wsel, noop, Y, X, cst, dram, out, xd, od):
    NX, TB, FC = NE - 1, CAP // P, F1 // P
    with ExitStack() as ctx:
        take = semaphores(nc, ctx)

        def sb(name, shape, dt=F32):
            return ctx.enter_context(nc.sbuf_tensor(f"c{name}", shape, dt))

        def sem(name):
            return take(f"c{name}")

        wi = sb("wi", [P, NX, F1])
        wo = sb("wo", [P, NX, FC, D])
        zero = sb("zero", [P, TB, D])
        xe = sb("xe", [P, 2, TB, D])
        xT = sb("xT", [P, 2, CAP])
        hid = sb("hid", [P, 2, FC, CAP])
        res = sb("res", [P, 2, TB, D])
        NR = 8
        got = sb("got", [P, NR, 2, D])
        mix = sb("mix", [P, 2, 3, D])
        stats = sb("stats", [P, NTILE, 6])
        mv = sb("mv", [P, NTILE, 2])
        ve = sb("ve", [P, NTILE])
        rs = sb("rs", [P, NTILE])
        half = sb("half", [P, 1])
        turn_ps = ctx.enter_context(nc.psum_tensor("cturn_ps", [P, 2, 512], F32))
        hid_ps = ctx.enter_context(nc.psum_tensor("chid_ps", [P, 4, 512], F32))
        out_ps = ctx.enter_context(nc.psum_tensor("cout_ps", [P, 2, 512], F32))
        s_w = sem("s_w")
        s_zero = sem("s_zero")
        s_clear = sem("s_clear")
        s_sent = sem("s_sent")
        s_xe = [sem("s_xe0"), sem("s_xe1")]
        s_turn = sem("s_turn")
        s_xT = sem("s_xT")
        s_hp = sem("s_hp")
        s_hid = sem("s_hid")
        s_op = sem("s_op")
        s_res = sem("s_res")
        s_od = [sem("s_od0"), sem("s_od1")]
        s_got = [sem(f"s_got{k}") for k in range(NR)]
        s_m = sem("s_m")
        s_ve = sem("s_ve")
        s_rs = sem("s_rs")
        s_x = sem("s_x")
        s_f = sem("s_f")
        s_n = sem("s_n")
        s_out = sem("s_out")
        block = ctx.enter_context(nc.Block())

        @block.sync
        def _(sp):
            def store(e):
                sp.wait_ge(s_res, e + 1)
                sp.dma_start(od[e * CAP:(e + 1) * CAP, :].rearrange("(c p) d -> p c d", p=P),
                             res[:, e % 2, :, :]).then_inc(s_od[e % 2], 16)

            sp.wait_ge(s_zero, 2)
            for e in range(NX):
                sp.dma_start(xd[e * CAP:(e + 1) * CAP, :].rearrange("(c p) d -> p c d", p=P), zero[:])\
                    .then_inc(s_clear, 16)
            for e in range(NX):
                sp.dma_start(wi[:, e, :], dram["L1_ffn_experts_inter"][e]).then_inc(s_w, 16)
                sp.dma_start(wo[:, e, :, :], dram["L1_ffn_experts_out"][e].rearrange("(c f) d -> f c d", f=P))\
                    .then_inc(s_w, 16)
            sp.wait_ge(s_sent, 16 * 2 * NTILE)
            for e in range(NX):
                if e >= 2:
                    sp.wait_ge(s_turn, e - 1)
                sp.dma_start(xe[:, e % 2, :, :], xd[e * CAP:(e + 1) * CAP, :].rearrange("(c p) d -> p c d", p=P))\
                    .then_inc(s_xe[e % 2], 16)
                if e >= 2:
                    store(e - 2)
            store(NX - 2)
            store(NX - 1)
            ot = out.rearrange("b (c p) d -> p (b c) d", p=P)
            for k in range(4):
                sp.wait_ge(s_x, 8 * (k + 1))
                sp.dma_start(ot[:, 8 * k:8 * k + 8, :], X[:, 8 * k:8 * k + 8, :]).then_inc(s_out, 16)
            sp.wait_ge(s_out, 64)

        @block.gpsimd
        def _(pool):
            pool.memset(zero[:], 0.0).then_inc(s_zero, 1)
            pool.memset(half[:], -0.5).then_inc(s_zero, 1)
            pool.memset(got[:], 0.0).then_inc(s_zero, 1)

            def group(k):
                pool.wait_ge(s_ve, k + 1)
                pool.tensor_tensor(rs[:, 8 * k:8 * k + 8], ve[:, 8 * k:8 * k + 8],
                                   half[:].to_broadcast([P, 8]), ALU.pow).then_inc(s_rs, 1)

            pool.wait_ge(s_zero, 3)
            pool.wait_ge(s_clear, 16 * NX)
            for t in range(NTILE):
                for c in range(2):
                    pool.indirect_dma_start(xd, bass.IndirectOffsetOnAxis(ap=idx[:, c, t:t + 1], axis=0),
                                            Y[:, t, :], None, bounds_check=NX * CAP - 1, oob_is_err=False)\
                        .then_inc(s_sent, 16)
            pool.wait_ge(s_od[0], 16 * 4)
            pool.wait_ge(s_od[1], 16 * 3)
            for t in range(NTILE):
                if t >= NR:
                    pool.wait_ge(s_m, 3 * (t - NR + 1))
                for c in range(2):
                    pool.indirect_dma_start(got[:, t % NR, c, :], None, od,
                                            bass.IndirectOffsetOnAxis(ap=idx[:, c, t:t + 1], axis=0),
                                            bounds_check=NX * CAP - 1, oob_is_err=False)\
                        .then_inc(s_got[t % NR], 16)
                if t % 8 == 7 and t > 8:
                    group(t // 8 - 1)
            group(3)

        @block.tensor
        def _(pe):
            ident = cst[:, C_IDENT:C_IDENT + P]
            pe.wait_ge(s_w, 16 * 2 * NX)

            def turn(e):
                pe.wait_ge(s_xe[e % 2], 16 * (e // 2 + 1))
                if e >= 2:
                    pe.wait_ge(s_xT, e - 1)
                for c in range(TB):
                    last = pe.transpose(turn_ps[:, e % 2, c * P:(c + 1) * P], xe[:, e % 2, c, :], ident)
                last.then_inc(s_turn, 1)

            def up(e):
                pe.wait_ge(s_xT, e + 1)
                for c in range(FC):
                    if e >= 1:
                        pe.wait_ge(s_hid, FC * (e - 1) + c + 1)
                    pe.matmul(hid_ps[:, c, :], wi[:, e, c * P:(c + 1) * P], xT[:, e % 2, :], start=True, stop=True)\
                      .then_inc(s_hp, 1)

            def down(e):
                pe.wait_ge(s_hid, FC * (e + 1))
                if e >= 2:
                    pe.wait_ge(s_res, e - 1)
                for t in range(TB):
                    for c in range(FC):
                        last = pe.matmul(out_ps[:, e % 2, t * D:(t + 1) * D], hid[:, e % 2, c, t * P:(t + 1) * P],
                                         wo[:, e, c, :], start=(c == 0), stop=(c == FC - 1))
                last.then_inc(s_op, 1)

            turn(0)
            for e in range(NX):
                up(e)
                if e + 1 < NX:
                    turn(e + 1)
                if e >= 1:
                    down(e - 1)
            down(NX - 1)

        @block.scalar
        def _(act):
            for e in range(NX):
                act.wait_ge(s_turn, e + 1)
                if e >= 2:
                    act.wait_ge(s_hp, FC * (e - 1))
                act.activation(xT[:, e % 2, :], turn_ps[:, e % 2, :], ACT.Copy).then_inc(s_xT, 1)
                for c in range(FC):
                    act.wait_ge(s_hp, FC * e + c + 1)
                    if e >= 2:
                        act.wait_ge(s_op, e - 1)
                    act.activation(hid[:, e % 2, c, :], hid_ps[:, c, :], ACT.Relu).then_inc(s_hid, 1)

        @block.vector
        def _(dve):
            for e in range(NX):
                dve.wait_ge(s_op, e + 1)
                if e >= 2:
                    dve.wait_ge(s_od[e % 2], 16 * (e // 2))
                dve.tensor_copy(res[:, e % 2, :, :].rearrange("p c d -> p (c d)"), out_ps[:, e % 2, :])\
                   .then_inc(s_res, 1)

            def finish(k):
                dve.wait_ge(s_rs, k + 1)
                for t in range(8 * k, 8 * k + 8):
                    dve.tensor_scalar(Y[:, t, :], Y[:, t, :], mv[:, t, 0:1], rs[:, t:t + 1],
                                      ALU.subtract, ALU.mult).then_inc(s_f, 1)
                    dve.wait_ge(s_f, t + 1)
                    dve.tensor_tensor(X[:, t, :], X[:, t, :], Y[:, t, :], ALU.add).then_inc(s_x, 1)

            for t in range(NTILE):
                dve.wait_ge(s_got[t % NR], 32 * (t // NR + 1))
                g = got[:, t % NR, :, :]
                dve.tensor_scalar(mix[:, t % 2, 0, :], Y[:, t, :], noop[:, t:t + 1], None, ALU.mult)\
                   .then_inc(s_m, 1)
                dve.wait_ge(s_m, 3 * t + 1)
                dve.scalar_tensor_tensor(mix[:, t % 2, 1, :], g[:, 0, :], wsel[:, 0, t:t + 1], mix[:, t % 2, 0, :],
                                         ALU.mult, ALU.add).then_inc(s_m, 1)
                dve.wait_ge(s_m, 3 * t + 2)
                dve.scalar_tensor_tensor(Y[:, t, :], g[:, 1, :], wsel[:, 1, t:t + 1], mix[:, t % 2, 1, :],
                                         ALU.mult, ALU.add).then_inc(s_m, 1)
                dve.wait_ge(s_m, 3 * t + 3)
                dve.bn_stats(stats[:, t, :], Y[:, t, :]).then_inc(s_n, 1)
                dve.wait_ge(s_n, 2 * t + 1)
                dve.bn_aggr(mv[:, t, :], stats[:, t, :]).then_inc(s_n, 1)
                if t % 8 == 7:
                    dve.wait_ge(s_n, 2 * t + 2)
                    k = t // 8
                    dve.tensor_scalar(ve[:, 8 * k:8 * k + 8], mv[:, 8 * k:8 * k + 8, 1], EPS_LN, None, ALU.add)\
                       .then_inc(s_ve, 1)
                    if k >= 1:
                        finish(k - 1)
            finish(3)


def build(nc, dram, out):
    with ExitStack() as ctx:
        def sb(name, shape, dt):
            return ctx.enter_context(nc.sbuf_tensor(name, shape, dt))

        X = sb("X", [P, NTILE, D], F32)
        XB = sb("XB", [P, NTILE, D], F32)
        cst = sb("cst", [P, C_ALL], F32)
        cstb = sb("cstb", [P, 2 * P], BF16)
        w = {"router0": sb("router0", [P, NE], F32), "router1": sb("router1", [P, NE], F32)}
        weights = []
        for n in range(3):
            a = {"wq": sb(f"wq_{n}", [P, NG, P], F32), "wk": sb(f"wk_{n}", [P, NG, P], F32),
                 "wv": sb(f"wv_{n}", [P, D + (H if n == 2 else 0)], F32)}
            if n < 2:
                a["wo"] = sb(f"wo_{n}", [P, D], F32)
            weights.append(a)
        weights[0]["bq"] = sb("bq", [P, NG], F32)
        weights[0]["bk"] = sb("bk", [P, NG], F32)
        weights[0]["bv"] = sb("bv", [1, D], F32)
        weights[0]["bo"] = sb("bo", [1, D], F32)
        load_weights(nc, cst, cstb, X, w, weights, dram)
        attention_layer(nc, 0, X, XB, cst, cstb, weights[0])
        attention_layer(nc, 1, X, XB, cst, cstb, weights[1])
        logits = sb("logits", [P, NTILE, NE], F32)
        with ExitStack() as c1:
            hT = c1.enter_context(nc.sbuf_tensor("hT", [P, NT], F32))
            comb = c1.enter_context(nc.sbuf_tensor("comb", [P, NTILE, NE], F32))
            router_layer(nc, 0, cst, XB, None, hT, logits, w["router0"])
            route(nc, 0, cst, logits, None, comb, None, None, None)
            gated_mixture(nc, hT, comb, XB, X, cst, dram)
        attention_layer(nc, 2, X, XB, cst, cstb, weights[2])
        idx = sb("idx", [P, 2, NTILE], U32)
        wsel = sb("wsel", [P, 2, NTILE], F32)
        noop = sb("noop", [P, NTILE], F32)
        xd = nc.dram_tensor("slots_in", [(NE - 1) * CAP, D], F32).ap()
        od = nc.dram_tensor("slots_out", [(NE - 1) * CAP, D], F32).ap()
        router_layer(nc, 1, cst, X, XB, None, logits, w["router1"])
        route(nc, 1, cst, logits, dram["L1_ffn_router_b"].rearrange("(a e) -> a e", a=1), None, idx, wsel, noop)
        capped_mixture(nc, idx, wsel, noop, XB, X, cst, dram, out, xd, od)


def kernel(**inputs):
    import numpy as _np
    import concourse.bacc as _bacc
    from concourse import mybir as _mybir
    from concourse.bass_utils import run_bass_kernel_spmd as _run

    nc = _bacc.Bacc("TRN2", target_bir_lowering=False, num_devices=1)
    arrays, dram = {}, {}
    for name, a in list(inputs.items()) + [("constants", constant_table())]:
        a = _np.ascontiguousarray(a)
        arrays[f"in_{name}_dram"] = a
        dram[name] = nc.dram_tensor(f"in_{name}_dram", a.shape, _mybir.dt.from_np(a.dtype), kind="ExternalInput").ap()
    out = nc.dram_tensor("out_0_dram", (NB, S, D), _mybir.dt.float32, kind="ExternalOutput").ap()
    build(nc, dram, out)
    r = _run(nc, [arrays], core_ids=[0])
    return r.results[0]["out_0_dram"]
```

```python
from contextlib import ExitStack

import concourse.bass as bass
from concourse import mybir
import numpy as np

F32 = mybir.dt.float32
F16 = mybir.dt.float16
BF16 = mybir.dt.bfloat16
I32 = mybir.dt.int32
U32 = mybir.dt.uint32
ALU = mybir.AluOpType
ACT = mybir.ActivationFunctionType
AX = mybir.AxisListType
ds = bass.ds

P = 128
NB, S, D = 16, 256, 128
NT = NB * S
NTILE = NT // P
TC = S // P
H, DH = 16, 8
NG, NJ = 4, 4
NE = 8
F0 = 256
F1 = 512
EPS_LN = 1e-5
EPS_RMS = 1e-6
EPS_POW = 1e-7
SCALE = float(DH) ** -0.5
SHIFT_ROW = 24
MASKED = -1e30
BIAS_RMS, BIAS_PLAIN = 0, 1

C_IDENT = 0
C_TRI = 128
C_LATE = 384
C_COL = 512
(K_LOW_Q, K_LOW_K, K_SHIFT, K_M0, K_M1, K_M2, K_M345, K_N3, K_N4, K_N5, K_M012) = range(11)
C_PRI = C_COL + 16
C_BASE = C_PRI + 8
C_ALL = C_BASE + 8


def constant_table():
    c = np.zeros((P, C_ALL), np.float32)
    p = np.arange(P)
    c[:, C_IDENT:C_IDENT + P] = np.eye(P)
    c[:, C_TRI:C_TRI + P] = p[:, None] <= p[None, :]
    c[:, C_TRI + P:C_TRI + 2 * P] = 1.0
    c[:, C_LATE:C_LATE + P] = np.where(p[:, None] > p[None, :], MASKED, 0.0)
    r = p % 32
    c[:, C_COL + K_LOW_Q] = -1.0 * ((r >= 16) & (r < 24))
    c[:, C_COL + K_LOW_K] = -1.0 * ((r >= 8) & (r < 16))
    c[:, C_COL + K_SHIFT] = r == SHIFT_ROW
    r = p % 8
    for k in range(3):
        c[:, C_COL + K_M0 + k] = r == k
        c[:, C_COL + K_N3 + k] = -1.0 * (r == 3 + k)
    c[:, C_COL + K_M345] = (r >= 3) & (r < 6)
    c[:, C_COL + K_M012] = r < 3
    c[:, C_PRI:C_PRI + 8] = 8 - np.arange(8)
    c[:, C_BASE:C_BASE + 8] = np.arange(8) * 512
    return c


def has(b):
    return not isinstance(b, int) or 0 <= b < NB


def upto(eng, sem, per, b, k):
    if isinstance(b, int) and per * b + k <= 0:
        return
    eng.wait_ge(sem, b * per + k)


def drive(eng, body):
    for b in (-2, -1, 0, 1):
        body(b, b % 3)
    with eng.Fori(0, 4) as i:
        for k in range(3):
            body(i * 3 + (2 + k), (2 + k) % 3)
    for b in range(14, NB + 1):
        body(b, b % 3)


class Link:

    def __init__(self, eng, sem, per, b):
        self.eng, self.sem, self.per, self.b, self.k = eng, sem, per, b, 0

    def __call__(self, *instructions):
        for ins in instructions:
            self.k += 1
            ins.then_inc(self.sem, 1)
        self.eng.wait_ge(self.sem, self.b * self.per + self.k)

    def skip_to(self, k):
        self.k = k
        return self


def semaphores(nc, ctx):
    taken = []

    def clear():
        nc.clear_and_free_semaphores(taken)
        nc.all_engine_barrier()

    def take(name):
        taken.append(nc.alloc_semaphore(name))
        return taken[-1]

    ctx.callback(clear)
    return take


def attention_layer(nc, kind, X, XB, cst, cstb, w):
    soft = kind < 2
    lag = 1 if soft else 3
    NU = H // 2
    NS = 2 * NU if soft else NU
    NPT = 6
    WU = 2 * S * 2 if soft else 2 * S + 2 * P
    LINKS_LN = 10 if kind == 1 else 5
    with ExitStack() as ctx:
        take = semaphores(nc, ctx)

        def sb(name, shape, dt):
            return ctx.enter_context(nc.sbuf_tensor(f"{name}{kind}", shape, dt))

        def pb(name, shape, dt):
            return ctx.enter_context(nc.psum_tensor(f"{name}{kind}", shape, dt))

        def sem(name):
            return take(f"{name}{kind}")

        if soft:
            score_ps = pb("score", [P, 2, 512], F32)
            st_ps = pb("st", [P, 3, 512], F32)
        else:
            turn_ps = pb("turn", [P, 3, 1024], F32)
        pv_ps = pb("pv", [P, 512], F32)
        misc = pb("misc", [P, 2 if soft else 1, 512], F32)

        pad = sb("pad", [1, 1], F32)
        stats = sb("stats", [P, TC, 6], F32)
        mv = sb("mv", [P, TC, 2], F32)
        ve = sb("ve", [P, 2, TC], F32)
        rs = sb("rs", [P, 2, TC], F32)
        half = sb("half", [P, TC], F32)
        pstats = sb("pstats", [P, TC, 6], F32)
        pmv = sb("pmv", [P, TC, 2], F32)
        pve = sb("pve", [P, TC], F32)
        prs = sb("prs", [P, TC], F32)
        y = sb("y", [P, TC, D], F32)
        yT = sb("yT", [P, S], F32)
        xq = sb("xq", [P, 2, 2, S], F32)
        hi = sb("hi", [P, 2, 2, S], F16)
        Kp = sb("Kp", [P, NG, S], F16)
        Qp = sb("Qp", [P, 3, NG, S], F16)
        Kz = sb("Kz", [P, 3, NG, NJ, S], F16)
        Vx = sb("Vx", [P, 3, TC, H, 32], F32)
        PT = sb("PT", [P, NPT, 2 * S] if soft else [P, 3, WU], F32)
        OS = sb("OS", [P, 2, 2, S], F32)
        rc = sb("rc", [P, TC, 8], F32)
        yn = sb("yn", [P, TC, D], F32)
        ynT = sb("ynT", [P, S], F32)
        ob = sb("ob", [P, TC, D], F32)
        tmp = sb("tmp", [P, TC, D], F32)
        if kind == 1:
            tmp2 = sb("tmp2", [P, 2, TC], F32)
            rs2 = sb("rs2", [P, TC], F32)
        if soft:
            mxs = sb("mxs", [P, 2, TC, 8], F32)
            nm = sb("nm", [8, 2, S], F16)
        else:
            rr = sb("rr", [P, 3, WU], F32)
            tt = sb("tt", [P, 3, WU], F32)
            uu = sb("uu", [P, 3, WU], F32)
            gl = sb("gl", [P, TC, H], F32)
            ga = sb("ga", [P, TC, H], F32)
            gm = sb("gm", [P, TC, H], F32)
            ge = sb("ge", [P, TC, H], F32)
            lgr = sb("lgr", [P, TC, H, 8], F32)
            LG = sb("LG", [P, S], F32)
            l1 = sb("l1", [P, S], BF16)
            l2 = sb("l2", [P, S], BF16)
            l3 = sb("l3", [P, S], BF16)
            lrem = sb("lrem", [P, 2, S], F32)
            Mt = sb("Mt", [P, 2, S], BF16)
            Ms = sb("Ms", [P, 3, 2, S], BF16)
            Mz = sb("Mz", [P, 3, H, S], BF16)

        schedule = ([("OTa", 0, 1), ("MXb", 1, 0), ("T", 1, 1), ("OTb", 2, 0), ("Qa", 3, 0), ("YT", 3, 1),
                     ("Ka", 4, 0), ("PR", 4, 1), ("Qb", 5, 0), ("MXa", 5, 1), ("Kb", 6, 0), ("V", 7, 0)] if soft
                    else [("OTa", 0, 1), ("T", 1, 1), ("V", 2, 1), ("Qa", 3, 0), ("Ka", 4, 0), ("OTb", 4, 1),
                          ("Qb", 5, 1), ("CS", 6, 1), ("Kb", 7, 1)])
        steps = [n for n, _, _ in schedule]
        MB = 2 if soft else 1
        offset = dict(MXb=0, OTa=-1, T=2, OTb=-1, Qa=2, YT=-1, Ka=2, PR=-1, Qb=2, Kb=2, MXa=1, V=2, CS=2)
        PACKED = (4, 5, 6, 7) if soft else (3, 4, 6, 9)
        full = {n: sem(f"full_{n}") for n in steps}
        free = {n: sem(f"free_{n}") for n in steps}
        s_init = sem("s_init")
        s_ve = sem("s_ve")
        s_rs = sem("s_rs")
        s_y = sem("s_y")
        s_pack = sem("s_pack")
        s_kz = [sem(f"s_kz{a}") for a in range(2)]
        s_S = sem("s_S")
        s_max = sem("s_max")
        s_sh = [sem(f"s_sh{a}") for a in range(2)]
        s_st = sem("s_st")
        s_exp = sem("s_exp")
        s_pv = sem("s_pv")
        s_os = sem("s_os")
        s_ln = sem("s_ln")
        s_lp = sem("s_lp")
        s_lo = sem("s_lo")
        s_pve = sem("s_pve")
        s_prs = sem("s_prs")
        s_post = sem("s_post")
        if not soft:
            s_dexp = sem("s_dexp")
            s_t = sem("s_t")
            s_u = sem("s_u")
            s_sqd = sem("s_sqd")
            s_sqp = sem("s_sqp")
            s_gl = sem("s_gl")
            s_ga = sem("s_ga")
            s_ge = sem("s_ge")
            s_gd = sem("s_gd")
            s_lgr = sem("s_lgr")
            s_lm = sem("s_lm")
            s_mz = sem("s_mz")

        def before(name, b):
            at, body = steps.index(name), b
            while True:
                at -= MB
                if at < 0:
                    at, body = at + len(steps), body - 1
                if isinstance(body, int) and body < -2:
                    return None
                if has(body + offset[steps[at]]):
                    return steps[at], body + offset[steps[at]]

        def bank(name):
            return misc[:, steps.index(name) % MB, :]

        def turn(slot, u, k):
            return turn_ps[:, (2 * NU * slot + 2 * u + k) % 3, 0:WU]

        def due(u, place, b):
            return [(n, b + offset[n]) for n, v, p in schedule if (v, p) == (u, place) and has(b + offset[n])]

        BY_DVE = (1, 4, 6)

        def squared(eng, b, u):
            if soft:
                upto(eng, s_exp, NS, b, 2 * u + 2)
            elif u in BY_DVE:
                upto(eng, s_sqd, len(BY_DVE), b, sum(v <= u for v in BY_DVE))
            else:
                upto(eng, s_sqp, NU - len(BY_DVE), b, sum(v not in BY_DVE for v in range(u + 1)))

        def third(slot, u):
            return (NU * slot + u) % 3

        def squares(eng, b, slot, u):
            u, b, slot = (u - 1, b, slot) if u >= 1 else (NU - 1, b - 1, slot + 2)
            at = third(slot, u)
            by_dve = u in BY_DVE
            if has(b) and by_dve == (eng is nc.vector):
                upto(eng, s_u, NU, b, u + 1)
                upto(eng, s_pv, NU, b, u - 2)
                eng.tensor_tensor(PT[:, at, :], uu[:, at, :], uu[:, at, :], ALU.mult)\
                   .then_inc(s_sqd if by_dve else s_sqp, 1)

        block = ctx.enter_context(nc.Block())

        @block.sync
        def _(sp):
            def shift(b, slot, a):
                upto(sp, free["MXb" if a else "MXa"], 1, b, 1)
                sp.dma_start(Qp[SHIFT_ROW:P:32, slot, 2 * a:2 * a + 2, :],
                             nm[:, a, :]).then_inc(s_sh[a], 16)

            def spread_keys(b, slot, a):
                g = slice(2 * a, 2 * a + 2) if soft else slice(0, NG)
                upto(sp, s_pack, 8, b, 4 * a + 4 if soft else 8)
                upto(sp, s_st, NS, b - 3, NS)
                if a == 0:
                    sp.wait_ge(s_init, 5)
                for j in range(NJ):
                    sp.dma_start(Kz[32 * j:32 * j + 32, slot, g, j, :],
                                 Kp[32 * j:32 * j + 32, g, :]).then_inc(s_kz[a], 16)

            def body(b, slot):
                nxt = (slot + 2) % 3
                if not soft:
                    if has(b + 1):
                        spread_keys(b + 1, (slot + 1) % 3, 0)
                        upto(sp, s_lm, 10, b + 1, 10)
                        for h in range(H):
                            sp.dma_start(Mz[8 * h:8 * h + 8, (slot + 1) % 3, h, :],
                                         Mt[8 * h:8 * h + 8, 1, :]).then_inc(s_mz, 16)
                    return
                if has(b):
                    shift(b, slot, 1)
                if has(b + 2):
                    spread_keys(b + 2, nxt, 0)
                if has(b + 1):
                    shift(b + 1, (slot + 1) % 3, 0)
                if has(b + 2):
                    spread_keys(b + 2, nxt, 1)

            drive(sp, body)

        @block.gpsimd
        def _(pool):
            pool.memset(half[:], -0.5).then_inc(s_init, 1)
            pool.memset(Kz[:].rearrange("p a g j s -> p (a g j s)").bitcast(F32), 0.0).then_inc(s_init, 1)
            if not soft:
                pool.memset(Mz[:].rearrange("p a h s -> p (a h s)").bitcast(F32), 0.0).then_inc(s_init, 1)
            else:
                pool.memset(tmp[:], 0.0).then_inc(s_init, 1)
            pool.wait_ge(s_init, 3)

            def body(b, slot):
                nxt = (slot + 2) % 3
                for u in range(NU):
                    if u == 0 and has(b + 2):
                        for k in range(2 if kind == 1 else 1):
                            upto(pool, s_ve, 2 if kind == 1 else 1, b + 2, k + 1)
                            pool.tensor_tensor(rs[:, k, :], ve[:, k, :], half[:], ALU.pow).then_inc(s_rs, 1)
                    if not soft:
                        squares(pool, b, slot, u)
                    if u == 6 and kind != 1 and has(b - 1):
                        upto(pool, s_pve, 1, b - 1, 1)
                        pool.tensor_tensor(prs[:], pve[:], half[:], ALU.pow).then_inc(s_prs, 1)

            drive(pool, body)

        @block.scalar
        def _(act):
            def consume(name, b, slot):
                if name in ("OTa", "OTb", "CS"):
                    return
                upto(act, full[name], 1, b, 1)
                ps = bank(name)
                if name in ("MXa", "MXb"):
                    a = int(name == "MXb")
                    upto(act, s_sh[a], 16, b - 1, 16)
                    act.activation(nm[:, a, :], ps[0:8, 0:S], ACT.Copy, scale=-1.0).then_inc(free[name], 1)
                elif name == "T":
                    upto(act, full["V"], 1, b - 1, 1)
                    act.activation(yT[:], ps[:, 0:S], ACT.Copy).then_inc(free[name], 1)
                elif name in ("Qa", "Ka", "Qb", "Kb"):
                    project(b, ["Qa", "Ka", "Qb", "Kb"].index(name), name, ps)
                elif name == "YT":
                    upto(act, full["PR"], 1, b - 1, 1)
                    act.activation(ynT[:], ps[:, 0:S], ACT.Copy).then_inc(free[name], 1)
                elif name == "PR":
                    upto(act, s_post, 1, b - 1, 1)
                    act.activation(ob[:].rearrange("p c d -> p (c d)"), ps[:, 0:S], ACT.Copy)\
                       .then_inc(free[name], 1)
                elif name == "V":
                    upto(act, s_pv, NU, b - 3, NU)
                    act.wait_ge(s_init, 5)
                    wide = ps.rearrange("p (c s) -> p c s", c=TC)
                    if not soft:
                        upto(act, s_ga, 2, b - 1, 2)
                        act.activation(gl[:], wide[:, :, D:D + H], ACT.Copy).then_inc(s_gl, 1)
                    act.activation(Vx[:, slot, :, :, 0:DH],
                                   wide[:, :, 0:D].rearrange("p c (h d) -> p c h d", d=DH), ACT.Copy)\
                       .then_inc(free[name], 1)

            def project(b, n, name, ps):
                upto(act, s_pack, 8, b, 2 * n - 2)
                if kind == 0:
                    bias = w["bq"] if n % 2 == 0 else w["bk"]
                    for k in range(2):
                        last = act.activation(xq[:, n % 2, k, :], ps[:, k * S:(k + 1) * S], ACT.Identity,
                                              bias=bias[:, n // 2 * 2 + k:n // 2 * 2 + k + 1])
                    last.then_inc(free[name], 1)
                    return
                flat = xq[:, n % 2, :, :].rearrange("p a s -> p (a s)")
                if n % 2 == 0 or not soft:
                    act.activation(flat, ps, ACT.Copy).then_inc(free[name], 1)
                else:
                    act.activation(flat, ps, ACT.Identity,
                                   bias=cst[:, C_COL + K_SHIFT:C_COL + K_SHIFT + 1]).then_inc(free[name], 1)

            def sums(b, a):
                upto(act, s_pv, NU, b, 4 * a + 4)
                upto(act, full["OTb" if a else "OTa"], 1, b - 1, 1)
                act.activation(OS[:, a, :, :].rearrange("p a s -> p (a s)"), pv_ps[:], ACT.Copy).then_inc(s_os, 1)

            def body(b, slot):
                for u in range(NU):
                    if u == lag and has(b - 1):
                        sums(b - 1, 1)
                    if u == 4 + lag and has(b):
                        sums(b, 0)
                    for name, batch in due(u, 0, b):
                        consume(name, batch, (slot + offset[name]) % 3)
                    if soft and has(b):
                        for c in range(TC):
                            v = 2 * u + c
                            at = 2 * NU * slot + v
                            upto(act, s_st, NS, b, v + 1)
                            upto(act, s_pv, NU, b, u - 2)
                            act.activation(PT[:, at % NPT, :], st_ps[:, at % 3, :], ACT.Exp, scale=SCALE)\
                               .then_inc(s_exp, 1)
                    if not soft and has(b):
                        upto(act, s_S, NU, b, u + 1)
                        upto(act, s_u, NU, b, u - 2)
                        act.activation(rr[:, third(slot, u), :], turn(slot, u, 0), ACT.Exp, scale=0.5).then_inc(s_dexp, 1)
                        upto(act, s_st, NS, b, u + 1)
                        upto(act, s_u, NU, b, u - 2)
                        act.activation(tt[:, third(slot, u), :], turn(slot, u, 1), ACT.Abs).then_inc(s_t, 1)
                    if not soft and u == 4 and has(b + 2):
                        upto(act, s_ga, 2, b + 2, 2)
                        upto(act, s_lgr, 1, b + 1, 1)
                        act.activation(ge[:], ga[:], ACT.Exp, scale=-1.0).then_inc(s_ge, 1)
                        upto(act, s_ge, 2, b + 2, 1)
                        act.activation(ge[:], ge[:], ACT.Ln, bias=1.0).then_inc(s_ge, 1)
                    for name, batch in due(u, 1, b):
                        consume(name, batch, (slot + offset[name]) % 3)

            drive(act, body)

        @block.vector
        def _(dve):
            dve.memset(Vx[:], 0.0).then_inc(s_init, 1)
            dve.wait_ge(s_init, 4)
            dve.memset(Vx[:, :, :, :, DH:DH + 1], 1.0).then_inc(s_init, 1)

            def pack(b, slot, n):
                a, is_k = n // 2, n % 2
                lk = Link(dve, s_pack, 8, b).skip_to(2 * n)
                upto(dve, free[["Qa", "Ka", "Qb", "Kb"][n]], 1, b, 1)
                upto(dve, s_pack, 8, b, 2 * n - 2)
                lk(dve.tensor_copy(hi[:, n % 2, :, :].rearrange("p a s -> p (a s)"),
                                   xq[:, n % 2, :, :].rearrange("p a s -> p (a s)")))
                mask = cst[:, C_COL + (K_LOW_K if is_k else K_LOW_Q):][:, 0:1]
                if is_k:
                    upto(dve, s_kz[a if soft else 0], 64, b - 1, 64)
                    dst = Kp[:, 2 * a:2 * a + 2, :]
                else:
                    upto(dve, s_st, NS, b - 3, NS)
                    dst = Qp[:, slot, 2 * a:2 * a + 2, :]
                dve.scalar_tensor_tensor(dst, hi[:, n % 2, :, :], mask, xq[:, n % 2, :, :], ALU.mult, ALU.add)\
                   .then_inc(s_pack, 1)

            def ln_stats(b):
                lk = Link(dve, s_ln, LINKS_LN, b)
                lk(*[dve.bn_stats(stats[:, c, :], X[:, ds(b * TC + c, 1), :].rearrange("p a d -> p (a d)"))
                     for c in range(TC)])
                dve.memset(pad[:], 0.0)
                lk(*[dve.bn_aggr(mv[:, c, :], stats[:, c, :]) for c in range(TC)])
                dve.tensor_scalar(ve[:, 0, :], mv[:, :, 1], EPS_LN, None, ALU.add).then_inc(s_ve, 1)
                if kind == 1:
                    upto(dve, s_rs, 2, b, 1)
                    lk(dve.tensor_tensor(tmp2[:, 0, :], mv[:, :, 1], rs[:, 0, :], ALU.mult))
                    lk(dve.tensor_tensor(tmp2[:, 1, :], tmp2[:, 0, :], rs[:, 0, :], ALU.mult))
                    dve.tensor_scalar(ve[:, 1, :], tmp2[:, 1, :], EPS_RMS, None, ALU.add).then_inc(s_ve, 1)

            def ln_apply(b):
                lk = Link(dve, s_ln, LINKS_LN, b).skip_to(6 if kind == 1 else 4)
                upto(dve, s_rs, 2 if kind == 1 else 1, b, 2 if kind == 1 else 1)
                upto(dve, full["T"], 1, b - 1, 1)
                rstd = rs[:, 0, :]
                if kind == 1:
                    lk(dve.tensor_tensor(rs2[:], rs[:, 0, :], rs[:, 1, :], ALU.mult))
                    rstd = rs2[:]
                    for c in range(TC):
                        lk(dve.tensor_scalar(XB[:, ds(b * TC + c, 1), :].rearrange("p a d -> p (a d)"),
                                             X[:, ds(b * TC + c, 1), :].rearrange("p a d -> p (a d)"),
                                             mv[:, c, 0:1], rs[:, 0, c:c + 1], ALU.subtract, ALU.mult))
                for c in range(TC):
                    last = dve.tensor_scalar(y[:, c, :], X[:, ds(b * TC + c, 1), :].rearrange("p a d -> p (a d)"),
                                             mv[:, c, 0:1], rstd[:, c:c + 1], ALU.subtract, ALU.mult)
                    if c == 0:
                        last.then_inc(s_ln, 1)
                last.then_inc(s_y, 1)

            def normalize(b, a):
                name = "OTa" if a == 0 else "OTb"
                upto(dve, full[name], 1, b, 1)
                if a == 0:
                    if soft:
                        upto(dve, full["YT"], 1, b - 1, 1)
                upto(dve, free["OTb" if a == 0 else "OTa"], 1, b - 1 if a == 0 else b, 1)
                v = bank(name).rearrange("p (c k r) -> p c k r", c=TC, r=32)
                dve.reciprocal(rc[:], v[:, :, :, DH]).then_inc(s_lo, 1)
                upto(dve, s_lo, 2, b, a + 1)
                dve.tensor_tensor(yn[:, :, 64 * a:64 * a + 64].rearrange("p c (k r) -> p c k r", r=DH),
                                  v[:, :, :, 0:DH], rc[:].unsqueeze(3).to_broadcast([P, TC, 8, DH]),
                                  ALU.mult).then_inc(free[name], 1)

            src = ob if soft else yn

            def post_stats(b):
                upto(dve, free["PR" if soft else "OTb"], 1, b, 1)
                if kind == 1:
                    xt = XB[:, ds(b * TC, TC), :]
                    dve.tensor_tensor(xt, xt, src[:], ALU.add).then_inc(s_post, 1)
                    return
                lk = Link(dve, s_lp, 6, b)
                lk(*[dve.bn_stats(pstats[:, c, :], src[:, c, :]) for c in range(TC)])
                dve.memset(pad[:], 0.0)
                lk(*[dve.bn_aggr(pmv[:, c, :], pstats[:, c, :]) for c in range(TC)])
                dve.tensor_scalar(pve[:], pmv[:, :, 1], EPS_LN, None, ALU.add).then_inc(s_pve, 1)

            def post_apply(b):
                lk = Link(dve, s_lp, 6, b).skip_to(4)
                upto(dve, s_prs, 1, b, 1)
                lk(*[dve.tensor_scalar(tmp[:, c, :], src[:, c, :], pmv[:, c, 0:1], prs[:, c:c + 1],
                                       ALU.subtract, ALU.mult) for c in range(TC)])
                xt = X[:, ds(b * TC, TC), :]
                dve.tensor_tensor(xt, xt, tmp[:], ALU.add).then_inc(s_post, 1)

            def body(b, slot):
                for u in range(NU):
                    if u == 0 and has(b + 2):
                        ln_stats(b + 2)
                    if not soft and u == 3 and has(b + 2):
                        upto(dve, s_gl, 1, b + 2, 1)
                        upto(dve, s_lgr, 1, b + 1, 1)
                        dve.scalar_tensor_tensor(ga[:], gl[:], -1.0, gl[:], ALU.mult, ALU.max).then_inc(s_ga, 1)
                        dve.tensor_scalar(gm[:], gl[:], 0.0, None, ALU.min).then_inc(s_ga, 1)
                    if soft and u == 1 and has(b + 2):
                        ln_apply(b + 2)
                    if soft and has(b + 1):
                        for c in range(TC):
                            upto(dve, s_S, 2 * NU, b + 1, 2 * u + c + 1)
                            if u in (0, 4) and c == 0:
                                upto(dve, full["MXa" if u == 0 else "MXb"], 1, b, 1)
                            j = 2 * (u % 2)
                            g2 = u // 2 % 2
                            dve.tensor_reduce(mxs[:, u // 4, c, 2 * j + g2:2 * j + g2 + 3:2],
                                              score_ps[:, c, :].rearrange("p (h s) -> p h s", h=2),
                                              AX.X, ALU.max).then_inc(s_max, 1)
                    if soft and u == 0 and has(b - 1):
                        normalize(b - 1, 0)
                    if soft and u == 2 and has(b - 1):
                        normalize(b - 1, 1)
                    if not soft:
                        squares(dve, b, slot, u)
                    if not soft and has(b):
                        upto(dve, s_dexp, NU, b, u + 1)
                        upto(dve, s_t, NU, b, u + 1)
                        at = third(slot, u)
                        if u >= 3:
                            squared(dve, b, u - 3)
                        elif has(b - 1):
                            squared(dve, b - 1, u + NU - 3)
                        dve.scalar_tensor_tensor(uu[:, at, :], tt[:, at, :], EPS_POW, rr[:, at, :],
                                                 ALU.add, ALU.mult).then_inc(s_u, 1)
                    if not soft and u in (0, 4) and has(b - 1):
                        normalize(b - 1, u // 4)
                    if not soft and u == 0 and has(b + 2):
                        ln_apply(b + 2)
                    if not soft and u == 5 and has(b + 2):
                        upto(dve, s_ge, 2, b + 2, 2)
                        upto(dve, full["CS"], 1, b + 1, 1)
                        dve.tensor_tensor(lgr[:], gm[:].unsqueeze(3).to_broadcast([P, TC, H, 8]),
                                          ge[:].unsqueeze(3).to_broadcast([P, TC, H, 8]),
                                          ALU.subtract).then_inc(s_lgr, 1)
                    if not soft and u == 6 and has(b + 2):
                        upto(dve, full["CS"], 1, b + 2, 1)
                        upto(dve, s_lm, 10, b + 1, 10)
                        dve.tensor_copy(LG[:], bank("CS")[:, 0:S]).then_inc(free["CS"], 1)
                    if u in PACKED and has(b + 2):
                        pack(b + 2, (slot + 2) % 3, PACKED.index(u))
                    if u + NU in PACKED and has(b + 1):
                        pack(b + 1, (slot + 1) % 3, PACKED.index(u + NU))
                    if not soft and u in (0, 1, 2) and has(b + 1):
                        cum_split(b + 1, (slot + 1) % 3, u)
                    if u == 6 and has(b - 1):
                        post_stats(b - 1)
                    if u == 7 and has(b - 1) and kind != 1:
                        post_apply(b - 1)

            def cum_split(b, slot, third):
                col = lambda k: cst[:, C_COL + k:C_COL + k + 1]
                if third == 0:
                    lk = Link(dve, s_lm, 10, b)
                    upto(dve, free["CS"], 1, b, 1)
                    lk(dve.tensor_copy(l1[:], LG[:]))
                    lk(dve.tensor_tensor(lrem[:, 0, :], LG[:], l1[:], ALU.subtract))
                    lk(dve.tensor_copy(l2[:], lrem[:, 0, :]))
                elif third == 1:
                    lk = Link(dve, s_lm, 10, b).skip_to(3)
                    upto(dve, s_mz, 256, b - 1, 256)
                    lk(dve.tensor_tensor(l3[:], lrem[:, 0, :], l2[:], ALU.subtract),
                       dve.tensor_scalar(Mt[:, 0, :], l1[:], col(K_M0), col(K_M345), ALU.mult, ALU.add),
                       dve.tensor_scalar(Ms[:, slot, 0, :], l1[:], col(K_N3), col(K_M012), ALU.mult, ALU.add))
                else:
                    lk = Link(dve, s_lm, 10, b).skip_to(6)
                    lk(dve.scalar_tensor_tensor(lrem[:, 0, :], l2[:], col(K_M1), Mt[:, 0, :],
                                                ALU.mult, ALU.add),
                       dve.scalar_tensor_tensor(lrem[:, 1, :], l2[:], col(K_N4), Ms[:, slot, 0, :],
                                                ALU.mult, ALU.add))
                    lk(dve.scalar_tensor_tensor(Mt[:, 1, :], l3[:], col(K_M2), lrem[:, 0, :],
                                                ALU.mult, ALU.add),
                       dve.scalar_tensor_tensor(Ms[:, slot, 1, :], l3[:], col(K_N5), lrem[:, 1, :],
                                                ALU.mult, ALU.add))

            drive(dve, body)

        @block.tensor
        def _(pe):
            ident = cst[:, C_IDENT:C_IDENT + P]

            def open_bank(name, b):
                at = before(name, b)
                if at is not None:
                    upto(pe, free[at[0]], 1, at[1], 1)

            def transposes(b):
                open_bank("T", b)
                upto(pe, s_y, 1, b + 2, 1)
                for c in range(TC):
                    last = pe.transpose(bank("T")[:, c * P:(c + 1) * P], y[:, c, :], ident)
                last.then_inc(full["T"], 1)

            def project(b, n):
                name = ["Qa", "Ka", "Qb", "Kb"][n]
                open_bank(name, b)
                upto(pe, free["T"], 1, b + 2, 1)
                wt = w["wq"] if n % 2 == 0 else w["wk"]
                for k in range(2):
                    g = n // 2 * 2 + k
                    last = pe.matmul(bank(name)[:, k * S:(k + 1) * S], wt[:, g, :], yT[:], start=True, stop=True)
                last.then_inc(full[name], 1)

            def values(b):
                open_bank("V", b)
                n = D if soft else D + H
                for c in range(TC):
                    out = bank("V")[:, c * S:c * S + n]
                    last = pe.matmul(out, yT[:, c * P:(c + 1) * P], w["wv"][:, 0:n], start=True, stop=kind != 0)
                    if kind == 0:
                        last = pe.matmul(out, cst[0:1, C_TRI + P:C_TRI + 2 * P], w["bv"][0:1, :],
                                         start=False, stop=True)
                last.then_inc(full["V"], 1)

            def shift_rows(b, batch, a):
                name = "MXb" if a else "MXa"
                open_bank(name, b)
                upto(pe, s_max, 2 * NU, batch, NU * (a + 1))
                for c in range(TC):
                    last = pe.transpose(bank(name)[0:8, c * P:(c + 1) * P], mxs[:, a, c, :], ident)
                last.then_inc(full[name], 1)

            def turn_out(b, a):
                name = "OTb" if a else "OTa"
                open_bank(name, b)
                upto(pe, s_os, 2, b - 1, a + 1)
                for c in range(TC):
                    for k in range(2):
                        o = (c * 2 + k) * P
                        last = pe.transpose(bank(name)[:, o:o + P], OS[:, a, k, c * P:(c + 1) * P], ident)
                last.then_inc(full[name], 1)

            def out_turn(b):
                open_bank("YT", b)
                upto(pe, free["OTb"], 1, b - 1, 1)
                for c in range(TC):
                    last = pe.transpose(bank("YT")[:, c * P:(c + 1) * P], yn[:, c, :], ident)
                last.then_inc(full["YT"], 1)

            def out_project(b):
                open_bank("PR", b)
                upto(pe, free["YT"], 1, b - 1, 1)
                for c in range(TC):
                    out = bank("PR")[:, c * D:(c + 1) * D]
                    last = pe.matmul(out, ynT[:, c * P:(c + 1) * P], w["wo"][:, :], start=True, stop=kind != 0)
                    if kind == 0:
                        last = pe.matmul(out, cst[0:1, C_TRI + P:C_TRI + 2 * P], w["bo"][0:1, :],
                                         start=False, stop=True)
                last.then_inc(full["PR"], 1)

            def scores(b, slot, u):
                g, j = u // 2, 2 * (u % 2)
                if u in (0, 4):
                    upto(pe, s_kz[u // 4], 64, b, 64)
                    upto(pe, s_pack, 8, b, 4 * (u // 4) + 2)
                for c in range(TC):
                    upto(pe, s_max, 2 * NU, b, 2 * u + c - 1)
                    pe.matmul(score_ps[:, c, :], Qp[:, slot, g, c * P:(c + 1) * P],
                              Kz[:, slot, g, j:j + 2, :].rearrange("p j s -> p (j s)"),
                              start=True, stop=True).then_inc(s_S, 1)

            def key_scores(b, slot, u):
                g, j = u // 2, 2 * (u % 2)
                if soft:
                    if u in (0, 4):
                        upto(pe, s_sh[u // 4], 16, b, 16)
                else:
                    if u == 0:
                        upto(pe, s_kz[0], 64, b, 64)
                        upto(pe, s_pack, 8, b, 8)
                    upto(pe, s_dexp, NU, b, u)
                for c in range(TC):
                    at = 2 * NU * slot + 2 * u + c
                    if soft:
                        upto(pe, s_exp, NS, b, 2 * u + c - 2)
                    for k in range(2):
                        key = Kz[:, slot, g, j + k, c * P:(c + 1) * P]
                        n = S if soft else S - P * c
                        o = S * k if soft else 2 * S * c + n * k
                        out = st_ps[:, at % 3, o:o + n] if soft else turn(slot, u, 1)[:, o:o + n]
                        last = pe.matmul(out, key, Qp[:, slot, g, S - n:S], start=True, stop=True)
                    if soft or c == TC - 1:
                        last.then_inc(s_st, 1)

            def decays(b, slot, u):
                if u == 0:
                    upto(pe, s_mz, 256, b, 256)
                    upto(pe, s_lm, 10, b, 10)
                upto(pe, s_t, NU, b, u - 1)
                for c in range(TC):
                    n = S - P * c
                    for k in range(2):
                        o = 2 * S * c + n * k
                        pe.matmul(turn(slot, u, 0)[:, o:o + n], Ms[:, slot, 1, c * P:(c + 1) * P],
                                  Mz[:, slot, 2 * u + k, S - n:S], start=True, stop=False)
                        last = pe.matmul(turn(slot, u, 0)[:, o:o + P], cstb[:, 0:P], cstb[:, P:2 * P],
                                         start=False, stop=True)
                last.then_inc(s_S, 1)

            def times_v(b, slot, u):
                g, j = u // 2, 2 * (u % 2)
                squared(pe, b, u)
                if u in (0, 4):
                    upto(pe, s_os, 2, b, u // 4)
                if u == 0:
                    upto(pe, free["V"], 1, b, 1)
                for k in range(2):
                    h = 2 * u + k
                    for c in range(TC):
                        n = S if soft else S - P * c
                        p = (PT[:, (2 * NU * slot + 2 * u + c) % NPT, S * k:S * k + S] if soft
                             else PT[:, third(slot, u), 2 * S * c + n * k:2 * S * c + n * k + n])
                        q = g % 2 * S + S
                        last = pe.matmul(pv_ps[32 * (j + k):32 * (j + k) + 32, q - n:q], Vx[:, slot, c, h, :],
                                         p, start=(c == 0), stop=(c == TC - 1),
                                         skip_group_check=True)
                last.then_inc(s_pv, 1)

            def step(name, b):
                if name == "T":
                    transposes(b)
                elif name in ("Qa", "Ka", "Qb", "Kb"):
                    project(b, ["Qa", "Ka", "Qb", "Kb"].index(name))
                elif name == "V":
                    values(b)
                elif name in ("MXa", "MXb"):
                    shift_rows(b, b + offset[name], int(name == "MXb"))
                elif name in ("OTa", "OTb"):
                    turn_out(b, int(name == "OTb"))
                elif name == "YT":
                    out_turn(b)
                elif name == "PR":
                    out_project(b)
                else:
                    cumulate(b)

            def body(b, slot):
                for u in range(NU):
                    if soft and has(b + 1):
                        scores(b + 1, (slot + 1) % 3, u)
                    for name, _ in due(u, 0, b):
                        step(name, b)
                    if not soft and has(b):
                        decays(b, slot, u)
                    if has(b):
                        key_scores(b, slot, u)
                    for name, _ in due(u, 1, b):
                        step(name, b)
                    if u >= lag and has(b):
                        times_v(b, slot, u - lag)
                    if u < lag and has(b - 1):
                        times_v(b - 1, (slot + 2) % 3, u + NU - lag)

            def cumulate(b):
                open_bank("CS", b)
                upto(pe, s_lgr, 1, b + 2, 1)
                pe.matmul(bank("CS")[:, 0:S], lgr[:, 0, :, :].rearrange("p h r -> p (h r)"),
                          cst[:, C_TRI:C_TRI + S], start=True, stop=False)
                pe.matmul(bank("CS")[:, P:S], lgr[:, 1, :, :].rearrange("p h r -> p (h r)"),
                          cst[:, C_TRI:C_TRI + P], start=False, stop=True).then_inc(full["CS"], 1)

            drive(pe, body)


def load_weights(nc, cst, cstb, X, w, weights, dram):
    with ExitStack() as ctx:
        take = semaphores(nc, ctx)

        def sem(name):
            return take(name)

        names = ["wq0", "wk0", "wv0", "wo0", "wq2", "wk2", "wv2"]
        rows = ctx.enter_context(nc.sbuf_tensor("rows", [P, len(names), D], F32))
        gates = ctx.enter_context(nc.sbuf_tensor("gates", [H + NE, D], F32))
        flat = ctx.enter_context(nc.sbuf_tensor("flat", [P, 3, D], F32))
        norm = ctx.enter_context(nc.sbuf_tensor("norm", [P, 2], F32))
        route0 = ctx.enter_context(nc.sbuf_tensor("route0", [P, NE], F32))
        bias = ctx.enter_context(nc.sbuf_tensor("bias", [1, 2, D], F32))
        wide = ctx.enter_context(nc.sbuf_tensor("wide", [1, 2, NG, NJ, 4, DH], F32))
        turned = ctx.enter_context(nc.psum_tensor("turned", [P, 8, 512], F32))
        s_rows = sem("s_rows")
        s_flat = sem("s_flat")
        s_x = sem("s_x")
        s_zero = sem("s_zero")
        s_turned = sem("s_turned")
        s_wide = sem("s_wide")
        s_columns = sem("s_columns")
        s_done = sem("s_done")
        block = ctx.enter_context(nc.Block())
        packed = {}
        for n in range(3):
            for name in ("wq", "wk"):
                packed[name, n] = weights[n][name][:].rearrange("p g (j c d) -> p g j c d", j=NJ, c=4)

        def heads(ap):
            return ap.rearrange("p (g j d) -> p g j d", g=NG, j=NJ)

        @block.sync
        def _(sp):
            for k, src in enumerate([dram["L0_attn_Wq"], dram["L0_attn_Wk"], dram["L0_attn_Wv"], dram["L0_attn_Wo"]]):
                sp.dma_start(rows[:, k, :], src).then_inc(s_rows, 16)
            sp.dma_start(rows[:, 4:7, :], dram["L1_attn_W"][0:3 * D, :].rearrange("(a p) d -> p a d", a=3))\
                .then_inc(s_rows, 16)
            sp.dma_start(gates[0:H, :], dram["L1_attn_W"][3 * D:3 * D + H, :]).then_inc(s_rows, 16)
            sp.dma_start(gates[H:H + NE, :], dram["L1_ffn_router_w"]).then_inc(s_rows, 16)
            sp.dma_start(cst[:], dram["constants"]).then_inc(s_rows, 16)
            for k, name in enumerate(["L0_attn_bq", "L0_attn_bk"]):
                sp.dma_start(bias[0:1, k, :], dram[name].rearrange("(a d) -> a d", a=1)).then_inc(s_flat, 16)
            sp.dma_start(weights[0]["bv"][:], dram["L0_attn_bv"].rearrange("(a d) -> a d", a=1)).then_inc(s_flat, 16)
            sp.dma_start(weights[0]["bo"][:], dram["L0_attn_bo"].rearrange("(a d) -> a d", a=1)).then_inc(s_flat, 16)
            for k, name in enumerate(["L0_ffn_wq", "L0_ffn_wk", "L0_ffn_wv"]):
                sp.dma_start(flat[:, k, :], dram[name]).then_inc(s_flat, 16)
            sp.dma_start(weights[1]["wo"][:], dram["L0_ffn_wo"]).then_inc(s_flat, 16)
            sp.dma_start(route0[:], dram["L0_ffn_router_w"]).then_inc(s_flat, 16)
            sp.dma_start(norm[:, 1:2], dram["L0_ffn_norm2_w"].rearrange("(d a) -> d a", a=1)).then_inc(s_flat, 16)
            sp.dma_start(norm[:, 0:1], dram["L0_ffn_norm1_w"].rearrange("(d a) -> d a", a=1)).then_inc(s_flat, 16)
            xt = dram["L0_attn_x"].rearrange("b (c p) d -> p (b c) d", p=P)
            for k in range(4):
                sp.dma_start(X[:, 8 * k:8 * k + 8, :], xt[:, 8 * k:8 * k + 8, :]).then_inc(s_x, 16)
            sp.wait_ge(s_x, 64)

        @block.gpsimd
        def _(pool):
            for n in range(3):
                for name in ("wq", "wk"):
                    pool.memset(packed[name, n][:, :, :, 3, :], 0.0).then_inc(s_zero, 1)
            pool.memset(wide[:], 0.0).then_inc(s_zero, 1)
            pool.wait_ge(s_zero, 7)
            pool.memset(wide[:, 1, :, :, 3, 0:1], 1.0).then_inc(s_zero, 1)

        @block.tensor
        def _(pe):
            pe.wait_ge(s_rows, 128)
            for k in range(len(names)):
                pe.transpose(turned[:, k, 0:P], rows[:, k, :], cst[:, 0:P]).then_inc(s_turned, 1)
            pe.transpose(turned[:, 7, 0:H + NE], gates[:], cst[0:H + NE, 0:H + NE]).then_inc(s_turned, 1)
            pe.wait_ge(s_wide, 6)
            pe.wait_ge(s_zero, 8)
            pe.wait_ge(s_done, 3)
            for k in range(2):
                for g in range(NG):
                    last = pe.matmul(turned[:, 0, k * NG + g:k * NG + g + 1],
                                     wide[0:1, k, g, :, :, :].rearrange("p j c d -> p (j c d)"),
                                     cst[0:1, C_TRI + P:C_TRI + P + 1], start=True, stop=True)
            last.then_inc(s_columns, 1)

        @block.vector
        def _(dve):
            dve.wait_ge(s_flat, 176)
            dve.wait_ge(s_zero, 8)
            for k in range(2):
                for c in range(3):
                    dve.tensor_copy(wide[:, k, :, :, c, :], heads(bias[0:1, k, :])).then_inc(s_wide, 1)
            for k, dst in enumerate([("wq", 0), ("wk", 0), None, None, ("wq", 2), ("wk", 2)]):
                dve.wait_ge(s_turned, k + 1)
                if dst:
                    for c in range(3):
                        dve.tensor_copy(packed[dst][:, :, :, c, :], heads(turned[:, k, 0:P])).then_inc(s_done, 1)
            dve.tensor_copy(weights[0]["wv"][:], turned[:, 2, 0:P])
            dve.tensor_copy(weights[0]["wo"][:], turned[:, 3, 0:P])
            dve.wait_ge(s_turned, 8)
            dve.tensor_copy(weights[2]["wv"][:, 0:D], turned[:, 6, 0:P])
            dve.tensor_copy(weights[2]["wv"][:, D:D + H], turned[:, 7, 0:H])
            dve.tensor_copy(w["router1"][:], turned[:, 7, H:H + NE])
            for k, name in enumerate(("wq", "wk")):
                for c in range(3):
                    dve.tensor_scalar(packed[name, 1][:, :, :, c, :], heads(flat[:, k, :]), norm[:, 0:1],
                                      None, ALU.mult)
            dve.tensor_scalar(weights[1]["wv"][:], flat[:, 2, :], norm[:, 0:1], None, ALU.mult)
            dve.tensor_scalar(w["router0"][:], route0[:], norm[:, 1:2], None, ALU.mult)
            dve.tensor_copy(cstb[:, 0:P], cst[:, C_IDENT:C_IDENT + P])
            dve.tensor_copy(cstb[:, P:2 * P], cst[:, C_LATE:C_LATE + P])
            dve.wait_ge(s_columns, 1)
            dve.tensor_copy(weights[0]["bq"][:], turned[:, 0, 0:NG])
            dve.tensor_copy(weights[0]["bk"][:], turned[:, 0, NG:2 * NG]).then_inc(s_done, 1)
            dve.wait_ge(s_done, 13)


def router_layer(nc, kind, cst, src, yall, hT, logits, router):
    NBLK, TB = 8, 4
    with ExitStack() as ctx:
        take = semaphores(nc, ctx)

        def sb(name, shape, dt):
            return ctx.enter_context(nc.sbuf_tensor(f"r{name}{kind}", shape, dt))

        def sem(name):
            return take(f"r{name}{kind}")

        pad = sb("pad", [1, 1], F32)
        stats = sb("stats", [P, TB, 6], F32)
        mv = sb("mv", [P, TB, 2], F32)
        sq = sb("sq", [P, TB], F32)
        ve = sb("ve", [P, TB], F32)
        rs = sb("rs", [P, TB], F32)
        half = sb("half", [P, TB], F32)
        y = sb("y", [P, 2, TB, D], F32)
        yT = sb("yT", [P, 2, TB * P], F32)
        turn_ps = ctx.enter_context(nc.psum_tensor(f"rturn{kind}", [P, 2, 512], F32))
        log_ps = ctx.enter_context(nc.psum_tensor(f"rlog{kind}", [P, 2, 512], F32))
        s_half = sem("s_half")
        s_link = sem("s_link")
        s_ve = sem("s_ve")
        s_rs = sem("s_rs")
        s_y = sem("s_y")
        s_turn = sem("s_turn")
        s_yT = sem("s_yT")
        s_log = sem("s_log")
        s_logits = sem("s_logits")
        block = ctx.enter_context(nc.Block())
        LINKS = 10 if kind == 0 else 8

        def loop(eng, body):
            body(0, 0)
            body(1, 1)
            with eng.Fori(0, NBLK // 2 - 1) as i:
                for k in range(2):
                    body(i * 2 + (2 + k), k)

        @block.vector
        def _(dve):
            def body(n, k):
                lk = Link(dve, s_link, LINKS, n)
                rows = [src[:, ds(n * TB + c, 1), :].rearrange("p a d -> p (a d)") for c in range(TB)]
                lk(*[dve.bn_stats(stats[:, c, :], rows[c]) for c in range(TB)])
                dve.memset(pad[:], 0.0)
                lk(*[dve.bn_aggr(mv[:, c, :], stats[:, c, :]) for c in range(TB)])
                if kind == 0:
                    lk(dve.tensor_tensor(sq[:], mv[:, :, 0], mv[:, :, 0], ALU.mult))
                    lk(dve.tensor_tensor(sq[:], sq[:], mv[:, :, 1], ALU.add))
                    dve.tensor_scalar(ve[:], sq[:], EPS_RMS, None, ALU.add).then_inc(s_ve, 1)
                else:
                    dve.tensor_scalar(ve[:], mv[:, :, 1], EPS_LN, None, ALU.add).then_inc(s_ve, 1)
                upto(dve, s_rs, 1, n, 1)
                upto(dve, s_turn, 1, n - 2, 1)
                for c in range(TB):
                    out = y[:, k, c, :] if kind == 0 else yall[:, ds(n * TB + c, 1), :].rearrange("p a d -> p (a d)")
                    if kind == 0:
                        last = dve.tensor_scalar(out, rows[c], rs[:, c:c + 1], None, ALU.mult)
                    else:
                        last = dve.tensor_scalar(out, rows[c], mv[:, c, 0:1], rs[:, c:c + 1],
                                                 ALU.subtract, ALU.mult)
                        lastc = dve.tensor_scalar(y[:, k, c, :], rows[c], mv[:, c, 0:1], rs[:, c:c + 1],
                                                  ALU.subtract, ALU.mult)
                        last = lastc
                last.then_inc(s_y, 1)
                upto(dve, s_log, 1, n, 1)
                dve.tensor_copy(logits[:, ds(n * TB, TB), :],
                                log_ps[:, k, 0:TB * NE].rearrange("p (c e) -> p c e", e=NE)).then_inc(s_logits, 1)

            loop(dve, body)

        @block.gpsimd
        def _(pool):
            pool.memset(half[:], -0.5).then_inc(s_half, 1)
            pool.wait_ge(s_half, 1)

            def body(n, k):
                upto(pool, s_ve, 1, n, 1)
                pool.tensor_tensor(rs[:], ve[:], half[:], ALU.pow).then_inc(s_rs, 1)

            loop(pool, body)

        @block.tensor
        def _(pe):
            def body(n, k):
                upto(pe, s_y, 1, n, 1)
                upto(pe, s_yT, 1, n - 2, 1)
                for c in range(TB):
                    last = pe.transpose(turn_ps[:, k, c * P:(c + 1) * P], y[:, k, c, :], ident)
                last.then_inc(s_turn, 1)
                upto(pe, s_yT, 1, n, 1)
                upto(pe, s_logits, 1, n - 2, 1)
                for c in range(TB):
                    last = pe.matmul(log_ps[:, k, c * NE:(c + 1) * NE], yT[:, k, c * P:(c + 1) * P], router[:],
                                     start=True, stop=True)
                last.then_inc(s_log, 1)

            ident = cst[:, C_IDENT:C_IDENT + P]
            loop(pe, body)

        @block.scalar
        def _(act):
            def body(n, k):
                upto(act, s_turn, 1, n, 1)
                if kind == 0:
                    act.activation(hT[:, ds(n * TB * P, TB * P)], turn_ps[:, k, :], ACT.Copy)
                upto(act, s_log, 1, n - 2, 1)
                act.activation(yT[:, k, :], turn_ps[:, k, :], ACT.Copy).then_inc(s_yT, 1)

            loop(act, body)


def route(nc, kind, cst, logits, bias_row, comb, idx, wsel, noop):
    T = NTILE
    with ExitStack() as ctx:
        take = semaphores(nc, ctx)

        def sb(name, shape, dt=F32):
            return ctx.enter_context(nc.sbuf_tensor(f"t{name}{kind}", shape, dt))

        def sem(name):
            return take(f"t{name}{kind}")

        c8 = [P, T, NE]
        pr = sb("pr", c8)
        p2 = sb("p2", c8)
        sc = sb("sc", c8)
        sel = sb("sel", [P, 2, T, NE])
        m = sb("m", [P, 2, T])
        one = sb("one", [P, T])
        two = sb("two", [P, T])
        s_v = sem("s_v")
        s_a = sem("s_a")
        s_p = sem("s_p")
        s_b = sem("s_b")
        if kind == 1:
            bias8 = sb("bias8", [P, NE])
            bias1 = sb("bias1", [1, NE])
            mask = sb("mask", c8)
            ranks = sb("ranks", c8)
            totals = sb("totals", [P, NE, T])
            prefix = sb("prefix", [P, NE, T])
            zeros = sb("zeros", [P, T])
            slot = sb("slot", [P, T])
            ok = sb("ok", [P, T])
            ps = ctx.enter_context(nc.psum_tensor("tps", [P, 3, 512], F32))
        block = ctx.enter_context(nc.Block())
        EXP0, EXP1 = 1, 2

        def wide(ap):
            return ap.unsqueeze(2).to_broadcast(c8)

        def row(at):
            return cst[:, at:at + NE].unsqueeze(1).to_broadcast(c8)

        marks = {}

        @block.vector
        def _(dve):
            lk = Link(dve, s_v, 0, 0)
            lg = logits[:]
            if kind == 1:
                dve.wait_ge(s_p, 1)
                lk(dve.tensor_copy(bias8[:], ps[:, 2, 0:NE]))
                lk(dve.tensor_tensor(lg, lg, bias8[:].unsqueeze(1).to_broadcast(c8), ALU.add))
                lk(dve.memset(zeros[:], 0.0))
            lk(dve.tensor_reduce(one[:], lg, AX.X, ALU.max))
            lk(dve.tensor_tensor(pr[:], lg, wide(one[:]), ALU.subtract))
            marks["pr"] = lk.k
            dve.wait_ge(s_a, EXP0)
            lk(dve.tensor_reduce(one[:], pr[:], AX.X, ALU.add))
            lk(dve.reciprocal(two[:], one[:]))
            lk(dve.tensor_tensor(pr[:], pr[:], wide(two[:]), ALU.mult))
            probs = pr
            for c in range(2):
                lk(dve.tensor_reduce(m[:, c, :], probs[:], AX.X, ALU.max))
                lk(dve.tensor_tensor(sc[:], probs[:], wide(m[:, c, :]), ALU.is_equal))
                lk(dve.tensor_tensor(sc[:], sc[:], row(C_PRI), ALU.mult))
                lk(dve.tensor_reduce(one[:], sc[:], AX.X, ALU.max))
                lk(dve.tensor_tensor(sel[:, c, :, :], sc[:], wide(one[:]), ALU.is_equal))
                if c == 0:
                    lk(dve.scalar_tensor_tensor(p2[:].rearrange("p t e -> p (t e)"),
                                                sel[:, 0, :, :].rearrange("p t e -> p (t e)"), -2.0,
                                                pr[:].rearrange("p t e -> p (t e)"), ALU.mult, ALU.add))
                    probs = p2
            if kind == 0:
                lk(dve.tensor_tensor(one[:], m[:, 1, :], m[:, 0, :], ALU.subtract))
                marks["d"] = lk.k
                dve.wait_ge(s_a, EXP1)
                lk(dve.tensor_scalar(two[:], one[:], 1.0, None, ALU.add))
                lk(dve.reciprocal(m[:, 0, :], two[:]))
                lk(dve.tensor_tensor(m[:, 1, :], one[:], m[:, 0, :], ALU.mult))
                lk(dve.tensor_tensor(sc[:], sel[:, 0, :, :], wide(m[:, 0, :]), ALU.mult))
                lk(dve.tensor_tensor(p2[:], sel[:, 1, :, :], wide(m[:, 1, :]), ALU.mult))
                lk(dve.tensor_tensor(comb[:], sc[:], p2[:], ALU.add))
                return
            for c in range(2):
                lk(dve.tensor_scalar(one[:], m[:, c, :], 0.0, None, ALU.is_gt))
                lk(dve.tensor_tensor(sel[:, c, :, :], sel[:, c, :, :], wide(one[:]), ALU.mult))
            lk(dve.tensor_tensor(mask[:], sel[:, 0, :, :], sel[:, 1, :, :], ALU.add))
            marks["mask"] = lk.k
            dve.wait_ge(s_p, 3)
            lk(dve.tensor_copy(totals[:], ps[:, 1, 0:T * NE].rearrange("p (t e) -> p e t", e=NE)))
            for e in range(NE):
                lk(dve.tensor_tensor_scan(prefix[:, e, :], totals[:, e, :], zeros[:], 0.0, ALU.add, ALU.add))
            lk(dve.tensor_tensor(prefix[:], prefix[:], totals[:], ALU.subtract))
            lk(dve.tensor_tensor(ranks[:], ps[:, 0, 0:T * NE].rearrange("p (t e) -> p t e", e=NE),
                                 prefix[:].rearrange("p e t -> p t e"), ALU.add))
            for c in range(2):
                lk(dve.tensor_tensor(sc[:], sel[:, c, :, :], ranks[:], ALU.mult))
                lk(dve.tensor_reduce(one[:], sc[:], AX.X, ALU.add))
                lk(dve.tensor_tensor(sc[:], sel[:, c, :, :], row(C_BASE), ALU.mult))
                lk(dve.tensor_reduce(two[:], sc[:], AX.X, ALU.add))
                lk(dve.scalar_tensor_tensor(slot[:], one[:], -1.0, two[:], ALU.add, ALU.add))
                lk(dve.tensor_scalar(ok[:], one[:], float(CAP), None, ALU.is_le))
                lk(dve.scalar_tensor_tensor(ok[:], one[:], 1.0, ok[:], ALU.is_ge, ALU.mult))
                lk(dve.scalar_tensor_tensor(ok[:], two[:], float(CAP * (NE - 1)), ok[:], ALU.is_lt, ALU.mult))
                lk(dve.tensor_tensor(wsel[:, c, :], ok[:], m[:, c, :], ALU.mult))
                lk(dve.tensor_scalar(ok[:], ok[:], -float(BEYOND), float(BEYOND), ALU.mult, ALU.add))
                lk(dve.scalar_tensor_tensor(slot[:], slot[:], 0.0, ok[:], ALU.max, ALU.add))
                lk(dve.tensor_copy(idx[:, c, :], slot[:]))
            lk(dve.tensor_tensor(one[:], sel[:, 0, :, NE - 1], m[:, 0, :], ALU.mult))
            lk(dve.tensor_tensor(two[:], sel[:, 1, :, NE - 1], m[:, 1, :], ALU.mult))
            lk(dve.tensor_tensor(noop[:], one[:], two[:], ALU.add))

        @block.scalar
        def _(act):
            act.wait_ge(s_v, marks["pr"])
            act.activation(pr[:], pr[:], ACT.Exp).then_inc(s_a, 1)
            if kind == 0:
                act.wait_ge(s_v, marks["d"])
                act.activation(one[:], one[:], ACT.Exp).then_inc(s_a, 1)

        if kind == 1:
            @block.sync
            def _(sp):
                sp.dma_start(bias1[:], bias_row).then_inc(s_b, 16)

            @block.tensor
            def _(pe):
                pe.wait_ge(s_b, 16)
                pe.matmul(ps[:, 2, 0:NE], cst[0:1, C_TRI + P:C_TRI + 2 * P], bias1[:], start=True, stop=True)\
                  .then_inc(s_p, 1)
                pe.wait_ge(s_v, marks["mask"])
                flat = mask[:].rearrange("p t e -> p (t e)")
                pe.matmul(ps[:, 0, 0:T * NE], cst[:, C_TRI:C_TRI + P], flat, start=True, stop=True).then_inc(s_p, 1)
                pe.matmul(ps[:, 1, 0:T * NE], cst[:, C_TRI + P:C_TRI + 2 * P], flat, start=True, stop=True)\
                  .then_inc(s_p, 1)


CAP = NT // NE
BEYOND = 1 << 20


def gated_mixture(nc, hT, comb, XB, X, cst, dram):
    NBLK, TB, EX, FC = 8, 4, NE + 1, F0 // P
    NQ = EX * FC
    with ExitStack() as ctx:
        take = semaphores(nc, ctx)

        def sb(name, shape, dt=F32):
            return ctx.enter_context(nc.sbuf_tensor(f"g{name}", shape, dt))

        def sem(name):
            return take(f"g{name}")

        wg = sb("wg", [P, EX, F0])
        wu = sb("wu", [P, EX, F0])
        wd = sb("wd", [P, EX, FC, D])
        norm = sb("norm", [P, 1])
        sg = sb("sg", [P, 2, 512])
        hid = sb("hid", [P, 2, FC, 512])
        acc = sb("acc", [P, 2, TB, D])
        pad = sb("pad", [1, 1])
        stats = sb("stats", [P, TB, 6])
        mv = sb("mv", [P, TB, 2])
        ve = sb("ve", [P, TB])
        rs = sb("rs", [P, TB])
        half = sb("half", [P, TB])
        tmp = sb("tmp", [P, TB, D])
        gate_ps = ctx.enter_context(nc.psum_tensor("gate_ps", [P, 2, 512], F32))
        up_ps = ctx.enter_context(nc.psum_tensor("up_ps", [P, 2, 512], F32))
        down_ps = ctx.enter_context(nc.psum_tensor("down_ps", [P, 2, 512], F32))
        s_w = sem("s_w")
        s_half = sem("s_half")
        s_scaled = sem("s_scaled")
        s_gu = sem("s_gu")
        s_sg = sem("s_sg")
        s_hid = sem("s_hid")
        s_down = sem("s_down")
        s_acc = sem("s_acc")
        s_l = sem("s_l")
        s_ve = sem("s_ve")
        s_rs = sem("s_rs")
        s_res = sem("s_res")
        block = ctx.enter_context(nc.Block())

        def blocks(eng, body):
            body(0)
            with eng.Fori(1, NBLK) as i:
                body(i)

        @block.sync
        def _(sp):
            sp.dma_start(wg[:, 0:NE, :], dram["L0_ffn_e_gate"].rearrange("e d f -> d e f")).then_inc(s_w, 16)
            sp.dma_start(wg[:, NE, :], dram["L0_ffn_sh_gate"]).then_inc(s_w, 16)
            sp.dma_start(wu[:, 0:NE, :], dram["L0_ffn_e_up"].rearrange("e d f -> d e f")).then_inc(s_w, 16)
            sp.dma_start(wu[:, NE, :], dram["L0_ffn_sh_up"]).then_inc(s_w, 16)
            for e in range(NE):
                sp.dma_start(wd[:, e, :, :], dram["L0_ffn_e_down"][e].rearrange("(c f) d -> f c d", f=P))\
                    .then_inc(s_w, 16)
            sp.dma_start(wd[:, NE, :, :], dram["L0_ffn_sh_down"].rearrange("(c f) d -> f c d", f=P)).then_inc(s_w, 16)
            sp.dma_start(norm[:], dram["L0_ffn_norm2_w"].rearrange("(d a) -> d a", a=1)).then_inc(s_w, 16)

        @block.gpsimd
        def _(pool):
            pool.memset(half[:], -0.5).then_inc(s_half, 1)
            pool.wait_ge(s_half, 1)

            def body(i):
                upto(pool, s_ve, 1, i, 1)
                pool.tensor_tensor(rs[:], ve[:], half[:], ALU.pow).then_inc(s_rs, 1)

            blocks(pool, body)

        @block.tensor
        def _(pe):
            pe.wait_ge(s_scaled, 2)

            def hidden(i, q):
                e, c = q // FC, q % FC
                upto(pe, s_hid, NQ, i, q - 1 if q >= 2 else 0)
                rhs = hT[:, ds(i * 512, 512)]
                pe.matmul(gate_ps[:, q % 2, :], wg[:, e, c * P:(c + 1) * P], rhs, start=True, stop=True)
                pe.matmul(up_ps[:, q % 2, :], wu[:, e, c * P:(c + 1) * P], rhs, start=True, stop=True)\
                  .then_inc(s_gu, 1)

            def down(i, e):
                upto(pe, s_hid, NQ, i, FC * (e + 1))
                if e >= 2:
                    upto(pe, s_acc, EX * TB, i, TB * (e - 1))
                else:
                    upto(pe, s_acc, EX * TB, i, 0)
                for t in range(TB):
                    for c in range(FC):
                        last = pe.matmul(down_ps[:, e % 2, t * D:(t + 1) * D], hid[:, e % 2, c, t * P:(t + 1) * P],
                                         wd[:, e, c, :], start=(c == 0), stop=(c == FC - 1))
                last.then_inc(s_down, 1)

            def body(i):
                for q in range(FC):
                    hidden(i, q)
                for e in range(EX):
                    for c in range(FC if e + 1 < EX else 0):
                        hidden(i, FC * (e + 1) + c)
                    down(i, e)

            blocks(pe, body)

        @block.scalar
        def _(act):
            def body(i):
                for q in range(NQ):
                    upto(act, s_gu, NQ, i, q + 1)
                    if q >= 2:
                        upto(act, s_hid, NQ, i, q - 1)
                    else:
                        upto(act, s_hid, NQ, i, 0)
                    act.activation(sg[:, q % 2, :], gate_ps[:, q % 2, :], ACT.Silu).then_inc(s_sg, 1)

            blocks(act, body)

        @block.vector
        def _(dve):
            dve.wait_ge(s_w, 14 * 16)
            for wt in (wg, wu):
                flat = wt[:].rearrange("p e f -> p (e f)")
                dve.tensor_scalar(flat, flat, norm[:, 0:1], None, ALU.mult).then_inc(s_scaled, 1)

            def body(i):
                def product(q):
                    e, c = q // FC, q % FC
                    upto(dve, s_sg, NQ, i, q + 1)
                    if e >= 2:
                        upto(dve, s_down, EX, i, e - 1)
                    else:
                        upto(dve, s_down, EX, i, 0)
                    dve.tensor_tensor(hid[:, e % 2, c, :], sg[:, q % 2, :], up_ps[:, q % 2, :], ALU.mult)\
                       .then_inc(s_hid, 1)

                def add(e):
                    upto(dve, s_down, EX, i, e + 1)
                    if e == 0:
                        upto(dve, s_res, 1, i, 0)
                    else:
                        dve.wait_ge(s_acc, i * (EX * TB) + TB * e)
                    for t in range(TB):
                        d = down_ps[:, e % 2, t * D:(t + 1) * D]
                        into = acc[:, e % 2, t, :]
                        xt = XB[:, ds(i * TB + t, 1), :].rearrange("p a d -> p (a d)")
                        if e == 0:
                            ins = dve.scalar_tensor_tensor(into, d, comb[:, ds(i * TB + t, 1), e], xt,
                                                           ALU.mult, ALU.add)
                        elif e < NE:
                            ins = dve.scalar_tensor_tensor(into, d, comb[:, ds(i * TB + t, 1), e],
                                                           acc[:, (e - 1) % 2, t, :], ALU.mult, ALU.add)
                        else:
                            ins = dve.tensor_tensor(into, d, acc[:, (e - 1) % 2, t, :], ALU.add)
                        ins.then_inc(s_acc, 1)

                for c in range(FC):
                    product(c)
                for e in range(EX):
                    if e + 1 < EX:
                        for c in range(FC):
                            product(FC * (e + 1) + c)
                    add(e)
                dve.wait_ge(s_acc, i * (EX * TB) + EX * TB)
                a = acc[:, (EX - 1) % 2, :, :]
                lk = Link(dve, s_l, 3 * TB, i)
                lk(*[dve.bn_stats(stats[:, t, :], a[:, t, :]) for t in range(TB)])
                dve.memset(pad[:], 0.0)
                lk(*[dve.bn_aggr(mv[:, t, :], stats[:, t, :]) for t in range(TB)])
                dve.tensor_scalar(ve[:], mv[:, :, 1], EPS_LN, None, ALU.add).then_inc(s_ve, 1)
                upto(dve, s_rs, 1, i, 1)
                lk(*[dve.tensor_scalar(tmp[:, t, :], a[:, t, :], mv[:, t, 0:1], rs[:, t:t + 1],
                                       ALU.subtract, ALU.mult) for t in range(TB)])
                xt = X[:, ds(i * TB, TB), :]
                dve.tensor_tensor(xt, xt, tmp[:], ALU.add).then_inc(s_res, 1)

            blocks(dve, body)
            dve.wait_ge(s_res, NBLK)


def capped_mixture(nc, idx, wsel, noop, Y, X, cst, dram, out, xd, od):
    NX, TB, FC = NE - 1, CAP // P, F1 // P
    with ExitStack() as ctx:
        take = semaphores(nc, ctx)

        def sb(name, shape, dt=F32):
            return ctx.enter_context(nc.sbuf_tensor(f"c{name}", shape, dt))

        def sem(name):
            return take(f"c{name}")

        wi = sb("wi", [P, NX, F1])
        wo = sb("wo", [P, NX, FC, D])
        zero = sb("zero", [P, TB, D])
        xe = sb("xe", [P, 2, TB, D])
        xT = sb("xT", [P, 2, CAP])
        hid = sb("hid", [P, 2, FC, CAP])
        res = sb("res", [P, 2, TB, D])
        NR = 8
        got = sb("got", [P, NR, 2, D])
        mix = sb("mix", [P, 2, 3, D])
        stats = sb("stats", [P, NTILE, 6])
        mv = sb("mv", [P, NTILE, 2])
        ve = sb("ve", [P, NTILE])
        rs = sb("rs", [P, NTILE])
        half = sb("half", [P, 1])
        turn_ps = ctx.enter_context(nc.psum_tensor("cturn_ps", [P, 2, 512], F32))
        hid_ps = ctx.enter_context(nc.psum_tensor("chid_ps", [P, 4, 512], F32))
        out_ps = ctx.enter_context(nc.psum_tensor("cout_ps", [P, 2, 512], F32))
        s_w = sem("s_w")
        s_zero = sem("s_zero")
        s_clear = sem("s_clear")
        s_sent = sem("s_sent")
        s_xe = [sem("s_xe0"), sem("s_xe1")]
        s_turn = sem("s_turn")
        s_xT = sem("s_xT")
        s_hp = sem("s_hp")
        s_hid = sem("s_hid")
        s_op = sem("s_op")
        s_res = sem("s_res")
        s_od = [sem("s_od0"), sem("s_od1")]
        s_got = [sem(f"s_got{k}") for k in range(NR)]
        s_m = sem("s_m")
        s_ve = sem("s_ve")
        s_rs = sem("s_rs")
        s_x = sem("s_x")
        s_f = sem("s_f")
        s_n = sem("s_n")
        s_out = sem("s_out")
        block = ctx.enter_context(nc.Block())

        @block.sync
        def _(sp):
            def store(e):
                sp.wait_ge(s_res, e + 1)
                sp.dma_start(od[e * CAP:(e + 1) * CAP, :].rearrange("(c p) d -> p c d", p=P),
                             res[:, e % 2, :, :]).then_inc(s_od[e % 2], 16)

            sp.wait_ge(s_zero, 2)
            for e in range(NX):
                sp.dma_start(xd[e * CAP:(e + 1) * CAP, :].rearrange("(c p) d -> p c d", p=P), zero[:])\
                    .then_inc(s_clear, 16)
            for e in range(NX):
                sp.dma_start(wi[:, e, :], dram["L1_ffn_experts_inter"][e]).then_inc(s_w, 16)
                sp.dma_start(wo[:, e, :, :], dram["L1_ffn_experts_out"][e].rearrange("(c f) d -> f c d", f=P))\
                    .then_inc(s_w, 16)
            sp.wait_ge(s_sent, 16 * 2 * NTILE)
            for e in range(NX):
                if e >= 2:
                    sp.wait_ge(s_turn, e - 1)
                sp.dma_start(xe[:, e % 2, :, :], xd[e * CAP:(e + 1) * CAP, :].rearrange("(c p) d -> p c d", p=P))\
                    .then_inc(s_xe[e % 2], 16)
                if e >= 2:
                    store(e - 2)
            store(NX - 2)
            store(NX - 1)
            ot = out.rearrange("b (c p) d -> p (b c) d", p=P)
            for k in range(4):
                sp.wait_ge(s_x, 8 * (k + 1))
                sp.dma_start(ot[:, 8 * k:8 * k + 8, :], X[:, 8 * k:8 * k + 8, :]).then_inc(s_out, 16)
            sp.wait_ge(s_out, 64)

        @block.gpsimd
        def _(pool):
            pool.memset(zero[:], 0.0).then_inc(s_zero, 1)
            pool.memset(half[:], -0.5).then_inc(s_zero, 1)
            pool.memset(got[:], 0.0).then_inc(s_zero, 1)

            def group(k):
                pool.wait_ge(s_ve, k + 1)
                pool.tensor_tensor(rs[:, 8 * k:8 * k + 8], ve[:, 8 * k:8 * k + 8],
                                   half[:].to_broadcast([P, 8]), ALU.pow).then_inc(s_rs, 1)

            pool.wait_ge(s_zero, 3)
            pool.wait_ge(s_clear, 16 * NX)
            for t in range(NTILE):
                for c in range(2):
                    pool.indirect_dma_start(xd, bass.IndirectOffsetOnAxis(ap=idx[:, c, t:t + 1], axis=0),
                                            Y[:, t, :], None, bounds_check=NX * CAP - 1, oob_is_err=False)\
                        .then_inc(s_sent, 16)
            pool.wait_ge(s_od[0], 16 * 4)
            pool.wait_ge(s_od[1], 16 * 3)
            for t in range(NTILE):
                if t >= NR:
                    pool.wait_ge(s_m, 3 * (t - NR + 1))
                for c in range(2):
                    pool.indirect_dma_start(got[:, t % NR, c, :], None, od,
                                            bass.IndirectOffsetOnAxis(ap=idx[:, c, t:t + 1], axis=0),
                                            bounds_check=NX * CAP - 1, oob_is_err=False)\
                        .then_inc(s_got[t % NR], 16)
                if t % 8 == 7 and t > 8:
                    group(t // 8 - 1)
            group(3)

        @block.tensor
        def _(pe):
            ident = cst[:, C_IDENT:C_IDENT + P]
            pe.wait_ge(s_w, 16 * 2 * NX)

            def turn(e):
                pe.wait_ge(s_xe[e % 2], 16 * (e // 2 + 1))
                if e >= 2:
                    pe.wait_ge(s_xT, e - 1)
                for c in range(TB):
                    last = pe.transpose(turn_ps[:, e % 2, c * P:(c + 1) * P], xe[:, e % 2, c, :], ident)
                last.then_inc(s_turn, 1)

            def up(e):
                pe.wait_ge(s_xT, e + 1)
                for c in range(FC):
                    if e >= 1:
                        pe.wait_ge(s_hid, FC * (e - 1) + c + 1)
                    pe.matmul(hid_ps[:, c, :], wi[:, e, c * P:(c + 1) * P], xT[:, e % 2, :], start=True, stop=True)\
                      .then_inc(s_hp, 1)

            def down(e):
                pe.wait_ge(s_hid, FC * (e + 1))
                if e >= 2:
                    pe.wait_ge(s_res, e - 1)
                for t in range(TB):
                    for c in range(FC):
                        last = pe.matmul(out_ps[:, e % 2, t * D:(t + 1) * D], hid[:, e % 2, c, t * P:(t + 1) * P],
                                         wo[:, e, c, :], start=(c == 0), stop=(c == FC - 1))
                last.then_inc(s_op, 1)

            turn(0)
            for e in range(NX):
                up(e)
                if e + 1 < NX:
                    turn(e + 1)
                if e >= 1:
                    down(e - 1)
            down(NX - 1)

        @block.scalar
        def _(act):
            for e in range(NX):
                act.wait_ge(s_turn, e + 1)
                if e >= 2:
                    act.wait_ge(s_hp, FC * (e - 1))
                act.activation(xT[:, e % 2, :], turn_ps[:, e % 2, :], ACT.Copy).then_inc(s_xT, 1)
                for c in range(FC):
                    act.wait_ge(s_hp, FC * e + c + 1)
                    if e >= 2:
                        act.wait_ge(s_op, e - 1)
                    act.activation(hid[:, e % 2, c, :], hid_ps[:, c, :], ACT.Relu).then_inc(s_hid, 1)

        @block.vector
        def _(dve):
            for e in range(NX):
                dve.wait_ge(s_op, e + 1)
                if e >= 2:
                    dve.wait_ge(s_od[e % 2], 16 * (e // 2))
                dve.tensor_copy(res[:, e % 2, :, :].rearrange("p c d -> p (c d)"), out_ps[:, e % 2, :])\
                   .then_inc(s_res, 1)

            def finish(k):
                dve.wait_ge(s_rs, k + 1)
                for t in range(8 * k, 8 * k + 8):
                    dve.tensor_scalar(Y[:, t, :], Y[:, t, :], mv[:, t, 0:1], rs[:, t:t + 1],
                                      ALU.subtract, ALU.mult).then_inc(s_f, 1)
                    dve.wait_ge(s_f, t + 1)
                    dve.tensor_tensor(X[:, t, :], X[:, t, :], Y[:, t, :], ALU.add).then_inc(s_x, 1)

            for t in range(NTILE):
                dve.wait_ge(s_got[t % NR], 32 * (t // NR + 1))
                g = got[:, t % NR, :, :]
                dve.tensor_scalar(mix[:, t % 2, 0, :], Y[:, t, :], noop[:, t:t + 1], None, ALU.mult)\
                   .then_inc(s_m, 1)
                dve.wait_ge(s_m, 3 * t + 1)
                dve.scalar_tensor_tensor(mix[:, t % 2, 1, :], g[:, 0, :], wsel[:, 0, t:t + 1], mix[:, t % 2, 0, :],
                                         ALU.mult, ALU.add).then_inc(s_m, 1)
                dve.wait_ge(s_m, 3 * t + 2)
                dve.scalar_tensor_tensor(Y[:, t, :], g[:, 1, :], wsel[:, 1, t:t + 1], mix[:, t % 2, 1, :],
                                         ALU.mult, ALU.add).then_inc(s_m, 1)
                dve.wait_ge(s_m, 3 * t + 3)
                dve.bn_stats(stats[:, t, :], Y[:, t, :]).then_inc(s_n, 1)
                dve.wait_ge(s_n, 2 * t + 1)
                dve.bn_aggr(mv[:, t, :], stats[:, t, :]).then_inc(s_n, 1)
                if t % 8 == 7:
                    dve.wait_ge(s_n, 2 * t + 2)
                    k = t // 8
                    dve.tensor_scalar(ve[:, 8 * k:8 * k + 8], mv[:, 8 * k:8 * k + 8, 1], EPS_LN, None, ALU.add)\
                       .then_inc(s_ve, 1)
                    if k >= 1:
                        finish(k - 1)
            finish(3)


def build(nc, dram, out):
    with ExitStack() as ctx:
        def sb(name, shape, dt):
            return ctx.enter_context(nc.sbuf_tensor(name, shape, dt))

        X = sb("X", [P, NTILE, D], F32)
        XB = sb("XB", [P, NTILE, D], F32)
        cst = sb("cst", [P, C_ALL], F32)
        cstb = sb("cstb", [P, 2 * P], BF16)
        w = {"router0": sb("router0", [P, NE], F32), "router1": sb("router1", [P, NE], F32)}
        weights = []
        for n in range(3):
            a = {"wq": sb(f"wq_{n}", [P, NG, P], F32), "wk": sb(f"wk_{n}", [P, NG, P], F32),
                 "wv": sb(f"wv_{n}", [P, D + (H if n == 2 else 0)], F32)}
            if n < 2:
                a["wo"] = sb(f"wo_{n}", [P, D], F32)
            weights.append(a)
        weights[0]["bq"] = sb("bq", [P, NG], F32)
        weights[0]["bk"] = sb("bk", [P, NG], F32)
        weights[0]["bv"] = sb("bv", [1, D], F32)
        weights[0]["bo"] = sb("bo", [1, D], F32)
        load_weights(nc, cst, cstb, X, w, weights, dram)
        attention_layer(nc, 0, X, XB, cst, cstb, weights[0])
        attention_layer(nc, 1, X, XB, cst, cstb, weights[1])
        logits = sb("logits", [P, NTILE, NE], F32)
        with ExitStack() as c1:
            hT = c1.enter_context(nc.sbuf_tensor("hT", [P, NT], F32))
            comb = c1.enter_context(nc.sbuf_tensor("comb", [P, NTILE, NE], F32))
            router_layer(nc, 0, cst, XB, None, hT, logits, w["router0"])
            route(nc, 0, cst, logits, None, comb, None, None, None)
            gated_mixture(nc, hT, comb, XB, X, cst, dram)
        attention_layer(nc, 2, X, XB, cst, cstb, weights[2])
        idx = sb("idx", [P, 2, NTILE], U32)
        wsel = sb("wsel", [P, 2, NTILE], F32)
        noop = sb("noop", [P, NTILE], F32)
        xd = nc.dram_tensor("slots_in", [(NE - 1) * CAP, D], F32).ap()
        od = nc.dram_tensor("slots_out", [(NE - 1) * CAP, D], F32).ap()
        router_layer(nc, 1, cst, X, XB, None, logits, w["router1"])
        route(nc, 1, cst, logits, dram["L1_ffn_router_b"].rearrange("(a e) -> a e", a=1), None, idx, wsel, noop)
        capped_mixture(nc, idx, wsel, noop, XB, X, cst, dram, out, xd, od)


def kernel(**inputs):
    import numpy as _np
    import concourse.bacc as _bacc
    from concourse import mybir as _mybir
    from concourse.bass_utils import run_bass_kernel_spmd as _run

    nc = _bacc.Bacc("TRN2", target_bir_lowering=False, num_devices=1)
    arrays, dram = {}, {}
    for name, a in list(inputs.items()) + [("constants", constant_table())]:
        a = _np.ascontiguousarray(a)
        arrays[f"in_{name}_dram"] = a
        dram[name] = nc.dram_tensor(f"in_{name}_dram", a.shape, _mybir.dt.from_np(a.dtype), kind="ExternalInput").ap()
    out = nc.dram_tensor("out_0_dram", (NB, S, D), _mybir.dt.float32, kind="ExternalOutput").ap()
    build(nc, dram, out)
    r = _run(nc, [arrays], core_ids=[0])
    return r.results[0]["out_0_dram"]
```

```python
from contextlib import ExitStack

import concourse.bass as bass
from concourse import mybir
import numpy as np

F32 = mybir.dt.float32
F16 = mybir.dt.float16
BF16 = mybir.dt.bfloat16
I32 = mybir.dt.int32
U32 = mybir.dt.uint32
ALU = mybir.AluOpType
ACT = mybir.ActivationFunctionType
AX = mybir.AxisListType
ds = bass.ds

P = 128
NB, S, D = 16, 256, 128
NT = NB * S
NTILE = NT // P
TC = S // P
H, DH = 16, 8
NG, NJ = 4, 4
NE = 8
F0 = 256
F1 = 512
EPS_LN = 1e-5
EPS_RMS = 1e-6
EPS_POW = 1e-7
SCALE = float(DH) ** -0.5
SHIFT_ROW = 24
MASKED = -1e30
BIAS_RMS, BIAS_PLAIN = 0, 1

C_IDENT = 0
C_TRI = 128
C_LATE = 384
C_COL = 512
(K_LOW_Q, K_LOW_K, K_SHIFT, K_M0, K_M1, K_M2, K_M345, K_N3, K_N4, K_N5, K_M012) = range(11)
C_PRI = C_COL + 16
C_BASE = C_PRI + 8
C_Q = C_BASE + 8
C_P = C_Q + P
C_ALL = C_P + 1


def constant_table():
    c = np.zeros((P, C_ALL), np.float32)
    p = np.arange(P)
    c[:, C_IDENT:C_IDENT + P] = np.eye(P)
    c[:, C_TRI:C_TRI + P] = p[:, None] <= p[None, :]
    c[:, C_TRI + P:C_TRI + 2 * P] = 1.0
    c[:, C_LATE:C_LATE + P] = np.where(p[:, None] > p[None, :], MASKED, 0.0)
    r = p % 32
    c[:, C_COL + K_LOW_Q] = -1.0 * ((r >= 16) & (r < 24))
    c[:, C_COL + K_LOW_K] = -1.0 * ((r >= 8) & (r < 16))
    c[:, C_COL + K_SHIFT] = r == SHIFT_ROW
    r = p % 8
    for k in range(3):
        c[:, C_COL + K_M0 + k] = r == k
        c[:, C_COL + K_N3 + k] = -1.0 * (r == 3 + k)
    c[:, C_COL + K_M345] = (r >= 3) & (r < 6)
    c[:, C_COL + K_M012] = r < 3
    c[:, C_PRI:C_PRI + 8] = 8 - np.arange(8)
    c[:, C_BASE:C_BASE + 8] = np.arange(8) * 512
    c[:, C_Q:C_Q + P] = np.arange(P)
    c[:, C_P] = p
    return c


def has(b):
    return not isinstance(b, int) or 0 <= b < NB


def upto(eng, sem, per, b, k):
    if isinstance(b, int) and per * b + k <= 0:
        return
    eng.wait_ge(sem, b * per + k)


def drive(eng, body, done):
    for b in (-2, -1, 0, 1):
        body(b, b % 3)
    with eng.Fori(0, 4) as i:
        for k in range(3):
            body(i * 3 + (2 + k), (2 + k) % 3)
    for b in range(14, NB + done):
        body(b, b % 3)


class Link:

    def __init__(self, eng, sem, per, b):
        self.eng, self.sem, self.per, self.b, self.k = eng, sem, per, b, 0

    def __call__(self, *instructions):
        for ins in instructions:
            self.k += 1
            ins.then_inc(self.sem, 1)
        self.eng.wait_ge(self.sem, self.b * self.per + self.k)

    def skip_to(self, k):
        self.k = k
        return self


def semaphores(nc, ctx):
    taken = []

    def clear():
        nc.clear_and_free_semaphores(taken)
        nc.all_engine_barrier()

    def take(name):
        taken.append(nc.alloc_semaphore(name))
        return taken[-1]

    ctx.callback(clear)
    return take


CHORES = (
    [("moments", 0, 0, 2), ("apply", 1, 0, 2), ("OTa", 1, 2, -1), ("post moments", 2, 2, -2),
     ("OTb", 2, 2, -1), ("post apply", 3, 2, -2), ("Qa", 4, 2, 2), ("Ka", 5, 2, 2), ("Qb", 6, 2, 2),
     ("Kb", 7, 2, 2)],
    [("moments", 1, 0, 2), ("OTa", 1, 2, -1), ("apply", 2, 0, 2), ("OTb", 2, 2, -1),
     ("post moments", 3, 2, -2), ("keep", 3, 2, 2), ("Qa", 4, 2, 2), ("Ka", 5, 1, 2), ("Qb", 6, 2, 2),
     ("Kb", 7, 2, 2)],
    [("moments", 0, 0, 2), ("split 0", 0, 0, 1), ("OTa", 0, 1, -1), ("apply", 0, 1, 2), ("Kb", 0, 1, 1),
     ("split 1", 1, 2, 1), ("gates", 1, 2, 2), ("split 2", 2, 1, 1), ("Qa", 3, 1, 2), ("OTb", 4, 2, -1),
     ("Ka", 4, 2, 2), ("log g", 5, 2, 2), ("Qb", 6, 2, 2), ("CS", 7, 0, 2), ("post moments", 7, 0, -1),
     ("post apply", 7, 2, -1)])
SECOND_BANK = ("MXb", "OTb", "YT", "PR", "MXa", "V")
LOG_SLOT = 4
SCHEDULES = (
    [("OTa", 0, 1), ("MXb", 1, 0), ("T", 2, 0), ("OTb", 2, 1), ("Qa", 3, 1), ("YT", 3, 1), ("Ka", 4, 0),
     ("PR", 4, 1), ("Qb", 5, 0), ("MXa", 5, 1), ("Kb", 6, 0), ("V", 7, 0)],
    [("OTa", 0, 1), ("MXb", 1, 0), ("T", 2, 1), ("OTb", 2, 1), ("Qa", 3, 0), ("YT", 3, 1), ("Ka", 4, 1),
     ("PR", 4, 1), ("Qb", 5, 1), ("MXa", 5, 1), ("Kb", 6, 1), ("V", 7, 0)],
    [("OTa", 0, 0), ("T", 2, 0), ("V", 3, 0), ("Qa", 3, 1), ("Ka", 5, 0), ("OTb", 5, 1), ("Qb", 7, 0),
     ("CS", 7, 1), ("Kb", 7, 1)])


def attention_layer(nc, kind, X, XB, cst, cstb, Kz, Vx, w):
    soft = kind < 2
    lag = 1 if soft else 3
    done = 2 if soft else 1
    NU = H // 2
    NS = 2 * NU if soft else NU
    NPT = 6
    WU = 2 * S * 2 if soft else 2 * S + 2 * P
    LINKS_LN = 9 if kind == 1 else 4
    with ExitStack() as ctx:
        take = semaphores(nc, ctx)

        def sb(name, shape, dt):
            return ctx.enter_context(nc.sbuf_tensor(f"{name}{kind}", shape, dt))

        def pb(name, shape, dt):
            return ctx.enter_context(nc.psum_tensor(f"{name}{kind}", shape, dt))

        def sem(name):
            return take(f"{name}{kind}")

        if soft:
            score_ps = pb("score", [P, 2, 512], F32)
            st_ps = pb("st", [P, 3, 512], F32)
        else:
            turn_ps = pb("turn", [P, 3, 1024], F32)
        pv_ps = pb("pv", [P, 512], F32)
        misc = pb("misc", [P, 2 if soft else 1, 512], F32)

        pad = sb("pad", [1, 1], F32)
        stats = sb("stats", [P, TC, 6], F32)
        mv = sb("mv", [P, TC, 2], F32)
        ve = sb("ve", [P, 2, TC], F32)
        rs = sb("rs", [P, 2, TC], F32)
        half = sb("half", [P, 2, TC], F32)
        pstats = sb("pstats", [P, TC, 6], F32)
        pmv = sb("pmv", [P, TC, 2], F32)
        pve = sb("pve", [P, TC], F32)
        prs = sb("prs", [P, TC], F32)
        y = sb("y", [P, TC, D], F32)
        yT = sb("yT", [P, S], F32)
        xq = sb("xq", [P, 2, 2, S], F32)
        hi = sb("hi", [P, 2, 2, S], F16)
        Kp = sb("Kp", [P, NG, S], F16)
        Qp = sb("Qp", [P, 3, NG, S], F16)
        PT = sb("PT", [P, NPT, 2 * S] if soft else [P, 3, WU], F32)
        OS = sb("OS", [P, 2, 2, S], F32)
        rc = sb("rc", [P, TC, 8], F32)
        yn = sb("yn", [P, TC, D], F32)
        ynT = sb("ynT", [P, S], F32)
        ob = sb("ob", [P, TC, D], F32)
        tmp = sb("tmp", [P, TC, D], F32)
        if kind == 1:
            tmp2 = sb("tmp2", [P, 2, TC], F32)
            rs2 = sb("rs2", [P, TC], F32)
        if soft:
            mxs = sb("mxs", [P, 2, TC, 8], F32)
            nm = sb("nm", [8, 2, S], F16)
        else:
            rr = sb("rr", [P, 3, WU], F32)
            tt = sb("tt", [P, 3, WU], F32)
            uu = sb("uu", [P, 3, WU], F32)
            gl = sb("gl", [P, TC, H], F32)
            ga = sb("ga", [P, TC, H], F32)
            gm = sb("gm", [P, TC, H], F32)
            ge = sb("ge", [P, TC, H], F32)
            lgr = sb("lgr", [P, TC, H, 8], F32)
            LG = sb("LG", [P, S], F32)
            l1 = sb("l1", [P, S], BF16)
            l2 = sb("l2", [P, S], BF16)
            l3 = sb("l3", [P, S], BF16)
            lrem = sb("lrem", [P, 2, S], F32)
            Mt = sb("Mt", [P, 2, S], BF16)
            Ms = sb("Ms", [P, 3, 2, S], BF16)
            Mz = sb("Mz", [P, 3, H, S], BF16)

        schedule = SCHEDULES[kind]
        steps = [n for n, _, _ in schedule]
        second_bank = SECOND_BANK if soft else ()
        offset = dict(MXb=0, OTa=-1, T=2, OTb=-1, Qa=2, YT=-1, Ka=2, PR=-1, Qb=2, Kb=2, MXa=1, V=2, CS=2)
        full = {n: sem(f"full_{n}") for n in steps}
        free = {n: sem(f"free_{n}") for n in steps}
        s_init = sem("s_init")
        s_ve = sem("s_ve")
        s_rs = sem("s_rs")
        s_y = sem("s_y")
        s_hi = sem("s_hi")
        s_pack = sem("s_pack")
        s_kz = [sem(f"s_kz{a}") for a in range(2)]
        s_S = sem("s_S")
        s_max = sem("s_max")
        s_sh = [sem(f"s_sh{a}") for a in range(2)]
        s_st = sem("s_st")
        s_exp = sem("s_exp")
        s_pv = sem("s_pv")
        s_os = sem("s_os")
        s_ln = sem("s_ln")
        s_lp = sem("s_lp")
        s_lo = sem("s_lo")
        s_pve = sem("s_pve")
        s_prs = sem("s_prs")
        s_post = sem("s_post")
        if not soft:
            s_dexp = sem("s_dexp")
            s_t = sem("s_t")
            s_u = sem("s_u")
            s_sqd = sem("s_sqd")
            s_sqp = sem("s_sqp")
            s_gl = sem("s_gl")
            s_ga = sem("s_ga")
            s_ge = sem("s_ge")
            s_gd = sem("s_gd")
            s_lgr = sem("s_lgr")
            s_lm = sem("s_lm")
            s_mz = sem("s_mz")

        chores = CHORES[kind]
        slot_of = {n: v for n, v, _, _ in chores}

        def before(name, b):
            at, body = steps.index(name), b
            while True:
                at -= 1
                if at < 0:
                    at, body = at + len(steps), body - 1
                if isinstance(body, int) and body < -2:
                    return None
                if (steps[at] in second_bank) == (name in second_bank) and has(body + offset[steps[at]]):
                    return steps[at], body + offset[steps[at]]

        def bank(name):
            return misc[:, int(name in second_bank), :]

        def turn(slot, u, k):
            return turn_ps[:, (2 * NU * slot + 2 * u + k) % 3, 0:WU]

        def due(u, place, b):
            return [(n, b + offset[n]) for n, v, p in schedule if (v, p) == (u, place) and has(b + offset[n])]

        BY_DVE = (4,)

        def squared(eng, b, u):
            if soft:
                upto(eng, s_exp, NS, b, 2 * u + 2)
            elif u in BY_DVE:
                upto(eng, s_sqd, len(BY_DVE), b, sum(v <= u for v in BY_DVE))
            else:
                upto(eng, s_sqp, NU - len(BY_DVE), b, sum(v not in BY_DVE for v in range(u + 1)))

        def third(slot, u):
            return (NU * slot + u) % 3

        def squares(eng, b, slot, u):
            u, b, slot = (u - 1, b, slot) if u >= 1 else (NU - 1, b - 1, slot + 2)
            at = third(slot, u)
            by_dve = u in BY_DVE
            if has(b) and by_dve == (eng is nc.vector):
                upto(eng, s_u, NU, b, u + 1)
                upto(eng, s_pv, NU, b, u - 2)
                eng.tensor_tensor(PT[:, at, :], uu[:, at, :], uu[:, at, :], ALU.mult)\
                   .then_inc(s_sqd if by_dve else s_sqp, 1)

        block = ctx.enter_context(nc.Block())

        @block.sync
        def _(sp):
            def shift(b, slot, a):
                upto(sp, free["MXb" if a else "MXa"], 1, b, 1)
                sp.dma_start(Qp[SHIFT_ROW:P:32, slot, 2 * a:2 * a + 2, :],
                             nm[:, a, :]).then_inc(s_sh[a], 16)

            def spread_keys(b, slot, a):
                g = slice(2 * a, 2 * a + 2) if soft else slice(0, NG)
                upto(sp, s_pack, 4, b, 2 * a + 2 if soft else 4)
                upto(sp, s_st, NS, b - 3, NS)
                for j in range(NJ):
                    sp.dma_start(Kz[32 * j:32 * j + 32, slot, g, j, :],
                                 Kp[32 * j:32 * j + 32, g, :]).then_inc(s_kz[a], 16)

            def body(b, slot):
                nxt = (slot + 2) % 3
                if not soft:
                    if has(b + 1):
                        spread_keys(b + 1, (slot + 1) % 3, 0)
                        upto(sp, s_lm, 10, b + 1, 10)
                        sp.wait_ge(s_init, 2)
                        for h in range(H):
                            sp.dma_start(Mz[8 * h:8 * h + 8, (slot + 1) % 3, h, :],
                                         Mt[8 * h:8 * h + 8, 1, :]).then_inc(s_mz, 16)
                    return
                if has(b):
                    shift(b, slot, 1)
                if has(b + 2):
                    spread_keys(b + 2, nxt, 0)
                if has(b + 1):
                    shift(b + 1, (slot + 1) % 3, 0)
                if has(b + 2):
                    spread_keys(b + 2, nxt, 1)

            drive(sp, body, done)

        @block.gpsimd
        def _(pool):
            pool.memset(half[:], -0.5).then_inc(s_init, 1)
            if not soft:
                pool.memset(Mz[:].rearrange("p a h s -> p (a h s)").bitcast(F32), 0.0).then_inc(s_init, 1)
            pool.wait_ge(s_init, 1)

            def body(b, slot):
                for u in range(NU):
                    if u == slot_of["moments"] and has(b + 2):
                        upto(pool, s_ve, 1, b + 2, 1)
                        k = 2 if kind == 1 else 1
                        pool.tensor_tensor(rs[:, 0:k, :], ve[:, 0:k, :], half[:, 0:k, :], ALU.pow).then_inc(s_rs, 1)
                    if not soft:
                        squares(pool, b, slot, u)
                    if u == slot_of["post moments"] and kind != 1 and has(b - done):
                        upto(pool, s_pve, 1, b - done, 1)
                        pool.tensor_tensor(prs[:], pve[:], half[:, 0, :], ALU.pow).then_inc(s_prs, 1)

            drive(pool, body, done)

        @block.scalar
        def _(act):
            def consume(name, b, slot):
                if name in ("OTa", "OTb", "CS"):
                    return
                upto(act, full[name], 1, b, 1)
                ps = bank(name)
                if name in ("MXa", "MXb"):
                    a = int(name == "MXb")
                    upto(act, s_sh[a], 16, b - 1, 16)
                    act.activation(nm[:, a, :], ps[0:8, 0:S], ACT.Copy, scale=-1.0).then_inc(free[name], 1)
                elif name == "T":
                    upto(act, full["V"], 1, b - 1, 1)
                    act.activation(yT[:], ps[:, 0:S], ACT.Copy).then_inc(free[name], 1)
                elif name in ("Qa", "Ka", "Qb", "Kb"):
                    project(b, ["Qa", "Ka", "Qb", "Kb"].index(name), name, ps)
                elif name == "YT":
                    upto(act, full["PR"], 1, b - 1, 1)
                    act.activation(ynT[:], ps[:, 0:S], ACT.Copy).then_inc(free[name], 1)
                elif name == "PR":
                    upto(act, s_post, 1, b - 1, 1)
                    act.activation(ob[:].rearrange("p c d -> p (c d)"), ps[:, 0:S], ACT.Copy)\
                       .then_inc(free[name], 1)
                elif name == "V":
                    upto(act, s_pv, NU, b - 3, NU)
                    wide = ps.rearrange("p (c s) -> p c s", c=TC)
                    if not soft:
                        upto(act, s_ga, 2, b - 1, 2)
                        act.activation(gl[:], wide[:, :, D:D + H], ACT.Copy).then_inc(s_gl, 1)
                    act.activation(Vx[:, slot, :, :, 0:DH],
                                   wide[:, :, 0:D].rearrange("p c (h d) -> p c h d", d=DH), ACT.Copy)\
                       .then_inc(free[name], 1)

            def project(b, n, name, ps):
                upto(act, s_pack, 4, b, n - 1)
                flat = xq[:, n % 2, :, :].rearrange("p a s -> p (a s)")
                if kind == 0:
                    bias = w["bq"] if n % 2 == 0 else w["bk"]
                    for k in range(2):
                        last = act.activation(xq[:, n % 2, k, :], ps[:, k * S:(k + 1) * S], ACT.Identity,
                                              bias=bias[:, n // 2 * 2 + k:n // 2 * 2 + k + 1])
                elif n % 2 == 0 or not soft:
                    last = act.activation(flat, ps, ACT.Copy)
                else:
                    last = act.activation(flat, ps, ACT.Identity, bias=cst[:, C_COL + K_SHIFT:C_COL + K_SHIFT + 1])
                last.then_inc(free[name], 1)
                upto(act, free[name], 1, b, 1)
                act.activation(hi[:, n % 2, :, :].rearrange("p a s -> p (a s)"), flat, ACT.Copy).then_inc(s_hi, 1)

            def sums(b, a):
                upto(act, s_pv, NU, b, 4 * a + 4)
                upto(act, full["OTb" if a else "OTa"], 1, b - 1, 1)
                act.activation(OS[:, a, :, :].rearrange("p a s -> p (a s)"), pv_ps[:], ACT.Copy).then_inc(s_os, 1)

            def body(b, slot):
                for u in range(NU):
                    if u == lag and has(b - 1):
                        sums(b - 1, 1)
                    if u == 4 + lag and has(b):
                        sums(b, 0)
                    for name, batch in due(u, 0, b):
                        consume(name, batch, (slot + offset[name]) % 3)
                    if soft and has(b):
                        for c in range(TC):
                            v = 2 * u + c
                            at = 2 * NU * slot + v
                            upto(act, s_st, NS, b, v + 1)
                            upto(act, s_pv, NU, b, u - 2)
                            act.activation(PT[:, at % NPT, :], st_ps[:, at % 3, :], ACT.Exp, scale=SCALE)\
                               .then_inc(s_exp, 1)
                    if not soft and has(b):
                        upto(act, s_S, NU, b, u + 1)
                        upto(act, s_u, NU, b, u - 2)
                        act.activation(rr[:, third(slot, u), :], turn(slot, u, 0), ACT.Exp, scale=0.5).then_inc(s_dexp, 1)
                        upto(act, s_st, NS, b, u + 1)
                        upto(act, s_u, NU, b, u - 2)
                        act.activation(tt[:, third(slot, u), :], turn(slot, u, 1), ACT.Abs).then_inc(s_t, 1)
                    if not soft and u == LOG_SLOT and has(b + 2):
                        upto(act, s_ga, 2, b + 2, 2)
                        upto(act, s_lgr, 1, b + 1, 1)
                        act.activation(ge[:], ga[:], ACT.Exp, scale=-1.0).then_inc(s_ge, 1)
                        upto(act, s_ge, 2, b + 2, 1)
                        act.activation(ge[:], ge[:], ACT.Ln, bias=1.0).then_inc(s_ge, 1)
                    for name, batch in due(u, 1, b):
                        consume(name, batch, (slot + offset[name]) % 3)

            if not soft:
                act.preload_act_table_set("natural_log_exp_and_others")
            drive(act, body, done)

        @block.vector
        def _(dve):
            def pack(b, slot, n):
                a, is_k = n // 2, n % 2
                upto(dve, s_hi, 4, b, n + 1)
                mask = cst[:, C_COL + (K_LOW_K if is_k else K_LOW_Q):][:, 0:1]
                if is_k:
                    upto(dve, s_kz[a if soft else 0], 64, b - 1, 64)
                    dst = Kp[:, 2 * a:2 * a + 2, :]
                else:
                    upto(dve, s_st, NS, b - 3, NS)
                    dst = Qp[:, slot, 2 * a:2 * a + 2, :]
                dve.scalar_tensor_tensor(dst, hi[:, n % 2, :, :], mask, xq[:, n % 2, :, :], ALU.mult, ALU.add)\
                   .then_inc(s_pack, 1)

            def ln_stats(b):
                lk = Link(dve, s_ln, LINKS_LN, b)
                lk(*[dve.bn_stats(stats[:, c, :], X[:, ds(b * TC + c, 1), :].rearrange("p a d -> p (a d)"))
                     for c in range(TC)])
                dve.memset(pad[:], 0.0)
                lk(*[dve.bn_aggr(mv[:, c, :], stats[:, c, :]) for c in range(TC)])
                dve.tensor_scalar(ve[:, 0, :], mv[:, :, 1], EPS_LN, None, ALU.add)\
                   .then_inc(s_ln if kind == 1 else s_ve, 1)
                if kind == 1:
                    lk.k += 1
                    upto(dve, s_ln, LINKS_LN, b, lk.k)
                    lk(dve.reciprocal(tmp2[:, 0, :], ve[:, 0, :]))
                    lk(dve.tensor_tensor(tmp2[:, 1, :], tmp2[:, 0, :], mv[:, :, 1], ALU.mult))
                    dve.tensor_scalar(ve[:, 1, :], tmp2[:, 1, :], EPS_RMS, None, ALU.add).then_inc(s_ve, 1)

            def ln_apply(b):
                rows = [X[:, ds(b * TC + c, 1), :].rearrange("p a d -> p (a d)") for c in range(TC)]
                upto(dve, s_rs, 1, b, 1)
                upto(dve, full["T"], 1, b - 1, 1)
                scale = rs[:, 0, :]
                if kind == 1:
                    lk = Link(dve, s_ln, LINKS_LN, b).skip_to(7)
                    lk(dve.tensor_tensor(rs2[:], rs[:, 0, :], rs[:, 1, :], ALU.mult))
                    scale = rs2[:]
                for c in range(TC):
                    last = dve.tensor_scalar(y[:, c, :], rows[c], mv[:, c, 0:1], scale[:, c:c + 1],
                                             ALU.subtract, ALU.mult)
                last.then_inc(s_y, 1)

            def keep_y(b):
                rows = [X[:, ds(b * TC + c, 1), :].rearrange("p a d -> p (a d)") for c in range(TC)]
                if kind == 1:
                    for c in range(TC):
                        last = dve.tensor_scalar(XB[:, ds(b * TC + c, 1), :].rearrange("p a d -> p (a d)"), rows[c],
                                                 mv[:, c, 0:1], rs[:, 0, c:c + 1], ALU.subtract, ALU.mult)
                    last.then_inc(s_ln, 1)

            def normalize(b, a):
                name = "OTa" if a == 0 else "OTb"
                upto(dve, full[name], 1, b, 1)
                if a == 0:
                    if soft:
                        upto(dve, full["YT"], 1, b - 1, 1)
                upto(dve, free["OTb" if a == 0 else "OTa"], 1, b - 1 if a == 0 else b, 1)
                v = bank(name).rearrange("p (c k r) -> p c k r", c=TC, r=32)
                dve.reciprocal(rc[:], v[:, :, :, DH]).then_inc(s_lo, 1)
                upto(dve, s_lo, 2, b, a + 1)
                dve.tensor_tensor(yn[:, :, 64 * a:64 * a + 64].rearrange("p c (k r) -> p c k r", r=DH),
                                  v[:, :, :, 0:DH], rc[:].unsqueeze(3).to_broadcast([P, TC, 8, DH]),
                                  ALU.mult).then_inc(free[name], 1)

            src = ob if soft else yn

            def post_stats(b):
                upto(dve, free["PR" if soft else "OTb"], 1, b, 1)
                if kind == 1:
                    upto(dve, s_ln, LINKS_LN, b, LINKS_LN)
                    xt = XB[:, ds(b * TC, TC), :]
                    dve.tensor_tensor(xt, xt, src[:], ALU.add).then_inc(s_post, 1)
                    return
                lk = Link(dve, s_lp, 6, b)
                lk(*[dve.bn_stats(pstats[:, c, :], src[:, c, :]) for c in range(TC)])
                dve.memset(pad[:], 0.0)
                lk(*[dve.bn_aggr(pmv[:, c, :], pstats[:, c, :]) for c in range(TC)])
                dve.tensor_scalar(pve[:], pmv[:, :, 1], EPS_LN, None, ALU.add).then_inc(s_pve, 1)

            def post_apply(b):
                lk = Link(dve, s_lp, 6, b).skip_to(4)
                upto(dve, s_prs, 1, b, 1)
                lk(*[dve.tensor_scalar(tmp[:, c, :], src[:, c, :], pmv[:, c, 0:1], prs[:, c:c + 1],
                                       ALU.subtract, ALU.mult) for c in range(TC)])
                xt = X[:, ds(b * TC, TC), :]
                dve.tensor_tensor(xt, xt, tmp[:], ALU.add).then_inc(s_post, 1)

            def chore(name, b, slot):
                if name == "moments":
                    ln_stats(b)
                elif name == "apply":
                    ln_apply(b)
                elif name == "keep":
                    keep_y(b)
                elif name in ("OTa", "OTb"):
                    normalize(b, int(name == "OTb"))
                elif name == "post moments":
                    post_stats(b)
                elif name == "post apply":
                    post_apply(b)
                elif name == "gates":
                    upto(dve, s_gl, 1, b, 1)
                    upto(dve, s_lgr, 1, b - 1, 1)
                    dve.scalar_tensor_tensor(ga[:], gl[:], -1.0, gl[:], ALU.mult, ALU.max).then_inc(s_ga, 1)
                    dve.tensor_scalar(gm[:], gl[:], 0.0, None, ALU.min).then_inc(s_ga, 1)
                elif name == "log g":
                    upto(dve, s_ge, 2, b, 2)
                    upto(dve, full["CS"], 1, b - 1, 1)
                    dve.tensor_tensor(lgr[:], gm[:].unsqueeze(3).to_broadcast([P, TC, H, 8]),
                                      ge[:].unsqueeze(3).to_broadcast([P, TC, H, 8]), ALU.subtract)\
                       .then_inc(s_lgr, 1)
                elif name == "CS":
                    upto(dve, full["CS"], 1, b, 1)
                    upto(dve, s_lm, 10, b - 1, 10)
                    dve.tensor_copy(LG[:], bank("CS")[:, 0:S]).then_inc(free["CS"], 1)
                elif name.startswith("split"):
                    cum_split(b, slot, int(name[-1]))
                else:
                    pack(b, slot, ["Qa", "Ka", "Qb", "Kb"].index(name))

            def do_chores(u, place, b, slot):
                for name, v, p, of in chores:
                    if (v, p) == (u, place) and has(b + of):
                        chore(name, b + of, (slot + of) % 3)

            def body_softmax(b, slot):
                for u in range(NU):
                    for c in range(TC):
                        do_chores(u, c, b, slot)
                        if has(b + 1):
                            upto(dve, s_S, 2 * NU, b + 1, 2 * u + c + 1)
                            if u in (0, 4) and c == 0:
                                upto(dve, full["MXa" if u == 0 else "MXb"], 1, b, 1)
                            j = 2 * (u % 2)
                            g2 = u // 2 % 2
                            dve.tensor_reduce(mxs[:, u // 4, c, 2 * j + g2:2 * j + g2 + 3:2],
                                              score_ps[:, c, :].rearrange("p (h s) -> p h s", h=2),
                                              AX.X, ALU.max).then_inc(s_max, 1)
                    do_chores(u, TC, b, slot)

            def body_power(b, slot):
                for u in range(NU):
                    do_chores(u, 0, b, slot)
                    squares(dve, b, slot, u)
                    do_chores(u, 1, b, slot)
                    if has(b):
                        upto(dve, s_dexp, NU, b, u + 1)
                        upto(dve, s_t, NU, b, u + 1)
                        at = third(slot, u)
                        if u >= 3:
                            squared(dve, b, u - 3)
                        elif has(b - 1):
                            squared(dve, b - 1, u + NU - 3)
                        dve.scalar_tensor_tensor(uu[:, at, :], tt[:, at, :], EPS_POW, rr[:, at, :],
                                                 ALU.add, ALU.mult).then_inc(s_u, 1)
                    do_chores(u, 2, b, slot)

            def cum_split(b, slot, third):
                col = lambda k: cst[:, C_COL + k:C_COL + k + 1]
                if third == 0:
                    lk = Link(dve, s_lm, 10, b)
                    upto(dve, free["CS"], 1, b, 1)
                    lk(dve.tensor_copy(l1[:], LG[:]))
                    lk(dve.tensor_tensor(lrem[:, 0, :], LG[:], l1[:], ALU.subtract))
                    lk(dve.tensor_copy(l2[:], lrem[:, 0, :]))
                elif third == 1:
                    lk = Link(dve, s_lm, 10, b).skip_to(3)
                    upto(dve, s_mz, 256, b - 1, 256)
                    lk(dve.tensor_tensor(l3[:], lrem[:, 0, :], l2[:], ALU.subtract),
                       dve.tensor_scalar(Mt[:, 0, :], l1[:], col(K_M0), col(K_M345), ALU.mult, ALU.add),
                       dve.tensor_scalar(Ms[:, slot, 0, :], l1[:], col(K_N3), col(K_M012), ALU.mult, ALU.add))
                else:
                    lk = Link(dve, s_lm, 10, b).skip_to(6)
                    lk(dve.scalar_tensor_tensor(lrem[:, 0, :], l2[:], col(K_M1), Mt[:, 0, :],
                                                ALU.mult, ALU.add),
                       dve.scalar_tensor_tensor(lrem[:, 1, :], l2[:], col(K_N4), Ms[:, slot, 0, :],
                                                ALU.mult, ALU.add))
                    lk(dve.scalar_tensor_tensor(Mt[:, 1, :], l3[:], col(K_M2), lrem[:, 0, :],
                                                ALU.mult, ALU.add),
                       dve.scalar_tensor_tensor(Ms[:, slot, 1, :], l3[:], col(K_N5), lrem[:, 1, :],
                                                ALU.mult, ALU.add))

            drive(dve, body_softmax if soft else body_power, done)

        @block.tensor
        def _(pe):
            ident = cst[:, C_IDENT:C_IDENT + P]

            def open_bank(name, b):
                at = before(name, b)
                if at is not None:
                    upto(pe, free[at[0]], 1, at[1], 1)

            def transposes(b):
                open_bank("T", b)
                upto(pe, s_y, 1, b + 2, 1)
                for c in range(TC):
                    last = pe.transpose(bank("T")[:, c * P:(c + 1) * P], y[:, c, :], ident)
                last.then_inc(full["T"], 1)

            def project(b, n):
                name = ["Qa", "Ka", "Qb", "Kb"][n]
                open_bank(name, b)
                upto(pe, free["T"], 1, b + 2, 1)
                wt = w["wq"] if n % 2 == 0 else w["wk"]
                for k in range(2):
                    g = n // 2 * 2 + k
                    last = pe.matmul(bank(name)[:, k * S:(k + 1) * S], wt[:, g, :], yT[:], start=True, stop=True)
                last.then_inc(full[name], 1)

            def values(b):
                open_bank("V", b)
                n = D if soft else D + H
                for c in range(TC):
                    out = bank("V")[:, c * S:c * S + n]
                    last = pe.matmul(out, yT[:, c * P:(c + 1) * P], w["wv"][:, 0:n], start=True, stop=kind != 0)
                    if kind == 0:
                        last = pe.matmul(out, cst[0:1, C_TRI + P:C_TRI + 2 * P], w["bv"][0:1, :],
                                         start=False, stop=True)
                last.then_inc(full["V"], 1)

            def shift_rows(b, batch, a):
                name = "MXb" if a else "MXa"
                open_bank(name, b)
                upto(pe, s_max, 2 * NU, batch, NU * (a + 1))
                for c in range(TC):
                    last = pe.transpose(bank(name)[0:8, c * P:(c + 1) * P], mxs[:, a, c, :], ident)
                last.then_inc(full[name], 1)

            def turn_out(b, a):
                name = "OTb" if a else "OTa"
                open_bank(name, b)
                upto(pe, s_os, 2, b - 1, a + 1)
                for c in range(TC):
                    for k in range(2):
                        o = (c * 2 + k) * P
                        last = pe.transpose(bank(name)[:, o:o + P], OS[:, a, k, c * P:(c + 1) * P], ident)
                last.then_inc(full[name], 1)

            def out_turn(b):
                open_bank("YT", b)
                upto(pe, free["OTb"], 1, b - 1, 1)
                for c in range(TC):
                    last = pe.transpose(bank("YT")[:, c * P:(c + 1) * P], yn[:, c, :], ident)
                last.then_inc(full["YT"], 1)

            def out_project(b):
                open_bank("PR", b)
                upto(pe, free["YT"], 1, b - 1, 1)
                for c in range(TC):
                    out = bank("PR")[:, c * D:(c + 1) * D]
                    last = pe.matmul(out, ynT[:, c * P:(c + 1) * P], w["wo"][:, :], start=True, stop=kind != 0)
                    if kind == 0:
                        last = pe.matmul(out, cst[0:1, C_TRI + P:C_TRI + 2 * P], w["bo"][0:1, :],
                                         start=False, stop=True)
                last.then_inc(full["PR"], 1)

            def scores(b, slot, u):
                g, j = u // 2, 2 * (u % 2)
                if u in (0, 4):
                    upto(pe, s_kz[u // 4], 64, b, 64)
                    upto(pe, s_pack, 4, b, 2 * (u // 4) + 1)
                for c in range(TC):
                    upto(pe, s_max, 2 * NU, b, 2 * u + c - 1)
                    pe.matmul(score_ps[:, c, :], Qp[:, slot, g, c * P:(c + 1) * P],
                              Kz[:, slot, g, j:j + 2, :].rearrange("p j s -> p (j s)"),
                              start=True, stop=True).then_inc(s_S, 1)

            def key_scores(b, slot, u):
                g, j = u // 2, 2 * (u % 2)
                if soft:
                    if u in (0, 4):
                        upto(pe, s_sh[u // 4], 16, b, 16)
                else:
                    if u == 0:
                        upto(pe, s_kz[0], 64, b, 64)
                        upto(pe, s_pack, 4, b, 4)
                    upto(pe, s_dexp, NU, b, u)
                for c in range(TC):
                    at = 2 * NU * slot + 2 * u + c
                    if soft:
                        upto(pe, s_exp, NS, b, 2 * u + c - 2)
                    for k in range(2):
                        key = Kz[:, slot, g, j + k, c * P:(c + 1) * P]
                        n = S if soft else S - P * c
                        o = S * k if soft else 2 * S * c + n * k
                        out = st_ps[:, at % 3, o:o + n] if soft else turn(slot, u, 1)[:, o:o + n]
                        last = pe.matmul(out, key, Qp[:, slot, g, S - n:S], start=True, stop=True)
                    if soft or c == TC - 1:
                        last.then_inc(s_st, 1)

            def decays(b, slot, u):
                if u == 0:
                    upto(pe, s_mz, 256, b, 256)
                    upto(pe, s_lm, 10, b, 10)
                upto(pe, s_t, NU, b, u - 1)
                for c in range(TC):
                    n = S - P * c
                    for k in range(2):
                        o = 2 * S * c + n * k
                        pe.matmul(turn(slot, u, 0)[:, o:o + n], Ms[:, slot, 1, c * P:(c + 1) * P],
                                  Mz[:, slot, 2 * u + k, S - n:S], start=True, stop=False)
                        last = pe.matmul(turn(slot, u, 0)[:, o:o + P], cstb[:, 0:P], cstb[:, P:2 * P],
                                         start=False, stop=True)
                last.then_inc(s_S, 1)

            def times_v(b, slot, u):
                g, j = u // 2, 2 * (u % 2)
                squared(pe, b, u)
                if u in (0, 4):
                    upto(pe, s_os, 2, b, u // 4)
                if u == 0:
                    upto(pe, free["V"], 1, b, 1)
                for k in range(2):
                    h = 2 * u + k
                    for c in range(TC):
                        n = S if soft else S - P * c
                        p = (PT[:, (2 * NU * slot + 2 * u + c) % NPT, S * k:S * k + S] if soft
                             else PT[:, third(slot, u), 2 * S * c + n * k:2 * S * c + n * k + n])
                        q = g % 2 * S + S
                        last = pe.matmul(pv_ps[32 * (j + k):32 * (j + k) + 32, q - n:q], Vx[:, slot, c, h, :],
                                         p, start=(c == 0), stop=(c == TC - 1),
                                         skip_group_check=True)
                last.then_inc(s_pv, 1)

            def step(name, b):
                if name == "T":
                    transposes(b)
                elif name in ("Qa", "Ka", "Qb", "Kb"):
                    project(b, ["Qa", "Ka", "Qb", "Kb"].index(name))
                elif name == "V":
                    values(b)
                elif name in ("MXa", "MXb"):
                    shift_rows(b, b + offset[name], int(name == "MXb"))
                elif name in ("OTa", "OTb"):
                    turn_out(b, int(name == "OTb"))
                elif name == "YT":
                    out_turn(b)
                elif name == "PR":
                    out_project(b)
                else:
                    cumulate(b)

            def body(b, slot):
                for u in range(NU):
                    if soft and has(b + 1):
                        scores(b + 1, (slot + 1) % 3, u)
                    for name, _ in due(u, 0, b):
                        step(name, b)
                    if not soft and has(b):
                        decays(b, slot, u)
                    if has(b):
                        key_scores(b, slot, u)
                    for name, _ in due(u, 1, b):
                        step(name, b)
                    if u >= lag and has(b):
                        times_v(b, slot, u - lag)
                    if u < lag and has(b - 1):
                        times_v(b - 1, (slot + 2) % 3, u + NU - lag)

            def cumulate(b):
                open_bank("CS", b)
                upto(pe, s_lgr, 1, b + 2, 1)
                pe.matmul(bank("CS")[:, 0:S], lgr[:, 0, :, :].rearrange("p h r -> p (h r)"),
                          cst[:, C_TRI:C_TRI + S], start=True, stop=False)
                pe.matmul(bank("CS")[:, P:S], lgr[:, 1, :, :].rearrange("p h r -> p (h r)"),
                          cst[:, C_TRI:C_TRI + P], start=False, stop=True).then_inc(full["CS"], 1)

            drive(pe, body, done)


def load_weights(nc, cst, cstb, X, Kz, Vx, w, weights, dram):
    with ExitStack() as ctx:
        take = semaphores(nc, ctx)

        def sem(name):
            return take(name)

        names = ["wq0", "wk0", "wv0", "wo0", "wq2", "wk2", "wv2"]
        rows = ctx.enter_context(nc.sbuf_tensor("rows", [P, len(names), D], F32))
        gates = ctx.enter_context(nc.sbuf_tensor("gates", [H + NE, D], F32))
        flat = ctx.enter_context(nc.sbuf_tensor("flat", [P, 3, D], F32))
        norm = ctx.enter_context(nc.sbuf_tensor("norm", [P, 2], F32))
        route0 = ctx.enter_context(nc.sbuf_tensor("route0", [P, NE], F32))
        bias = ctx.enter_context(nc.sbuf_tensor("bias", [1, 2, D], F32))
        wide = ctx.enter_context(nc.sbuf_tensor("wide", [1, 2, NG, NJ, 4, DH], F32))
        turned = ctx.enter_context(nc.psum_tensor("turned", [P, 8, 512], F32))
        s_rows = sem("s_rows")
        s_flat = sem("s_flat")
        s_bias = sem("s_bias")
        s_x = sem("s_x")
        s_zero = sem("s_zero")
        s_turned = sem("s_turned")
        s_wide = sem("s_wide")
        s_columns = sem("s_columns")
        s_done = sem("s_done")
        block = ctx.enter_context(nc.Block())
        packed = {}
        for n in range(3):
            for name in ("wq", "wk"):
                packed[name, n] = weights[n][name][:].rearrange("p g (j c d) -> p g j c d", j=NJ, c=4)

        def heads(ap):
            return ap.rearrange("p (g j d) -> p g j d", g=NG, j=NJ)

        @block.sync
        def _(sp):
            for k, src in enumerate([dram["L0_attn_Wq"], dram["L0_attn_Wk"], dram["L0_attn_Wv"], dram["L0_attn_Wo"]]):
                sp.dma_start(rows[:, k, :], src).then_inc(s_rows, 16)
            sp.dma_start(rows[:, 4:7, :], dram["L1_attn_W"][0:3 * D, :].rearrange("(a p) d -> p a d", a=3))\
                .then_inc(s_rows, 16)
            sp.dma_start(gates[0:H, :], dram["L1_attn_W"][3 * D:3 * D + H, :]).then_inc(s_rows, 16)
            sp.dma_start(gates[H:H + NE, :], dram["L1_ffn_router_w"]).then_inc(s_rows, 16)
            sp.dma_start(cst[:], dram["constants"]).then_inc(s_rows, 16)
            for k, name in enumerate(["L0_attn_bq", "L0_attn_bk"]):
                sp.dma_start(bias[0:1, k, :], dram[name].rearrange("(a d) -> a d", a=1)).then_inc(s_bias, 16)
            xt = dram["L0_attn_x"].rearrange("b (c p) d -> p (b c) d", p=P)
            for k in range(4):
                sp.dma_start(X[:, 8 * k:8 * k + 8, :], xt[:, 8 * k:8 * k + 8, :]).then_inc(s_x, 16)
            sp.dma_start(weights[0]["bv"][:], dram["L0_attn_bv"].rearrange("(a d) -> a d", a=1)).then_inc(s_flat, 16)
            sp.dma_start(weights[0]["bo"][:], dram["L0_attn_bo"].rearrange("(a d) -> a d", a=1)).then_inc(s_flat, 16)
            for k, name in enumerate(["L0_ffn_wq", "L0_ffn_wk", "L0_ffn_wv"]):
                sp.dma_start(flat[:, k, :], dram[name]).then_inc(s_flat, 16)
            sp.dma_start(weights[1]["wo"][:], dram["L0_ffn_wo"]).then_inc(s_flat, 16)
            sp.dma_start(route0[:], dram["L0_ffn_router_w"]).then_inc(s_flat, 16)
            sp.dma_start(norm[:, 1:2], dram["L0_ffn_norm2_w"].rearrange("(d a) -> d a", a=1)).then_inc(s_flat, 16)
            sp.dma_start(norm[:, 0:1], dram["L0_ffn_norm1_w"].rearrange("(d a) -> d a", a=1)).then_inc(s_flat, 16)
            sp.wait_ge(s_x, 64)

        @block.gpsimd
        def _(pool):
            for n in range(3):
                for name in ("wq", "wk"):
                    pool.memset(packed[name, n][:, :, :, 3, :], 0.0).then_inc(s_zero, 1)
            pool.memset(wide[:], 0.0).then_inc(s_zero, 1)
            pool.wait_ge(s_zero, 7)
            pool.memset(wide[:, 1, :, :, 3, 0:1], 1.0).then_inc(s_zero, 1)
            pool.memset(Vx[:], 0.0).then_inc(s_zero, 1)
            pool.memset(Kz[:].rearrange("p a g j s -> p (a g j s)").bitcast(F32), 0.0).then_inc(s_zero, 1)
            pool.wait_ge(s_zero, 9)
            pool.memset(Vx[:, :, :, :, DH:DH + 1], 1.0).then_inc(s_zero, 1)

        @block.tensor
        def _(pe):
            pe.wait_ge(s_rows, 128)
            for k in range(len(names)):
                pe.transpose(turned[:, k, 0:P], rows[:, k, :], cst[:, 0:P]).then_inc(s_turned, 1)
            pe.transpose(turned[:, 7, 0:H + NE], gates[:], cst[0:H + NE, 0:H + NE]).then_inc(s_turned, 1)
            pe.wait_ge(s_wide, 6)
            pe.wait_ge(s_zero, 8)
            pe.wait_ge(s_done, 3)
            for k in range(2):
                for g in range(NG):
                    last = pe.matmul(turned[:, 0, k * NG + g:k * NG + g + 1],
                                     wide[0:1, k, g, :, :, :].rearrange("p j c d -> p (j c d)"),
                                     cst[0:1, C_TRI + P:C_TRI + P + 1], start=True, stop=True)
            last.then_inc(s_columns, 1)

        @block.vector
        def _(dve):
            dve.wait_ge(s_zero, 8)
            dve.wait_ge(s_bias, 32)
            for k in range(2):
                for c in range(3):
                    dve.tensor_copy(wide[:, k, :, :, c, :], heads(bias[0:1, k, :])).then_inc(s_wide, 1)
            for k, dst in enumerate([("wq", 0), ("wk", 0), None, None, ("wq", 2), ("wk", 2)]):
                dve.wait_ge(s_turned, k + 1)
                if dst:
                    for c in range(3):
                        dve.tensor_copy(packed[dst][:, :, :, c, :], heads(turned[:, k, 0:P])).then_inc(s_done, 1)
            dve.tensor_copy(weights[0]["wv"][:], turned[:, 2, 0:P])
            dve.tensor_copy(weights[0]["wo"][:], turned[:, 3, 0:P])
            dve.wait_ge(s_turned, 8)
            dve.tensor_copy(weights[2]["wv"][:, 0:D], turned[:, 6, 0:P])
            dve.tensor_copy(weights[2]["wv"][:, D:D + H], turned[:, 7, 0:H])
            dve.tensor_copy(w["router1"][:], turned[:, 7, H:H + NE])
            dve.wait_ge(s_flat, 9 * 16)
            for k, name in enumerate(("wq", "wk")):
                for c in range(3):
                    dve.tensor_scalar(packed[name, 1][:, :, :, c, :], heads(flat[:, k, :]), norm[:, 0:1],
                                      None, ALU.mult)
            dve.tensor_scalar(weights[1]["wv"][:], flat[:, 2, :], norm[:, 0:1], None, ALU.mult)
            dve.tensor_scalar(w["router0"][:], route0[:], norm[:, 1:2], None, ALU.mult)
            dve.tensor_copy(cstb[:, 0:P], cst[:, C_IDENT:C_IDENT + P])
            dve.tensor_copy(cstb[:, P:2 * P], cst[:, C_LATE:C_LATE + P])
            dve.wait_ge(s_columns, 1)
            dve.tensor_copy(weights[0]["bq"][:], turned[:, 0, 0:NG])
            dve.tensor_copy(weights[0]["bk"][:], turned[:, 0, NG:2 * NG]).then_inc(s_done, 1)
            dve.wait_ge(s_done, 13)


def router_layer(nc, kind, cst, src, yall, yd, hT, logits, router, clear=None, experts=None, dram=None):
    NBLK, TB, T, NY = 8, 4, NTILE, 4
    with ExitStack() as ctx:
        take = semaphores(nc, ctx)

        def sb(name, shape, dt):
            return ctx.enter_context(nc.sbuf_tensor(f"r{name}{kind}", shape, dt))

        def sem(name):
            return take(f"r{name}{kind}")

        stats = sb("stats", [P, T, 6], F32)
        mv = sb("mv", [P, T, 2], F32)
        sq = sb("sq", [P, T], F32)
        ve = sb("ve", [P, T], F32)
        rs = sb("rs", [P, T], F32)
        half = sb("half", [P, T], F32)
        y = sb("y", [P, NY, TB, D], F32)
        yT = sb("yT", [P, 2, TB * P], F32)
        zero = sb("zero", [P, 1024], F32) if clear is not None else None
        turn_ps = ctx.enter_context(nc.psum_tensor(f"rturn{kind}", [P, 2, 512], F32))
        log_ps = ctx.enter_context(nc.psum_tensor(f"rlog{kind}", [P, 2, 512], F32))
        s_half = sem("s_half")
        s_stats = sem("s_stats")
        s_mv = sem("s_mv")
        s_sq = sem("s_sq")
        s_ve = sem("s_ve")
        s_rs = sem("s_rs")
        s_y = sem("s_y")
        s_turn = sem("s_turn")
        s_yT = sem("s_yT")
        s_log = sem("s_log")
        s_logits = sem("s_logits")
        s_keep = sem("s_keep")
        s_yd = [sem(f"s_yd{k}_") for k in range(NY)]
        s_side = sem("s_side")
        s_low = sem("s_low")
        block = ctx.enter_context(nc.Block())

        def tile(t):
            return src[:, t, :]

        @block.vector
        def _(dve):
            def moments(n):
                part = slice(n * TB, (n + 1) * TB)
                for t in range(n * TB, (n + 1) * TB):
                    dve.bn_stats(stats[:, t, :], tile(t)).then_inc(s_stats, 1)
                for t in range(n * TB, (n + 1) * TB):
                    dve.wait_ge(s_stats, t + 1)
                    dve.bn_aggr(mv[:, t, :], stats[:, t, :]).then_inc(s_mv, 1)
                dve.wait_ge(s_mv, (n + 1) * TB)
                if kind == 0:
                    dve.tensor_tensor(sq[:, part], mv[:, part, 0], mv[:, part, 0], ALU.mult).then_inc(s_sq, 1)
                    dve.wait_ge(s_sq, n + 1)
                    dve.scalar_tensor_tensor(ve[:, part], sq[:, part], EPS_RMS, mv[:, part, 1], ALU.add, ALU.add)\
                       .then_inc(s_ve, 1)
                else:
                    dve.tensor_scalar(ve[:, part], mv[:, part, 1], EPS_LN, None, ALU.add).then_inc(s_ve, 1)

            def take_logits(n, k):
                upto(dve, s_log, 1, n, 1)
                dve.tensor_copy(logits[:, n * TB:(n + 1) * TB, :],
                                log_ps[:, k, 0:TB * NE].rearrange("p (c e) -> p c e", e=NE)).then_inc(s_logits, 1)

            def low(n):
                cols = slice(n * TB * P, (n + 1) * TB * P)
                dve.wait_ge(s_yT, n + 1)
                dve.tensor_tensor(hT[:, 1, cols], yT[:, n % 2, :], hT[:, 0, cols], ALU.subtract).then_inc(s_low, 1)

            moments(0)
            for n in range(NBLK):
                if n + 1 < NBLK:
                    moments(n + 1)
                dve.wait_ge(s_rs, n + 1)
                upto(dve, s_turn, 1, n - NY, 1)
                if kind == 1 and n >= NY:
                    dve.wait_ge(s_keep, n - NY + 1)
                    dve.wait_ge(s_yd[n % NY], n // NY * 16)
                for c in range(TB):
                    t = n * TB + c
                    if kind == 0:
                        last = dve.tensor_scalar(y[:, n % NY, c, :], tile(t), rs[:, t:t + 1], None, ALU.mult)
                    else:
                        last = dve.tensor_scalar(y[:, n % NY, c, :], tile(t), mv[:, t, 0:1], rs[:, t:t + 1],
                                                 ALU.subtract, ALU.mult)
                last.then_inc(s_y, 1)
                if n > 0:
                    take_logits(n - 1, (n - 1) % 2)
                    if kind == 0:
                        low(n - 1)
            take_logits(NBLK - 1, 1)
            if kind == 0:
                low(NBLK - 1)
                dve.wait_ge(s_low, NBLK)
            dve.wait_ge(s_logits, NBLK)

        @block.gpsimd
        def _(pool):
            pool.memset(half[:], -0.5).then_inc(s_half, 1)
            if clear is not None:
                pool.memset(zero[:], 0.0).then_inc(s_half, 1)
            pool.wait_ge(s_half, 1)

            def keep(n):
                pool.wait_ge(s_y, n + 1)
                pool.tensor_copy(yall[:, n * TB:(n + 1) * TB, :], y[:, n % NY, :, :]).then_inc(s_keep, 1)

            for n in range(NBLK):
                part = slice(n * TB, (n + 1) * TB)
                pool.wait_ge(s_ve, n + 1)
                pool.tensor_tensor(rs[:, part], ve[:, part], half[:, part], ALU.pow).then_inc(s_rs, 1)
                if kind == 1 and n > 0:
                    keep(n - 1)
            if kind == 1:
                keep(NBLK - 1)

        if kind == 0:
            @block.sync
            def _(sp):
                wg, wu, wd, norm, _ = experts
                sp.dma_start(norm[:], dram["L0_ffn_norm2_w"].rearrange("(d a) -> d a", a=1)).then_inc(s_side, 16)
                sp.dma_start(wg[:, 0:NE, :], dram["L0_ffn_e_gate"].rearrange("e d f -> d e f")).then_inc(s_side, 16)
                sp.dma_start(wg[:, NE, :], dram["L0_ffn_sh_gate"]).then_inc(s_side, 16)
                sp.dma_start(wu[:, 0:NE, :], dram["L0_ffn_e_up"].rearrange("e d f -> d e f")).then_inc(s_side, 16)
                sp.dma_start(wu[:, NE, :], dram["L0_ffn_sh_up"]).then_inc(s_side, 16)
                for e in range(NE):
                    sp.dma_start(wd[:, e, :, :], dram["L0_ffn_e_down"][e].rearrange("(c f) d -> f c d", f=P))\
                        .then_inc(s_side, 16)
                sp.dma_start(wd[:, NE, :, :], dram["L0_ffn_sh_down"].rearrange("(c f) d -> f c d", f=P))\
                  .then_inc(s_side, 16)
                sp.wait_ge(s_side, 14 * 16)

        if kind == 1:
            @block.sync
            def _(sp):
                rows = yd.rearrange("(t p) d -> p t d", p=P)
                sp.wait_ge(s_half, 2)
                span = clear.rearrange("(k p r) d -> k p (r d)", p=P, r=1024 // D)
                for n in range(NBLK):
                    sp.dma_start(span[n], zero[:]).then_inc(s_side, 16)
                    sp.wait_ge(s_y, n + 1)
                    sp.dma_start(rows[:, n * TB:(n + 1) * TB, :], y[:, n % NY, :, :]).then_inc(s_yd[n % NY], 16)
                assert span.shape[0] == NBLK
                sp.wait_ge(s_side, 16 * NBLK)
                for k in range(NY):
                    sp.wait_ge(s_yd[k], 16 * NBLK // NY)

        @block.tensor
        def _(pe):
            ident = cst[:, C_IDENT:C_IDENT + P]

            def score(n):
                k = n % 2
                pe.wait_ge(s_yT, n + 1)
                upto(pe, s_logits, 1, n - 2, 1)
                for c in range(TB):
                    last = pe.matmul(log_ps[:, k, c * NE:(c + 1) * NE], yT[:, k, c * P:(c + 1) * P], router[:],
                                     start=True, stop=True)
                last.then_inc(s_log, 1)

            for n in range(NBLK):
                pe.wait_ge(s_y, n + 1)
                upto(pe, s_yT, 1, n - 2, 1)
                for c in range(TB):
                    last = pe.transpose(turn_ps[:, n % 2, c * P:(c + 1) * P], y[:, n % NY, c, :], ident)
                last.then_inc(s_turn, 1)
                if n > 0:
                    score(n - 1)
            score(NBLK - 1)

        @block.scalar
        def _(act):
            for n in range(NBLK):
                act.wait_ge(s_turn, n + 1)
                upto(act, s_log, 1, n - 2, 1)
                if kind == 0:
                    upto(act, s_low, 1, n - 2, 1)
                    act.activation(hT[:, 0, n * TB * P:(n + 1) * TB * P], turn_ps[:, n % 2, :], ACT.Copy)
                act.activation(yT[:, n % 2, :], turn_ps[:, n % 2, :], ACT.Copy).then_inc(s_yT, 1)


def route(nc, kind, cst, logits, bias_row, comb, idx_in, idx_out, wsel, noop,
          wi=None, wo=None, dram=None, experts=None):
    T = NTILE
    with ExitStack() as ctx:
        take = semaphores(nc, ctx)

        def sb(name, shape, dt=F32):
            return ctx.enter_context(nc.sbuf_tensor(f"t{name}{kind}", shape, dt))

        def sem(name):
            return take(f"t{name}{kind}")

        c8 = [P, T, NE]
        pr = sb("pr", c8)
        p2 = sb("p2", c8)
        sc = sb("sc", c8)
        sel = sb("sel", [P, 2, T, NE])
        m = sb("m", [P, 2, T])
        one = sb("one", [P, T])
        two = sb("two", [P, T])
        s_v = sem("s_v")
        s_a = sem("s_a")
        s_p = sem("s_p")
        s_b = sem("s_b")
        s_w = sem("s_w")
        if kind == 0:
            lift = sb("lift", [P, 1])
        if kind == 1:
            bias8 = sb("bias8", [P, NE])
            bias1 = sb("bias1", [1, NE])
            mask = sb("mask", c8, BF16)
            tri = sb("tri", [P, 2 * P], BF16)
            ranks = sb("ranks", c8)
            totals = sb("totals", [P, NE, T])
            prefix = sb("prefix", [P, NE, T])
            zeros = sb("zeros", [P, T])
            slot = sb("slot", [P, 2, T])
            whole = sb("whole", [P, 2 * T], I32)
            part = sb("part", [P, 2, 2 * T], I32)
            place = sb("place", [P, 2, 2 * T])
            in_row = sb("in_row", [P, 2 * T, P], BF16)
            in_tile = sb("in_tile", [P, 2 * T, NSLOT], BF16)
            found = sb("found", [P, 2 * T, 2, NSLOT], BF16)
            who = sb("who", [P, 2, NSLOT])
            empty = sb("empty", [P, NSLOT])
            late = sb("late", [P, NSLOT])
            number = sb("number", [P, NSLOT])
            to = sb("to", [P, 2, NSLOT])
            ok = sb("ok", [P, T])
            ps = ctx.enter_context(nc.psum_tensor("tps", [P, 4, 512], F32))
        block = ctx.enter_context(nc.Block())
        EXP0, EXP1 = 1, 2

        def wide(ap):
            return ap.unsqueeze(2).to_broadcast(c8)

        def row(at):
            return cst[:, at:at + NE].unsqueeze(1).to_broadcast(c8)

        marks = {}

        @block.vector
        def _(dve):
            lk = Link(dve, s_v, 0, 0)
            lg = logits[:]
            if kind == 1:
                dve.wait_ge(s_p, 1)
                lk(dve.tensor_copy(bias8[:], ps[:, 2, 0:NE]))
                lk(dve.tensor_tensor(lg, lg, bias8[:].unsqueeze(1).to_broadcast(c8), ALU.add))
                lk(dve.memset(zeros[:], 0.0))
                lk(dve.tensor_copy(tri[:], cst[:, C_TRI:C_TRI + 2 * P]))
            lk(dve.tensor_reduce(one[:], lg, AX.X, ALU.max))
            lk(dve.tensor_tensor(pr[:], lg, wide(one[:]), ALU.subtract))
            marks["pr"] = lk.k
            dve.wait_ge(s_a, EXP0)
            lk(dve.tensor_reduce(one[:], pr[:], AX.X, ALU.add))
            lk(dve.reciprocal(two[:], one[:]))
            lk(dve.tensor_tensor(pr[:], pr[:], wide(two[:]), ALU.mult))
            probs = pr
            for c in range(2):
                lk(dve.tensor_reduce(m[:, c, :], probs[:], AX.X, ALU.max))
                lk(dve.tensor_tensor(sc[:], probs[:], wide(m[:, c, :]), ALU.is_equal))
                lk(dve.tensor_tensor(sc[:], sc[:], row(C_PRI), ALU.mult))
                lk(dve.tensor_reduce(one[:], sc[:], AX.X, ALU.max))
                lk(dve.tensor_tensor(sel[:, c, :, :], sc[:], wide(one[:]), ALU.is_equal))
                if c == 0:
                    lk(dve.scalar_tensor_tensor(p2[:].rearrange("p t e -> p (t e)"),
                                                sel[:, 0, :, :].rearrange("p t e -> p (t e)"), -2.0,
                                                pr[:].rearrange("p t e -> p (t e)"), ALU.mult, ALU.add))
                    probs = p2
            if kind == 0:
                lk(dve.tensor_tensor(one[:], m[:, 1, :], m[:, 0, :], ALU.subtract))
                marks["d"] = lk.k
                dve.wait_ge(s_a, EXP1)
                lk(dve.tensor_scalar(two[:], one[:], 1.0, None, ALU.add))
                lk(dve.reciprocal(m[:, 0, :], two[:]))
                lk(dve.tensor_scalar(m[:, 0, :], m[:, 0, :], LIFT ** -2, None, ALU.mult))
                lk(dve.tensor_tensor(m[:, 1, :], one[:], m[:, 0, :], ALU.mult))
                lk(dve.tensor_tensor(sc[:], sel[:, 0, :, :], wide(m[:, 0, :]), ALU.mult))
                lk(dve.tensor_tensor(p2[:], sel[:, 1, :, :], wide(m[:, 1, :]), ALU.mult))
                lk(dve.tensor_tensor(comb[:], sc[:], p2[:], ALU.add))
                return
            for c in range(2):
                lk(dve.tensor_scalar(one[:], m[:, c, :], 0.0, None, ALU.is_gt))
                lk(dve.tensor_tensor(sel[:, c, :, :], sel[:, c, :, :], wide(one[:]), ALU.mult))
            lk(dve.tensor_tensor(mask[:], sel[:, 0, :, :], sel[:, 1, :, :], ALU.add))
            marks["mask"] = lk.k
            dve.wait_ge(s_p, 3)
            lk(dve.tensor_copy(totals[:], ps[:, 1, 0:T * NE].rearrange("p (t e) -> p e t", e=NE)))
            for e in range(NE):
                lk(dve.tensor_tensor_scan(prefix[:, e, :], totals[:, e, :], zeros[:], 0.0, ALU.add, ALU.add))
            lk(dve.tensor_tensor(prefix[:], prefix[:], totals[:], ALU.subtract))
            lk(dve.tensor_tensor(ranks[:], ps[:, 0, 0:T * NE].rearrange("p (t e) -> p t e", e=NE),
                                 prefix[:].rearrange("p e t -> p t e"), ALU.add))
            for c in range(2):
                lk(dve.tensor_tensor(sc[:], sel[:, c, :, :], ranks[:], ALU.mult))
                lk(dve.tensor_reduce(one[:], sc[:], AX.X, ALU.add))
                lk(dve.tensor_tensor(sc[:], sel[:, c, :, :], row(C_BASE), ALU.mult))
                lk(dve.tensor_reduce(two[:], sc[:], AX.X, ALU.add))
                lk(dve.scalar_tensor_tensor(slot[:, c, :], one[:], -1.0, two[:], ALU.add, ALU.add))
                lk(dve.tensor_scalar(ok[:], one[:], float(CAP), None, ALU.is_le))
                lk(dve.scalar_tensor_tensor(ok[:], one[:], 1.0, ok[:], ALU.is_ge, ALU.mult))
                lk(dve.scalar_tensor_tensor(ok[:], two[:], float(CAP * (NE - 1)), ok[:], ALU.is_lt, ALU.mult))
                lk(dve.tensor_tensor(wsel[:, c, :], ok[:], m[:, c, :], ALU.mult))
                lk(dve.tensor_scalar(ok[:], ok[:], -float(BEYOND), float(BEYOND), ALU.mult, ALU.add))
                lk(dve.scalar_tensor_tensor(slot[:, c, :], slot[:, c, :], 0.0, ok[:], ALU.max, ALU.add))
            lk(dve.tensor_copy(whole[:], slot[:].rearrange("p c t -> p (c t)")))
            lk(dve.tensor_scalar(part[:, 0, :], whole[:], 7, None, ALU.logical_shift_right),
               dve.tensor_scalar(part[:, 1, :], whole[:], P - 1, None, ALU.bitwise_and))
            lk(dve.tensor_copy(place[:], part[:]))
            lk(dve.tensor_tensor(in_tile[:], cst[:, C_Q:C_Q + NSLOT].unsqueeze(1).to_broadcast([P, 2 * T, NSLOT]),
                                 place[:, 0, :].unsqueeze(2).to_broadcast([P, 2 * T, NSLOT]), ALU.is_equal))
            lk(dve.tensor_tensor(found[:, :, 0, :], in_tile[:],
                                 cst[:, C_Q + 1:C_Q + 1 + 2 * T].unsqueeze(2).to_broadcast([P, 2 * T, NSLOT]),
                                 ALU.mult),
               dve.tensor_scalar(found[:, :, 1, :], in_tile[:], cst[:, C_P:C_P + 1], None, ALU.mult))
            for n in range(8):
                part8 = slice(n * T // 4, (n + 1) * T // 4)
                lk(dve.tensor_tensor(in_row[:, part8, :], cst[:, C_Q:C_Q + P].unsqueeze(1).to_broadcast([P, T // 4, P]),
                                     place[:, 1, part8].unsqueeze(2).to_broadcast([P, T // 4, P]), ALU.is_equal))
                marks["in_row", n] = lk.k
            lk(dve.tensor_tensor(one[:], sel[:, 0, :, NE - 1], m[:, 0, :], ALU.mult))
            lk(dve.tensor_tensor(two[:], sel[:, 1, :, NE - 1], m[:, 1, :], ALU.mult))
            lk(dve.tensor_tensor(noop[:], one[:], two[:], ALU.add))
            dve.wait_ge(s_p, 4)
            lk(dve.tensor_copy(who[:].rearrange("p a n -> p (a n)"), ps[:, 3, 0:2 * NSLOT]))
            lk(dve.tensor_scalar(empty[:], who[:, 0, :], 0.0, float(BEYOND), ALU.is_equal, ALU.mult),
               dve.tensor_scalar(late[:], who[:, 0, :], T + 0.5, -float(NT), ALU.is_gt, ALU.mult),
               dve.scalar_tensor_tensor(number[:], who[:, 0, :], float(P), who[:, 1, :], ALU.mult, ALU.add))
            lk(dve.scalar_tensor_tensor(to[:, 0, :], number[:], -float(P), empty[:], ALU.add, ALU.add))
            lk(dve.tensor_tensor(to[:, 1, :], to[:, 0, :], late[:], ALU.add))
            lk(dve.tensor_copy(idx_out[:], to[:, 0, :]), dve.tensor_copy(idx_in[:], to[:, 1, :]))

        @block.scalar
        def _(act):
            act.wait_ge(s_v, marks["pr"])
            act.activation(pr[:], pr[:], ACT.Exp).then_inc(s_a, 1)
            if kind == 0:
                wg, wu, wd, norm, split = experts
                act.activation(lift[:], norm[:], ACT.Copy, scale=float(LIFT)).then_inc(s_b, 1)
                for k, wt in enumerate((wg, wu, wd)):
                    flat = wt[:].rearrange("p e f -> p (e f)") if k < 2 else wt[:].rearrange("p e c d -> p (e c d)")
                    if k == 0:
                        act.wait_ge(s_b, 1)
                    act.activation(flat, flat, ACT.Copy, scale=lift[:, 0:1] if k < 2 else float(LIFT)).then_inc(s_b, 1)
                    act.wait_ge(s_b, 2 * k + 2)
                    act.activation(split[:, k, 0, :], flat, ACT.Copy).then_inc(s_b, 1)
                act.wait_ge(s_v, marks["d"])
                act.activation(one[:], one[:], ACT.Exp).then_inc(s_a, 1)

        if kind == 0:
            @block.gpsimd
            def _(pool):
                for k, wt in enumerate(experts[0:3]):
                    flat = wt[:].rearrange("p e f -> p (e f)") if k < 2 else wt[:].rearrange("p e c d -> p (e c d)")
                    pool.wait_ge(s_b, 2 * k + 3)
                    pool.tensor_tensor(experts[4][:, k, 1, :], flat, experts[4][:, k, 0, :], ALU.subtract)\
                        .then_inc(s_w, 1)
                pool.wait_ge(s_w, 3)

        if kind == 1:
            @block.sync
            def _(sp):
                sp.dma_start(bias1[:], bias_row).then_inc(s_b, 16)
                sp.dma_start(wi[:], dram["L1_ffn_experts_inter"].rearrange("e d f -> d e f")).then_inc(s_w, 16)
                for e in range(NE - 1):
                    sp.dma_start(wo[:, e, :, :], dram["L1_ffn_experts_out"][e].rearrange("(c f) d -> f c d", f=P))\
                        .then_inc(s_w, 16)
                sp.wait_ge(s_w, 16 * NE)

            @block.tensor
            def _(pe):
                pe.wait_ge(s_b, 16)
                pe.matmul(ps[:, 2, 0:NE], cst[0:1, C_TRI + P:C_TRI + 2 * P], bias1[:], start=True, stop=True)\
                  .then_inc(s_p, 1)
                pe.wait_ge(s_v, marks["mask"])
                flat = mask[:].rearrange("p t e -> p (t e)")
                pe.matmul(ps[:, 0, 0:T * NE], tri[:, 0:P], flat, start=True, stop=True).then_inc(s_p, 1)
                pe.matmul(ps[:, 1, 0:T * NE], tri[:, P:2 * P], flat, start=True, stop=True)\
                  .then_inc(s_p, 1)
                for t in range(2 * T):
                    if t % (T // 4) == 0:
                        pe.wait_ge(s_v, marks["in_row", t // (T // 4)])
                    last = pe.matmul(ps[:, 3, 0:2 * NSLOT], in_row[:, t, :],
                                     found[:, t, :, :].rearrange("p a n -> p (a n)"),
                                     start=(t == 0), stop=(t == 2 * T - 1))
                last.then_inc(s_p, 1)


CAP = NT // NE
NSLOT = CAP * (NE - 1) // P
BEYOND = 1 << 20
LIFT = 64


def gated_mixture(nc, hT, comb, XB, X, cst, experts):
    NBLK, TB, EX, FC = 8, 4, NE + 1, F0 // P
    NQ = EX * FC
    PARTS = ((0, 0), (0, 1), (1, 0))
    with ExitStack() as ctx:
        take = semaphores(nc, ctx)

        def sb(name, shape, dt=F32):
            return ctx.enter_context(nc.sbuf_tensor(f"g{name}", shape, dt))

        def sem(name):
            return take(f"g{name}")

        split = experts[4]
        gate_w, up_w = (split[:, k, :, :].rearrange("p l (e f) -> p l e f", e=EX) for k in range(2))
        down_w = split[:, 2, :, :].rearrange("p l (e c d) -> p l e c d", e=EX, c=FC)
        sg = sb("sg", [P, 2, 512])
        prod = sb("prod", [P, 2, 512])
        hid = sb("hid", [P, 3, 2, FC, 512], F16)
        acc = sb("acc", [P, 3, TB, D])
        pad = sb("pad", [1, 1])
        stats = sb("stats", [P, TB, 6])
        mv = sb("mv", [P, TB, 2])
        ve = sb("ve", [P, TB])
        rs = sb("rs", [P, TB])
        half = sb("half", [P, TB])
        tmp = sb("tmp", [P, TB, D])
        gate_ps = ctx.enter_context(nc.psum_tensor("gate_ps", [P, 2, 512], F32))
        up_ps = ctx.enter_context(nc.psum_tensor("up_ps", [P, 2, 512], F32))
        down_ps = ctx.enter_context(nc.psum_tensor("down_ps", [P, 3, 512], F32))
        s_half = sem("s_half")
        s_gu = sem("s_gu")
        s_sg = sem("s_sg")
        s_prod = sem("s_prod")
        s_high = sem("s_high")
        s_hid = sem("s_hid")
        s_down = sem("s_down")
        s_acc = sem("s_acc")
        s_l = sem("s_l")
        s_ve = sem("s_ve")
        s_rs = sem("s_rs")
        s_res = sem("s_res")
        block = ctx.enter_context(nc.Block())

        def blocks(eng, body):
            body(0)
            with eng.Fori(1, NBLK) as i:
                body(i)
            body(NBLK)

        def new(i):
            return not isinstance(i, int) or i < NBLK

        def there(i, k):
            return not isinstance(i, int) or (i < NBLK if k >= 0 else i > 0)

        @block.gpsimd
        def _(pool):
            pool.memset(half[:], -0.5).then_inc(s_half, 1)
            pool.wait_ge(s_half, 1)

            def body(i):
                upto(pool, s_ve, 1, i, 1)
                pool.tensor_tensor(rs[:], ve[:], half[:], ALU.pow).then_inc(s_rs, 1)

            body(0)
            with pool.Fori(1, NBLK) as i:
                body(i)

        @block.tensor
        def _(pe):
            def hidden(i, q):
                e, c = q // FC, q % FC
                upto(pe, s_prod, NQ, i, q - 1)
                cols = slice(c * P, (c + 1) * P)
                for ps, wt in ((gate_ps, gate_w), (up_ps, up_w)):
                    for k, (lw, lh) in enumerate(PARTS):
                        last = pe.matmul(ps[:, q % 2, :], wt[:, lw, e, cols], hT[:, lh, ds(i * 512, 512)],
                                         start=(k == 0), stop=(k == 2))
                last.then_inc(s_gu, 1)

            def down(i, e):
                upto(pe, s_hid, NQ, i, FC * (e + 1))
                upto(pe, s_acc, EX, i, e - 2)
                for t in range(TB):
                    for c in range(FC):
                        for k, (lh, lw) in enumerate(PARTS):
                            last = pe.matmul(down_ps[:, e % 3, t * D:(t + 1) * D],
                                             hid[:, e % 3, lh, c, t * P:(t + 1) * P], down_w[:, lw, e % EX, c, :],
                                             start=(c == 0 and k == 0), stop=(c == FC - 1 and k == 2))
                last.then_inc(s_down, 1)

            def body(i):
                for q in range(NQ):
                    if new(i):
                        hidden(i, q)
                    if q % FC == 0 and there(i, q // FC - 2):
                        down(i, q // FC - 2)

            blocks(pe, body)

        @block.scalar
        def _(act):
            def high(i, q):
                e, c = q // FC, q % FC
                upto(act, s_prod, NQ, i, q + 1)
                upto(act, s_down, EX, i, e - 2)
                act.activation(hid[:, e % 3, 0, c, :], prod[:, q % 2, :], ACT.Copy).then_inc(s_high, 1)

            def body(i):
                for q in range(NQ):
                    if new(i):
                        upto(act, s_gu, NQ, i, q + 1)
                        upto(act, s_prod, NQ, i, q - 1)
                        act.activation(sg[:, q % 2, :], gate_ps[:, q % 2, :], ACT.Silu, scale=1.0 / LIFT)\
                           .then_inc(s_sg, 1)
                    if there(i, q - 1):
                        high(i, q - 1)

            blocks(act, body)

        @block.vector
        def _(dve):
            def product(i, q):
                upto(dve, s_sg, NQ, i, q + 1)
                upto(dve, s_hid, NQ, i, q - 1)
                dve.tensor_tensor(prod[:, q % 2, :], sg[:, q % 2, :], up_ps[:, q % 2, :], ALU.mult)\
                   .then_inc(s_prod, 1)

            def low(i, q):
                e, c = q // FC, q % FC
                upto(dve, s_high, NQ, i, q + 1)
                dve.tensor_tensor(hid[:, e % 3, 1, c, :], prod[:, q % 2, :], hid[:, e % 3, 0, c, :],
                                  ALU.subtract).then_inc(s_hid, 1)

            def add(i, e):
                upto(dve, s_down, EX, i, e + 1)
                upto(dve, s_acc, EX, i, e)
                if e == 2:
                    upto(dve, s_res, 1, i, 0)
                block_of, which = (i, e) if e >= 0 else (i - 1, e + EX)
                for t in range(TB):
                    d = down_ps[:, e % 3, t * D:(t + 1) * D]
                    tile = ds(block_of * TB + t, 1)
                    before = acc[:, (e - 1) % 3, t, :] if which else XB[:, tile, :].rearrange("p a d -> p (a d)")
                    by = comb[:, tile, which] if which < NE else LIFT ** -2
                    last = dve.scalar_tensor_tensor(acc[:, e % 3, t, :], d, by, before, ALU.mult, ALU.add)
                last.then_inc(s_acc, 1)

            def norm_moments(i):
                upto(dve, s_acc, EX, i, 0)
                a = acc[:, (EX - 1) % 3, :, :]
                lk = Link(dve, s_l, 3 * TB, i - 1)
                lk(*[dve.bn_stats(stats[:, t, :], a[:, t, :]) for t in range(TB)])
                dve.memset(pad[:], 0.0)
                lk(*[dve.bn_aggr(mv[:, t, :], stats[:, t, :]) for t in range(TB)])
                dve.tensor_scalar(ve[:], mv[:, :, 1], EPS_LN, None, ALU.add).then_inc(s_ve, 1)

            def norm_apply(i):
                a = acc[:, (EX - 1) % 3, :, :]
                lk = Link(dve, s_l, 3 * TB, i - 1).skip_to(2 * TB)
                upto(dve, s_rs, 1, i, 0)
                lk(*[dve.tensor_scalar(tmp[:, t, :], a[:, t, :], mv[:, t, 0:1], rs[:, t:t + 1],
                                       ALU.subtract, ALU.mult) for t in range(TB)])
                xt = X[:, ds((i - 1) * TB, TB), :]
                dve.tensor_tensor(xt, xt, tmp[:], ALU.add).then_inc(s_res, 1)

            def body(i):
                for q in range(NQ):
                    if new(i):
                        product(i, q)
                    if there(i, q - 1):
                        low(i, q - 1)
                    e = (q - 1) // FC - 2
                    if q % FC == 1 and there(i, e):
                        add(i, e)
                    if q == 5 and there(i, -1):
                        norm_moments(i)
                    if q == 7 and there(i, -1):
                        norm_apply(i)

            blocks(dve, body)
            dve.wait_ge(s_res, NBLK)


def capped_mixture(nc, idx_in, idx_out, wsel, noop, Y, X, cst, wi, wo, out, yd, od):
    NX, TB, FC = NE - 1, CAP // P, F1 // P
    NBLK = NTILE // TB
    with ExitStack() as ctx:
        take = semaphores(nc, ctx)

        def sb(name, shape, dt=F32):
            return ctx.enter_context(nc.sbuf_tensor(f"c{name}", shape, dt))

        def sem(name):
            return take(f"c{name}")

        xe = sb("xe", [P, 3, TB, D])
        xT = sb("xT", [P, 2, CAP])
        hid = sb("hid", [P, 2, FC, CAP])
        res = sb("res", [P, 2, TB, D])
        got = sb("got", [P, 2, NTILE, D])
        stats = sb("stats", [P, NTILE, 6])
        mv = sb("mv", [P, NTILE, 2])
        ve = sb("ve", [P, NTILE])
        rs = sb("rs", [P, NTILE])
        nm = sb("nm", [P, NTILE])
        half = sb("half", [P, 1])
        turn_ps = ctx.enter_context(nc.psum_tensor("cturn_ps", [P, 2, 512], F32))
        hid_ps = ctx.enter_context(nc.psum_tensor("chid_ps", [P, 4, 512], F32))
        out_ps = ctx.enter_context(nc.psum_tensor("cout_ps", [P, 2, 512], F32))
        s_ready = sem("s_ready")
        s_xe = [sem(f"s_xe{k}") for k in range(3)]
        s_turn = sem("s_turn")
        s_xT = sem("s_xT")
        s_hp = sem("s_hp")
        s_hid = sem("s_hid")
        s_op = sem("s_op")
        s_res = sem("s_res")
        s_sent = [sem(f"s_sent{k}") for k in range(2)]
        s_got = [sem(f"s_got{k}") for k in range(NBLK)]
        s_pass = sem("s_pass")
        s_m = sem("s_m")
        s_ve = sem("s_ve")
        s_rs = sem("s_rs")
        s_x = sem("s_x")
        s_nm = sem("s_nm")
        s_f = sem("s_f")
        s_n = sem("s_n")
        s_out = sem("s_out")
        block = ctx.enter_context(nc.Block())

        @block.sync
        def _(sp):
            sp.wait_ge(s_sent[0], 16 * TB * 4)
            sp.wait_ge(s_sent[1], 16 * TB * 3)
            rows = od.rearrange("(c t p) d -> c p t d", c=2, p=P)
            for n in range(NBLK):
                for c in range(2):
                    sp.dma_start(got[:, c, n * TB:(n + 1) * TB, :], rows[c, :, n * TB:(n + 1) * TB, :])\
                      .then_inc(s_got[n], 16)
            ot = out.rearrange("b (c p) d -> p (b c) d", p=P)
            for n in range(NBLK):
                sp.wait_ge(s_x, n + 1)
                sp.dma_start(ot[:, TB * n:TB * n + TB, :], X[:, TB * n:TB * n + TB, :]).then_inc(s_out, 16)
            sp.wait_ge(s_out, 16 * NBLK)

        @block.gpsimd
        def _(pool):
            pool.memset(xe[:], 0.0).then_inc(s_ready, 1)
            pool.memset(half[:], -0.5).then_inc(s_ready, 1)
            pool.wait_ge(s_ready, 2)

            def gather(e):
                if e >= 3:
                    pool.wait_ge(s_turn, e - 2)
                for c in range(TB):
                    t = e * TB + c
                    pool.indirect_dma_start(xe[:, e % 3, c, :], None, yd,
                                            bass.IndirectOffsetOnAxis(ap=idx_in[:, t:t + 1], axis=0),
                                            bounds_check=NT - 1, oob_is_err=False).then_inc(s_xe[e % 3], 16)

            def scatter(e):
                pool.wait_ge(s_res, e + 1)
                for c in range(TB):
                    t = e * TB + c
                    pool.indirect_dma_start(od, bass.IndirectOffsetOnAxis(ap=idx_out[:, t:t + 1], axis=0),
                                            res[:, e % 2, c, :], None, bounds_check=2 * NT - 1, oob_is_err=False)\
                        .then_inc(s_sent[e % 2], 16)

            def residual(n):
                pool.wait_ge(s_f, n + 1)
                part = slice(TB * n, TB * n + TB)
                pool.tensor_tensor(X[:, part, :], X[:, part, :], Y[:, part, :], ALU.add).then_inc(s_x, 1)

            gather(0)
            gather(1)
            gather(2)
            for e in range(NX):
                if e + 3 < NX:
                    gather(e + 3)
                scatter(e)
            for n in range(NBLK):
                pool.wait_ge(s_ve, n + 1)
                pool.tensor_tensor(rs[:, TB * n:TB * n + TB], ve[:, TB * n:TB * n + TB],
                                   half[:].to_broadcast([P, TB]), ALU.pow).then_inc(s_rs, 1)
                if n >= 1:
                    residual(n - 1)
            residual(NBLK - 1)

        @block.tensor
        def _(pe):
            ident = cst[:, C_IDENT:C_IDENT + P]

            def turn(e):
                pe.wait_ge(s_xe[e % 3], 16 * TB * (e // 3 + 1))
                if e >= 2:
                    pe.wait_ge(s_xT, e - 1)
                for c in range(TB):
                    last = pe.transpose(turn_ps[:, e % 2, c * P:(c + 1) * P], xe[:, e % 3, c, :], ident)
                last.then_inc(s_turn, 1)

            def up(e):
                pe.wait_ge(s_xT, e + 1)
                for c in range(FC):
                    if e >= 1:
                        pe.wait_ge(s_hid, FC * (e - 1) + c + 1)
                    pe.matmul(hid_ps[:, c, :], wi[:, e, c * P:(c + 1) * P], xT[:, e % 2, :], start=True, stop=True)\
                      .then_inc(s_hp, 1)

            def down(e):
                pe.wait_ge(s_hid, FC * (e + 1))
                if e >= 2:
                    pe.wait_ge(s_res, e - 1)
                for t in range(TB):
                    for c in range(FC):
                        last = pe.matmul(out_ps[:, e % 2, t * D:(t + 1) * D], hid[:, e % 2, c, t * P:(t + 1) * P],
                                         wo[:, e, c, :], start=(c == 0), stop=(c == FC - 1))
                last.then_inc(s_op, 1)

            turn(0)
            for e in range(NX):
                up(e)
                if e + 1 < NX:
                    turn(e + 1)
                if e >= 1:
                    down(e - 1)
            down(NX - 1)

        @block.scalar
        def _(act):
            for e in range(NX):
                act.wait_ge(s_turn, e + 1)
                if e >= 2:
                    act.wait_ge(s_hp, FC * (e - 1))
                act.activation(xT[:, e % 2, :], turn_ps[:, e % 2, :], ACT.Copy).then_inc(s_xT, 1)
                for c in range(FC):
                    act.wait_ge(s_hp, FC * e + c + 1)
                    if e >= 2:
                        act.wait_ge(s_op, e - 1)
                    act.activation(hid[:, e % 2, c, :], hid_ps[:, c, :], ACT.Relu).then_inc(s_hid, 1)
            for n in range(NBLK):
                act.wait_ge(s_nm, n + 1)
                for t in range(TB * n, TB * n + TB):
                    last = act.activation(Y[:, t, :], Y[:, t, :], ACT.Identity, bias=nm[:, t:t + 1],
                                          scale=rs[:, t:t + 1])
                last.then_inc(s_f, 1)

        @block.vector
        def _(dve):
            passed = 0
            for e in range(NX):
                for t in range(passed, min(NTILE, passed + 5)):
                    dve.tensor_scalar(Y[:, t, :], Y[:, t, :], noop[:, t:t + 1], None, ALU.mult).then_inc(s_pass, 1)
                    passed = t + 1
                dve.wait_ge(s_op, e + 1)
                if e >= 2:
                    dve.wait_ge(s_sent[e % 2], 16 * TB * (e // 2))
                dve.tensor_copy(res[:, e % 2, :, :].rearrange("p c d -> p (c d)"), out_ps[:, e % 2, :])\
                   .then_inc(s_res, 1)
            assert passed == NTILE
            dve.wait_ge(s_pass, NTILE)

            def shift(n):
                dve.wait_ge(s_rs, n + 1)
                part = slice(TB * n, TB * n + TB)
                dve.scalar_tensor_tensor(nm[:, part], mv[:, part, 0], -1.0, rs[:, part], ALU.mult, ALU.mult)\
                   .then_inc(s_nm, 1)

            for n in range(NBLK):
                dve.wait_ge(s_got[n], 32)
                for t in range(TB * n, TB * n + TB):
                    dve.scalar_tensor_tensor(got[:, 0, t, :], got[:, 0, t, :], wsel[:, 0, t:t + 1], Y[:, t, :],
                                             ALU.mult, ALU.add).then_inc(s_m, 1)
                for t in range(TB * n, TB * n + TB):
                    dve.wait_ge(s_m, TB * n + t + 1)
                    dve.scalar_tensor_tensor(Y[:, t, :], got[:, 1, t, :], wsel[:, 1, t:t + 1], got[:, 0, t, :],
                                             ALU.mult, ALU.add).then_inc(s_m, 1)
                for t in range(TB * n, TB * n + TB):
                    dve.wait_ge(s_m, TB * (n + 1) + t + 1)
                    dve.bn_stats(stats[:, t, :], Y[:, t, :]).then_inc(s_n, 1)
                for t in range(TB * n, TB * n + TB):
                    dve.wait_ge(s_n, TB * n + t + 1)
                    dve.bn_aggr(mv[:, t, :], stats[:, t, :]).then_inc(s_n, 1)
                dve.wait_ge(s_n, 2 * TB * (n + 1))
                dve.tensor_scalar(ve[:, TB * n:TB * n + TB], mv[:, TB * n:TB * n + TB, 1], EPS_LN, None, ALU.add)\
                   .then_inc(s_ve, 1)
                if n >= 1:
                    shift(n - 1)
            shift(NBLK - 1)


def build(nc, dram, out):
    with ExitStack() as ctx:
        def sb(name, shape, dt):
            return ctx.enter_context(nc.sbuf_tensor(name, shape, dt))

        X = sb("X", [P, NTILE, D], F32)
        XB = sb("XB", [P, NTILE, D], F32)
        cst = sb("cst", [P, C_ALL], F32)
        cstb = sb("cstb", [P, 2 * P], BF16)
        w = {"router0": sb("router0", [P, NE], F32), "router1": sb("router1", [P, NE], F32)}
        weights = []
        for n in range(3):
            a = {"wq": sb(f"wq_{n}", [P, NG, P], F32), "wk": sb(f"wk_{n}", [P, NG, P], F32),
                 "wv": sb(f"wv_{n}", [P, D + (H if n == 2 else 0)], F32)}
            if n < 2:
                a["wo"] = sb(f"wo_{n}", [P, D], F32)
            weights.append(a)
        weights[0]["bq"] = sb("bq", [P, NG], F32)
        weights[0]["bk"] = sb("bk", [P, NG], F32)
        weights[0]["bv"] = sb("bv", [1, D], F32)
        weights[0]["bo"] = sb("bo", [1, D], F32)
        Kz = sb("Kz", [P, 3, NG, NJ, S], F16)
        Vx = sb("Vx", [P, 3, TC, H, 32], F32)
        load_weights(nc, cst, cstb, X, Kz, Vx, w, weights, dram)
        attention_layer(nc, 0, X, XB, cst, cstb, Kz, Vx, weights[0])
        attention_layer(nc, 1, X, XB, cst, cstb, Kz, Vx, weights[1])
        logits = sb("logits", [P, NTILE, NE], F32)
        with ExitStack() as c1:
            hT = c1.enter_context(nc.sbuf_tensor("hT", [P, 2, NT], F16))
            comb = c1.enter_context(nc.sbuf_tensor("comb", [P, NTILE, NE], F32))
            wg = c1.enter_context(nc.sbuf_tensor("wg", [P, NE + 1, F0], F32))
            wu = c1.enter_context(nc.sbuf_tensor("wu", [P, NE + 1, F0], F32))
            wd = c1.enter_context(nc.sbuf_tensor("wd", [P, NE + 1, F0 // P, D], F32))
            norm = c1.enter_context(nc.sbuf_tensor("norm2", [P, 1], F32))
            split = c1.enter_context(nc.sbuf_tensor("split", [P, 3, 2, (NE + 1) * F0], F16))
            experts = (wg, wu, wd, norm, split)
            router_layer(nc, 0, cst, XB, None, None, hT, logits, w["router0"], None, experts, dram)
            route(nc, 0, cst, logits, None, comb, None, None, None, None, experts=experts)
            gated_mixture(nc, hT, comb, XB, X, cst, experts)
        attention_layer(nc, 2, X, XB, cst, cstb, Kz, Vx, weights[2])
        idx_in = sb("idx_in", [P, NSLOT], U32)
        idx_out = sb("idx_out", [P, NSLOT], U32)
        wsel = sb("wsel", [P, 2, NTILE], F32)
        noop = sb("noop", [P, NTILE], F32)
        yd = nc.dram_tensor("tokens", [NT, D], F32).ap()
        od = nc.dram_tensor("expert_outputs", [2 * NT, D], F32).ap()
        wi = sb("wi", [P, NE - 1, F1], F32)
        wo = sb("wo", [P, NE - 1, F1 // P, D], F32)
        router_layer(nc, 1, cst, X, XB, yd, None, logits, w["router1"], od)
        route(nc, 1, cst, logits, dram["L1_ffn_router_b"].rearrange("(a e) -> a e", a=1), None, idx_in,
              idx_out, wsel, noop, wi, wo, dram)
        capped_mixture(nc, idx_in, idx_out, wsel, noop, XB, X, cst, wi, wo, out, yd, od)


def kernel(**inputs):
    import numpy as _np
    import concourse.bacc as _bacc
    from concourse import mybir as _mybir
    from concourse.bass_utils import run_bass_kernel_spmd as _run

    nc = _bacc.Bacc("TRN2", target_bir_lowering=False, num_devices=1)
    arrays, dram = {}, {}
    for name, a in list(inputs.items()) + [("constants", constant_table())]:
        a = _np.ascontiguousarray(a)
        arrays[f"in_{name}_dram"] = a
        dram[name] = nc.dram_tensor(f"in_{name}_dram", a.shape, _mybir.dt.from_np(a.dtype), kind="ExternalInput").ap()
    out = nc.dram_tensor("out_0_dram", (NB, S, D), _mybir.dt.float32, kind="ExternalOutput").ap()
    build(nc, dram, out)
    r = _run(nc, [arrays], core_ids=[0])
    return r.results[0]["out_0_dram"]
```
